# Optimizing a Trainium2 kernel written in Bass

```python
import numpy as np
import jax
import jax.numpy as jnp

def _softmax(x, axis=-1):
    return jax.nn.softmax(x, axis=axis)

def _gelu(x):
    return jax.nn.gelu(x, approximate=True)

def _silu(x):
    return jax.nn.silu(x)

def _sigmoid(x):
    return jax.nn.sigmoid(x)

def _layernorm(x, axis=-1, eps=1e-05):
    m = jnp.mean(x, axis=axis, keepdims=True)
    v = jnp.var(x, axis=axis, keepdims=True)
    return (x - m) / jnp.sqrt(v + eps)

def _scatter_add(tgt, idx, src, axis=0):
    return tgt.at[idx].add(src)

def _segment_sum(src, seg, n):
    return jax.ops.segment_sum(src, seg, n)
kernel_name = 'mk_metaformer_d2_conv_nchw256_r4_e6bd26'

def setup_inputs(seed: int=0):
    np.random.seed(seed)
    _w = jnp.asarray

    def _rec_inputs():
        import jax
        import jax.numpy as jnp
        _gk = jax.random.key(seed)
        x = -0.000125 + 0.9999 * jax.random.normal(jax.random.fold_in(_gk, 1), (8, 64, 32, 32), jnp.float32)
        return x
    x = _rec_inputs()

    def _L0_conv_setup():
        import jax, jax.numpy as jnp
        import numpy as np
        CHAN, KEY_DIM, VALUE_DIM, HEADS = (64, 16, 16, 8)
        key = jax.random.key(seed)
        ks = jax.random.split(key, 9)
        b, h, w = (8, 32, 32)
        s = 0.02
        return {'x': jax.random.normal(ks[0], (b, CHAN, h, w), dtype=jnp.float32), 'Wq': jax.random.normal(ks[1], (KEY_DIM * HEADS, CHAN), dtype=jnp.float32) * s, 'bq': jnp.zeros((KEY_DIM * HEADS,), dtype=jnp.float32), 'Wk': jax.random.normal(ks[2], (KEY_DIM, CHAN), dtype=jnp.float32) * s, 'bk': jnp.zeros((KEY_DIM,), dtype=jnp.float32), 'Wv': jax.random.normal(ks[3], (VALUE_DIM, CHAN), dtype=jnp.float32) * s, 'bv': jnp.zeros((VALUE_DIM,), dtype=jnp.float32), 'Wout': jax.random.normal(ks[4], (CHAN, VALUE_DIM * HEADS), dtype=jnp.float32) * s, 'bout': jnp.zeros((CHAN,), dtype=jnp.float32)}
    _L0_conv_all = _L0_conv_setup()
    _L0_conv_in = {k: v for k, v in _L0_conv_all.items() if k in ('Wq', 'bq', 'Wk', 'bk', 'Wv', 'bv', 'Wout', 'bout')}
    del _L0_conv_all

    def _L0_ffn_setup():
        import math
        import jax, jax.numpy as jnp
        import numpy as np
        CAPACITY_FACTOR = 1.25
        TOP_K = 2
        LN_EPS = 1e-05

        def _layer_norm(x, gamma, beta):
            mu = jnp.mean(x, axis=-1, keepdims=True)
            var = jnp.var(x, axis=-1, keepdims=True)
            return (x - mu) * jax.lax.rsqrt(var + LN_EPS) * gamma + beta
        key = jax.random.key(seed)
        ks = jax.random.split(key, 4)
        B, S, D, F, E = (8, 1024, 64, 128, 8)
        x = jax.random.normal(ks[0], (B, S, D), dtype=jnp.float32)
        Wr = jax.random.normal(ks[1], (D, E), dtype=jnp.float32) / np.sqrt(D)
        br = jnp.zeros((E,), jnp.float32)
        W1 = jax.random.normal(ks[2], (E, D, F), dtype=jnp.float32) / np.sqrt(D)
        b1 = jnp.zeros((E, F), jnp.float32)
        W2 = jax.random.normal(ks[3], (E, F, D), dtype=jnp.float32) / np.sqrt(F)
        b2 = jnp.zeros((E, D), jnp.float32)
        gamma = jnp.ones((D,), jnp.float32)
        beta = jnp.zeros((D,), jnp.float32)
        return {'x': x, 'Wr': Wr, 'br': br, 'W1': W1, 'b1': b1, 'W2': W2, 'b2': b2, 'gamma': gamma, 'beta': beta}
    _L0_ffn_all = _L0_ffn_setup()
    _L0_ffn_in = {k: v for k, v in _L0_ffn_all.items() if k in ('Wr', 'br', 'W1', 'b1', 'W2', 'b2', 'gamma', 'beta')}
    del _L0_ffn_all

    def _L1_conv_setup():
        import jax, jax.numpy as jnp
        import numpy as np
        STRIDE = 1
        PADDING = 1

        def sign_ste(w):
            s = 2.0 * (w > 0.0).astype(w.dtype) - 1.0
            return w + jax.lax.stop_gradient(s - w)
        key = jax.random.key(seed)
        kx, kw = jax.random.split(key)
        x = jax.random.normal(kx, (32, 64, 56, 56), dtype=jnp.float32)
        weight = jax.random.uniform(kw, (64, 64, 3, 3), dtype=jnp.float32) * 0.001
        return {'x': x, 'weight': weight}
    _L1_conv_all = _L1_conv_setup()
    _L1_conv_in = {k: v for k, v in _L1_conv_all.items() if k in ('weight',)}
    del _L1_conv_all

    def _L1_ffn_setup():
        import jax, jax.numpy as jnp
        import numpy as np
        B, T, D, H, E = (16, 1024, 64, 128, 8)
        key = jax.random.key(seed)
        ks = jax.random.split(key, 5)
        x = jax.random.normal(ks[0], (B, T, D), dtype=jnp.float32)
        gate_w = jax.random.normal(ks[1], (D, E), dtype=jnp.float32) * 0.02
        gate_b = jnp.zeros((E,), dtype=jnp.float32)
        W1 = jax.random.normal(ks[2], (E, D, H), dtype=jnp.float32) * 0.02
        b1 = jnp.zeros((E, H), dtype=jnp.float32)
        W2 = jax.random.normal(ks[3], (E, H, D), dtype=jnp.float32) * 0.02
        b2 = jnp.zeros((E, D), dtype=jnp.float32)
        return {'x': x, 'gate_w': gate_w, 'gate_b': gate_b, 'W1': W1, 'b1': b1, 'W2': W2, 'b2': b2}
    _L1_ffn_all = _L1_ffn_setup()
    _L1_ffn_in = {k: v for k, v in _L1_ffn_all.items() if k in ('gate_w', 'gate_b', 'W1', 'b1', 'W2', 'b2')}
    del _L1_ffn_all
    return {'x': x, 'L0_conv_Wq': _L0_conv_in['Wq'], 'L0_conv_bq': _L0_conv_in['bq'], 'L0_conv_Wk': _L0_conv_in['Wk'], 'L0_conv_bk': _L0_conv_in['bk'], 'L0_conv_Wv': _L0_conv_in['Wv'], 'L0_conv_bv': _L0_conv_in['bv'], 'L0_conv_Wout': _L0_conv_in['Wout'], 'L0_conv_bout': _L0_conv_in['bout'], 'L0_ffn_Wr': _L0_ffn_in['Wr'], 'L0_ffn_br': _L0_ffn_in['br'], 'L0_ffn_W1': _L0_ffn_in['W1'], 'L0_ffn_b1': _L0_ffn_in['b1'], 'L0_ffn_W2': _L0_ffn_in['W2'], 'L0_ffn_b2': _L0_ffn_in['b2'], 'L0_ffn_gamma': _L0_ffn_in['gamma'], 'L0_ffn_beta': _L0_ffn_in['beta'], 'L1_conv_weight': _L1_conv_in['weight'], 'L1_ffn_gate_w': _L1_ffn_in['gate_w'], 'L1_ffn_gate_b': _L1_ffn_in['gate_b'], 'L1_ffn_W1': _L1_ffn_in['W1'], 'L1_ffn_b1': _L1_ffn_in['b1'], 'L1_ffn_W2': _L1_ffn_in['W2'], 'L1_ffn_b2': _L1_ffn_in['b2']}

def reference(x, L0_conv_Wq, L0_conv_bq, L0_conv_Wk, L0_conv_bk, L0_conv_Wv, L0_conv_bv, L0_conv_Wout, L0_conv_bout, L0_ffn_Wr, L0_ffn_br, L0_ffn_W1, L0_ffn_b1, L0_ffn_W2, L0_ffn_b2, L0_ffn_gamma, L0_ffn_beta, L1_conv_weight, L1_ffn_gate_w, L1_ffn_gate_b, L1_ffn_W1, L1_ffn_b1, L1_ffn_W2, L1_ffn_b2):
    import jax
    import jax.numpy as jnp

    def _L0_conv_ref(x, Wq, bq, Wk, bk, Wv, bv, Wout, bout):
        import jax, jax.numpy as jnp
        import numpy as np
        CHAN, KEY_DIM, VALUE_DIM, HEADS = (64, 16, 16, 8)
        b, c, h, w = x.shape
        n = h * w
        q = jnp.einsum('oc,bchw->bohw', Wq, x) + bq[None, :, None, None]
        k = jnp.einsum('oc,bchw->bohw', Wk, x) + bk[None, :, None, None]
        v = jnp.einsum('oc,bchw->bohw', Wv, x) + bv[None, :, None, None]
        q = q.reshape(b, HEADS, KEY_DIM, n)
        k = k.reshape(b, KEY_DIM, n)
        v = v.reshape(b, VALUE_DIM, n)
        k = jax.nn.softmax(k, axis=2)
        q = jax.nn.softmax(q, axis=2)
        context = jnp.einsum('bdn,ben->bde', k, v)
        out = jnp.einsum('bhdn,bde->bhen', q, context)
        out = out.reshape(b, HEADS * VALUE_DIM, h, w)
        out = jnp.einsum('oc,bchw->bohw', Wout, out) + bout[None, :, None, None]
        return out

    def _L0_ffn_ref(x, Wr, br, W1, b1, W2, b2, gamma, beta):
        import math
        import jax, jax.numpy as jnp
        import numpy as np
        CAPACITY_FACTOR = 1.25
        TOP_K = 2
        LN_EPS = 1e-05

        def _layer_norm(x, gamma, beta):
            mu = jnp.mean(x, axis=-1, keepdims=True)
            var = jnp.var(x, axis=-1, keepdims=True)
            return (x - mu) * jax.lax.rsqrt(var + LN_EPS) * gamma + beta
        B, S, D = x.shape
        E = Wr.shape[1]
        N = B * S
        K = TOP_K
        logits = jnp.mean(x, axis=1) @ Wr + br
        routing_weights = jax.nn.softmax(logits, axis=-1)
        capacity = float(math.ceil(N * CAPACITY_FACTOR / E))
        expected_loads = routing_weights.sum(axis=0) * (N / B)
        scale = jnp.where(expected_loads > capacity, capacity / expected_loads, 1.0)
        routing_weights = jax.nn.softmax(routing_weights * scale, axis=-1)
        rw_tok = jnp.broadcast_to(routing_weights[:, None, :], (B, S, E)).reshape(N, E)
        top_w, top_i = jax.lax.top_k(rw_tok, K)
        top_w = jax.nn.softmax(top_w, axis=-1)
        xf = x.reshape(N, D)
        h = jax.nn.gelu(jnp.einsum('nd,edf->enf', xf, W1) + b1[:, None, :], approximate=False)
        y = jnp.einsum('enf,efd->end', h, W2) + b2[:, None, :]
        w_dense = jnp.zeros((N, E), x.dtype).at[jnp.arange(N)[:, None], top_i].add(top_w)
        out = jnp.einsum('ne,end->nd', w_dense, y).reshape(B, S, D)
        out = _layer_norm(out + x, gamma, beta)
        return out

    def _L1_conv_ref(x, weight):
        import jax, jax.numpy as jnp
        import numpy as np
        STRIDE = 1
        PADDING = 1

        def sign_ste(w):
            s = 2.0 * (w > 0.0).astype(w.dtype) - 1.0
            return w + jax.lax.stop_gradient(s - w)
        scaling = jnp.mean(jnp.abs(weight), axis=(1, 2, 3), keepdims=True)
        scaling = jax.lax.stop_gradient(scaling)
        binary_weights = scaling * sign_ste(weight)
        y = jax.lax.conv_general_dilated(x, binary_weights, window_strides=(STRIDE, STRIDE), padding=[(PADDING, PADDING), (PADDING, PADDING)], dimension_numbers=('NCHW', 'OIHW', 'NCHW'))
        return y

    def _L1_ffn_ref(x, gate_w, gate_b, W1, b1, W2, b2):
        import jax, jax.numpy as jnp
        import numpy as np
        B, T, D, H, E = (16, 1024, 64, 128, 8)
        Bb, Tt, Dd = x.shape
        Ee = gate_w.shape[1]
        xf = x.reshape(-1, Dd)
        N = xf.shape[0]
        logits = xf @ gate_w + gate_b
        probs = jax.nn.softmax(logits, axis=-1)
        top2_vals, top2_idx = jax.lax.top_k(probs, 2)
        cw = jnp.zeros((N, Ee), dtype=xf.dtype).at[jnp.arange(N)[:, None], top2_idx].add(top2_vals)

        def step(acc, params):
            w1, bb1, w2, bb2, we = params
            h = jax.nn.gelu(xf @ w1 + bb1, approximate=False)
            y = h @ w2 + bb2
            return (acc + we[:, None] * y, None)
        out, _ = jax.lax.scan(step, jnp.zeros_like(xf), (W1, b1, W2, b2, cw.T))
        return out.reshape(Bb, Tt, Dd)

    def _gn(v, G=32, eps=1e-05):
        B_, C_, H_, W_ = v.shape
        g = v.reshape(B_, G, C_ // G, H_, W_)
        m = jnp.mean(g, axis=(2, 3, 4), keepdims=True)
        s = jnp.var(g, axis=(2, 3, 4), keepdims=True)
        return ((g - m) / jnp.sqrt(s + eps)).reshape(v.shape)

    def _ln_c(v, eps=1e-06):
        m = jnp.mean(v, axis=1, keepdims=True)
        s = jnp.var(v, axis=1, keepdims=True)
        return (v - m) / jnp.sqrt(s + eps)

    def _ln_t(v, eps=1e-05):
        m = jnp.mean(v, axis=-1, keepdims=True)
        s = jnp.var(v, axis=-1, keepdims=True)
        return (v - m) / jnp.sqrt(s + eps)

    def _to_tokens(v):
        B_, C_, H_, W_ = v.shape
        return v.reshape(B_, C_, H_ * W_).transpose(0, 2, 1)

    def _from_tokens(t, like):
        B_, C_, H_, W_ = like.shape
        return t.transpose(0, 2, 1).reshape(B_, C_, H_, W_)
    x = x + _L0_conv_ref(_ln_c(x), L0_conv_Wq, L0_conv_bq, L0_conv_Wk, L0_conv_bk, L0_conv_Wv, L0_conv_bv, L0_conv_Wout, L0_conv_bout)
    t = _to_tokens(x)
    t = t + _L0_ffn_ref(_ln_t(t), L0_ffn_Wr, L0_ffn_br, L0_ffn_W1, L0_ffn_b1, L0_ffn_W2, L0_ffn_b2, L0_ffn_gamma, L0_ffn_beta)
    x = _from_tokens(t, x)
    x = x + _L1_conv_ref(_ln_c(x), L1_conv_weight)
    t = _to_tokens(x)
    t = t + _L1_ffn_ref(_ln_t(t), L1_ffn_gate_w, L1_ffn_gate_b, L1_ffn_W1, L1_ffn_b1, L1_ffn_W2, L1_ffn_b2)
    x = _from_tokens(t, x)
    return x

_drawn_inputs = setup_inputs


def setup_inputs(seed=0):
    import zlib

    import numpy as np

    out = dict(_drawn_inputs(seed))
    spreads = {'L0_conv_bq': (0.0, 2.0),
     'L0_conv_bk': (0.0, 2.0),
     'L0_conv_bv': (0.0, 0.31),
     'L0_conv_bout': (0.0, 0.1),
     'L0_ffn_br': (0.0, 0.1),
     'L0_ffn_b1': (0.0, 0.312),
     'L0_ffn_b2': (0.0, 0.1),
     'L0_ffn_gamma': (1.0, 0.2),
     'L0_ffn_beta': (0.0, 0.1),
     'L1_ffn_gate_b': (0.0, 0.8),
     'L1_ffn_b1': (0.0, 0.8),
     'L1_ffn_b2': (0.0, 0.725)}
    factors = {'L0_conv_Wq': 8.0,
     'L0_conv_Wk': 8.0,
     'L0_conv_Wv': 8.0,
     'L1_ffn_gate_w': 5.678,
     'L1_ffn_W1': 8.0,
     'L1_ffn_W2': 8.0,
     'L1_conv_weight': 8.0}
    for name, (base, spread) in spreads.items():
        noise = np.random.default_rng([zlib.crc32(name.encode()), seed]).standard_normal(out[name].shape)
        drawn = base * np.exp(spread * noise) if base else spread * noise
        out[name] = jnp.asarray(drawn.astype(out[name].dtype))
    for name, factor in factors.items():
        out[name] = (out[name] * factor).astype(out[name].dtype)
    return out
```

```python
from contextlib import ExitStack

import numpy as np

import concourse.bass as bass
from concourse import mybir

F32 = mybir.dt.float32
F32R = mybir.dt.float32r
I32 = mybir.dt.int32
ALU = mybir.AluOpType
ACT = mybir.ActivationFunctionType
X = mybir.AxisListType.X

B, C, H, W = 8, 64, 32, 32
S = H * W
P = 128
TILES = S // P
PAIRS = B // 2
HEADS, KD = 8, 16
E, F = 8, 128
UNITS = 4 * PAIRS
UT_ = 2
HALF = S // 2
TAPS = 9
CAPACITY = float(-(-B * S * 5 // (4 * E)))
LN_C_EPS, LN_T_EPS = 1e-6, 1e-5

K_ID, K_CEN, K_IC, K_HEAD, K_REV, K_PAIR, K_HL = 0, 128, 256, 512, 520, 528, 530
K_N = 532


def steps_of(eng, sem, base=0):
    return Steps(eng, sem, base)


class Steps:
    def __init__(self, eng, sem, base):
        self.eng, self.sem, self.base, self.n = eng, sem, base, 0

    def done(self, instruction):
        instruction.then_inc(self.sem, 1)
        self.n += 1

    def wait(self):
        self.eng.wait_ge(self.sem, self.base + self.n)


TOP2_STEPS = 11


def top2(vec, steps, p, n, probs, rev, m, eq, rank, q, first, rest, second):
    wide = [p, n, E]
    for k, (vals, onehot) in enumerate(((probs, first), (rest, second))):
        steps.wait()
        steps.done(vec.tensor_reduce(m, vals, X, ALU.max))
        steps.wait()
        steps.done(vec.tensor_tensor(eq, vals, m.unsqueeze(2).broadcast_to(wide), ALU.is_equal))
        steps.wait()
        steps.done(vec.tensor_tensor(rank, eq, rev.unsqueeze(1).broadcast_to(wide), ALU.mult))
        steps.wait()
        steps.done(vec.tensor_reduce(q[:, k, :], rank, X, ALU.max))
        steps.wait()
        steps.done(vec.tensor_tensor(onehot, rank, q[:, k, :].unsqueeze(2).broadcast_to(wide), ALU.is_equal))
        if k == 0:
            steps.wait()
            steps.done(vec.scalar_tensor_tensor(rest, first, -2.0, probs, ALU.mult, ALU.add))


def build(nc, x, consts, wqb, bq2, wkv, bkv, wout, bout2, wr, br, w1a, b1a, w2ta, b2ta, gammab, betab,
          wconv, wcs, gw, gbb, w1b, b1b, w2b, b2b, selb, out):
    ctx = ExitStack()
    with ctx:
        def sb(name, shape, dt=F32):
            return ctx.enter_context(nc.sbuf_tensor(name, shape, dt))

        def tiles(ap):
            return ap.rearrange("p (t c) -> p t c", c=C)

        def sem(name):
            return ctx.enter_context(nc.semaphore(name))

        K = sb("K", [P, K_N])
        ident = K[:, K_ID:K_ID + P]
        cen = K[:, K_CEN:K_CEN + P]
        ic = K[:, K_IC:K_IC + 256]
        headmask = K[:, K_HEAD:K_HEAD + HEADS]
        rev = K[:, K_REV:K_REV + E]
        pairmask = K[0:32, K_PAIR:K_PAIR + 2]
        hlmask = K[0:32, K_HL:K_HL + 2]
        ident_r = sb("ident_r", [P, P], F32R)
        ones_r = sb("ones_r", [C, P], F32R)
        ones = sb("ones", [E, P])
        WQB = sb("WQB", [P, 256])
        BQ2 = sb("BQ2", [C, P])
        CWTB = sb("CWTB", [C, 2 * S], F32R)
        BQR = CWTB[:, 0:512]
        WKV = sb("WKV", [P, C])
        BKV = sb("BKV", [C, 1])
        WOUT = sb("WOUT", [C, P])
        BOUT2 = sb("BOUT2", [C, C])
        WOC = sb("WOC", [P, P])
        BOR = CWTB[:, 512:1024]
        WR = sb("WR", [P, E])
        BR = sb("BR", [E, E])
        W1stage = sb("W1stage", [P, E, F])
        W1A = sb("W1A", [P, E, 2, F], F32R)
        B1A = sb("B1A", [F, E])
        HB = sb("HB", [F, 2, HALF])
        W2TA = HB[0:C, :, :].rearrange("p a (e f) -> p (a e) f", f=F)
        W2A = sb("W2A", [F, E, C])
        B2TA = sb("B2TA", [C, E])
        B2A = sb("B2A", [E, C])
        GAMMA = sb("GAMMA", [P, C])
        BETA = sb("BETA", [P, C])
        WCstage = W1stage[:, 0:5, :].rearrange("p a n -> p (a n)")[:, 0:TAPS * C].rearrange("p (t c) -> p t c", c=C)
        WC = sb("WC", [P, TAPS, C], F32R)
        WCS = W1stage[0:C, 0:5, :].rearrange("p a n -> p (a n)")[:, 0:C * TAPS]
        CSCALE = sb("CSCALE", [C, 1])
        GWstage = sb("GWstage", [P, E])
        GW = sb("GW", [P, 2, E], F32R)
        GBB = sb("GBB", [P, TILES, E])
        W1B = sb("W1B", [P, E, 2, F], F32R)
        B1B = sb("B1B", [F, E])
        W2B = sb("W2B", [F, E, C])
        B2stage = sb("B2stage", [32, C])
        B2hi = sb("B2hi", [32, C], F32R)
        B2lo = sb("B2lo", [32, C])
        B2B = sb("B2B", [32, P], F32R)
        SELstage = W1stage[0:32, :, :]
        SEL = sb("SEL", [32, E, P], F32R)
        XC = sb("XC", [P, PAIRS, S])
        T = sb("T", [P, B, TILES, C])
        U = sb("U", [P, B, TILES, C])
        UTR = sb("UTR", [P, B, S], F32R)
        usum = sb("usum", [P, B, 4])
        SQ1 = sb("SQ1", [P, TILES, P])
        ss1 = sb("ss1", [P, 2 * TILES])
        var1 = sb("var1", [P, 2 * TILES])
        rstd1 = sb("rstd1", [P, 2 * TILES])
        XNT = sb("XNT", [P, TILES, P])
        XN = sb("XN", [P, 2, S])
        KV = sb("KV", [C, S])
        nkmax = sb("nkmax", [32, 1])
        ksum = sb("ksum", [32, 1])
        rksum = sb("rksum", [32, 1])
        r01 = sb("r01", [32, 2])
        KVT = sb("KVT", [P, TILES, C])
        Z = sb("Z", [32, HEADS, KD])
        BD = sb("BD", [P, 2, HEADS, KD])
        M = sb("M", [P, 2, 2, P])
        qmax = sb("qmax", [P, 32])
        QS = sb("QS", [P, 2, 512])
        qsum = sb("qsum", [P, 32])
        rqsum = sb("rqsum", [P, 2, 32])
        QT = sb("QT", [P, 2, 4, P])
        SQ2 = sb("SQ2", [P, 2, 4, C])
        ss2 = sb("ss2", [P, 2, 4])
        var2 = sb("var2", [P, 2, 4])
        rstd2 = sb("rstd2", [P, 2, 4])
        US = sb("US", [P, 2, 4, 2, C], F32R)
        pow_half = sb("pow_half", [P, 2 * TILES])
        u8 = sb("u8", [P, E])
        R = sb("R", [E, 32, E])
        RV = sb("RV", [E, 16, 1])
        Rq = sb("Rq", [E, 2, 1])
        vals = sb("vals", [E, 4])
        D1 = KV[0:E, 0:B * C].rearrange("p (b c) -> p b c", c=C)
        D2 = sb("D2", [E, B, 4])
        wdT = sb("wdT", [E, E])
        b2row = sb("b2row", [E, C])
        WI = sb("WI", [P, B, 4])
        IDX = sb("IDX", [1, B * 2], I32)
        B2A_b = SQ2[:, :, :, :].rearrange("p k r c -> p (k r) c")
        W1S = sb("W1S", [P, 2, 2, F], F32R)
        B1S = sb("B1S", [F, 2])
        W2S = sb("W2S", [F, 2, C])
        HA = XC[:, 0:2, :]
        ZA, SQA, ZN, ZG = (tiles(XN[:, k // 2, (k % 2) * HALF:(k % 2 + 1) * HALF]) for k in range(4))
        ssA = sb("ssA", [P, TILES])
        varA = sb("varA", [P, TILES])
        rstdA = sb("rstdA", [P, TILES])
        sumA = sb("sumA", [P, TILES])
        spare = sb("spare", [P, 3])
        TA = sb("TA", [P, TILES, C])
        XA = XNT[:, :, 0:C]
        V = XNT[:, :, C:P]
        VS = US[:, :, :, :, :].rearrange("p k r a c -> p (k r) a c")
        VP = sb("VP", [P, 2, H + 2, W + 2], F32R)
        CV = sb("CV", [P, HALF])
        TF = QT[:, :, :, :].rearrange("p k r (a c) -> p k (r a) c", c=C)
        sumB = sb("sumB", [P, TILES])
        XB = SQ1[:, :, 0:C]
        SQB = SQ1[:, :, C:P]
        ssB = sb("ssB", [P, TILES])
        varB = sb("varB", [P, TILES])
        rstdB = sb("rstdB", [P, TILES])
        EN = tiles(QS[:, 0, :])
        ES = sb("ES", [P, TILES, 2, C], F32R)
        ET = sb("ET", [P, 2, S], F32R)
        G = sb("G", [P, 10, TILES, E])
        gv = sb("gv", [P, 4, TILES])
        gq = sb("gq", [P, 2, TILES])
        CWS = sb("CWS", [P, TILES, 4, E], F32R)
        CWT = CWTB[0:32, :].rearrange("p (k n) -> p k n", k=2)
        HG = XC[:, 2:4, :].rearrange("p a (k n) -> p (a k) n", k=2)
        OO = QS[0:C, 1, :]
        OUT = W1stage[0:C, :, :].rearrange("p (c a) n -> p c (a n)", c=2)

        ps = ctx.enter_context(nc.psum_tensor("ps", [P, 8, HALF], F32))

        s = {name: sem(name) for name in (
            "ld_const", "ld_x0", "ld_x", "ld_att", "ld_ffn0", "ld_conv", "ld_ffn1", "ld_w1b", "ld_sel", "memsets", "set_dve", "set_w2",
            "set_woc", "set_bo", "set_wocev", "set_w2ev", "set_b2ev",
            "centred", "sq1", "ss1", "var1", "rstd1", "xn_tok", "xnT", "xn", "kv_ps", "kv", "kmax", "kexp",
            "rk", "kvT_ps", "kvT", "ctx", "z", "ctxT", "bd", "m_ps", "m",
            "q_ps", "qmax", "qsub", "qexp", "qsum", "rqsum", "qnorm", "qT_ps", "qT", "att", "t_res", "sq2",
            "ss2", "var2", "rstd2", "u", "uhi", "ulo", "uT_ps", "uT",
            "router_dve", "router_pe", "router_act", "u_biased", "t_beta",
            "a_sel", "a_h", "a_gelu", "a_z_ps", "a_z", "a_sq", "a_ss", "a_var", "a_rstd", "a_zn", "a_zg", "a_t",
            "a_sum", "a_xc", "a_v", "a_vhi", "a_vlo", "a_vT", "a_img",
            "b_conv", "b_cv", "b_cvT", "b_t", "b_sum", "b_xc", "b_sq", "b_ss", "b_var", "b_rstd", "b_en", "b_ehi",
            "b_elo", "b_eT", "b_et", "b_gate", "b_lg", "b_exp", "b_top", "b_cw", "b_cwT", "b_cwt",
            "f_h", "f_gelu", "f_cw", "f_hg", "f_w2", "f_acc", "f_odd", "f_out", "f_stored0", "f_stored1",
        )}
        block = ctx.enter_context(nc.Block())

        SA = ps[:, 0:2, :].rearrange("p a n -> p (a n)")
        Q_BANK, QT_BANK, AT_BANK, UT_BANK = (2, 3), 4, (5, 6), 7
        A_BANK, B_BANK, H_BANK, CW_BANK, ACC_BANK = (0, 1), (2, 3), (4, 5), 6, 7

        def image(tile, b):
            return tile[:, bass.ds(b, 1), :, :].rearrange("p a t c -> p (a t) c")

        def f32(ap):
            return ap.bitcast(F32)

        SET_BQ, SET_BO, SET_W1A, SET_SIGNS, SET_CONV, SET_W1B, SET_F1 = 3, 5, 7, 9, 11, 13, 20
        LD_ATT, LD_FFN0, LD_FFN1 = 6 * 16, 8 * 16, 5 * 16

        @block.sync
        def _(sp):
            xp = x.rearrange("(q i) c n -> q (i c) n", i=2)
            sp.dma_start(K[:, :], consts).then_inc(s["ld_const"], 16)
            sp.dma_start(XC[:, 0, :], xp[0]).then_inc(s["ld_x0"], 16)
            for dst, src in ((WKV[:, :], wkv), (BKV[:, :], bkv), (WQB[:, :], wqb), (BQ2[:, :], bq2),
                             (WOUT[:, :], wout), (BOUT2[:, :], bout2)):
                sp.dma_start(dst, src).then_inc(s["ld_att"], 16)
            sp.dma_start(XC[:, 1:PAIRS, :], xp[1:PAIRS].rearrange("q p n -> p q n")).then_inc(s["ld_x"], 16)
            for dst, src in ((WR[:, :], wr), (BR[:, :], br), (W1stage[:, :, :], w1a), (B1A[:, :], b1a),
                             (W2TA[:, :, :], w2ta), (B2TA[:, :], b2ta), (GAMMA[:, :], gammab), (BETA[:, :], betab)):
                sp.dma_start(dst, src).then_inc(s["ld_ffn0"], 16)
            for dst, src in ((GWstage[:, :], gw), (GBB[:, :, :], gbb), (B1B[:, :], b1b),
                             (W2B[:, :, :], w2b), (B2stage[:, :], b2b)):
                sp.dma_start(dst, src).then_inc(s["ld_ffn1"], 16)
            for dst, src, step, sig in ((WCstage, wconv, SET_W1A, "ld_conv"), (WCS, wcs, SET_SIGNS, "ld_conv"),
                                        (W1stage[:, :, :], w1b, SET_CONV, "ld_w1b"),
                                        (SELstage, selb, SET_W1B, "ld_sel")):
                sp.wait_ge(s["set_dve"], step)
                sp.dma_start(dst, src).then_inc(s[sig], 16)

            def store(b):
                for c in range(2):
                    sp.wait_ge(s["f_out"], 2 * b + c + 2)
                    sp.dma_start(out[bass.ds(b, 1), :, c * HALF:(c + 1) * HALF].rearrange("a c n -> c (a n)"),
                                 OUT[:, c, :]).then_inc(s[f"f_stored{c}"], 16)

            with sp.Fori(0, B) as b:
                store(b)
            for c in range(2):
                sp.wait_ge(s[f"f_stored{c}"], 16 * B + 16)

        @block.gpsimd
        def _(pool):
            for tile, value in ((pow_half[:, :], -0.5), (ones[:, :], 1.0), (f32(ones_r[:, :]), 1.0),
                                (f32(VP[:, :, :, :]), 0.0), (f32(B2B[:, :]), 0.0)):
                pool.memset(tile, value).then_inc(s["memsets"], 1)

            def rstd(var, out_, n, k, var_sem, rstd_sem):
                pool.wait_ge(s[var_sem], k)
                pool.tensor_tensor(out_, var, pow_half[:, 0:n], ALU.pow).then_inc(s[rstd_sem], 1)

            def qnorm(n):
                pool.wait_ge(s["rqsum"], n + 1)
                q = QS[:, n % 2, :].rearrange("p (g d) -> p g d", d=KD)
                pool.tensor_tensor(q, q, rqsum[:, n % 2, :].unsqueeze(2).broadcast_to([P, 32, KD]), ALU.mult)\
                    .then_inc(s["qnorm"], 1)

            def ulo(n):
                p, g, k = n // 4, n % 4, n % 2
                pool.wait_ge(s["uhi"], n + 1)
                hi = f32(US[:, k, :, 0, :]).rearrange("p (j b) c -> p b j c", b=2)
                lo = US[:, k, :, 1, :].rearrange("p (j b) c -> p b j c", b=2)
                for i in range(2):
                    ins = pool.tensor_tensor(lo[:, i], U[:, 2 * p + i, UT_ * g:UT_ * g + UT_, :], hi[:, i],
                                             ALU.subtract)
                ins.then_inc(s["ulo"], 1)

            pool.memset(spare[:, 0:1], 0.0).then_inc(s["f_out"], 1)
            for c in range(2):
                pool.memset(spare[:, c + 1:c + 2], 0.0).then_inc(s[f"f_stored{c}"], 16)
            pool.wait_ge(s["memsets"], 1)
            for i in range(-S1_LEAD, UNITS + 4):
                if 1 <= i <= UNITS:
                    qnorm(i - 1)
                if 2 <= i <= UNITS + 1:
                    n = i - 2
                    rstd(var2[:, n % 2, :], rstd2[:, n % 2, :], 4, n + 1, "var2", "rstd2")
                if 3 <= i <= UNITS + 2:
                    ulo(i - 3)
                if (i + 2) % 4 == 0 and 0 <= (i + 2) // 4 < PAIRS:
                    rstd(var1[:, :], rstd1[:, :], 2 * TILES, (i + 2) // 4 + 1, "var1", "rstd1")

            pool.wait_ge(s["router_act"], ROUTER_ACT)
            pool.wait_ge(s["ld_ffn0"], LD_FFN0)
            pool.wait_ge(s["t_res"], UNITS)
            with pool.Fori(0, B) as b:
                pool.tensor_tensor(image(U, b), image(U, b),
                                   B2A_b[:, bass.ds(b, 1), :].broadcast_to([P, TILES, C]),
                                   ALU.add).then_inc(s["u_biased"], 1)
                pool.tensor_tensor(image(T, b), image(T, b), BETA[:, :].unsqueeze(1).broadcast_to([P, TILES, C]),
                                   ALU.add).then_inc(s["t_beta"], 1)

            def lo_part(whole, parts, have, b, sig):
                pool.wait_ge(s[have], b + 1)
                pool.tensor_tensor(parts[:, :, 1, :], whole[:, :, :], f32(parts[:, :, 0, :]), ALU.subtract)\
                    .then_inc(s[sig], 1)

            def period(b, do_b, do_a):
                if do_a:
                    rstd(varA[:, :], rstdA[:, :], TILES, 2 * (b + 2) + 1, "a_var", "a_rstd")
                    pool.wait_ge(s["a_zn"], b + 2 + 1)
                    pool.tensor_tensor(ZG[:, :, :], ZN[:, :, :],
                                       GAMMA[:, :].unsqueeze(1).broadcast_to([P, TILES, C]), ALU.mult)\
                        .then_inc(s["a_zg"], 1)
                if do_b:
                    rstd(varB[:, :], rstdB[:, :], TILES, b + 1 + 1, "b_var", "b_rstd")
                if do_a:
                    rstd(varA[:, :], rstdA[:, :], TILES, 2 * (b + 2) + 2, "a_var", "a_rstd")
                if do_b:
                    lo_part(EN, ES, "b_ehi", b + 1, "b_elo")
                if do_a:
                    lo_part(V, VS, "a_vhi", b + 2, "a_vlo")

            period(-2, False, True)
            period(-1, True, True)
            with pool.Fori(0, B - 2) as b:
                period(b, True, True)
            period(B - 2, True, False)

        @block.tensor
        def _(pe):
            mm = pe.matmul

            def centre(p):
                if p == 0:
                    pe.wait_ge(s["ld_const"], 16)
                    pe.wait_ge(s["ld_x0"], 16)
                else:
                    pe.wait_ge(s["ld_x"], 16)
                    pe.wait_ge(s["m"], p)
                for t in range(TILES):
                    ins = mm(SA[:, t * P:(t + 1) * P], XC[:, p, t * P:(t + 1) * P], cen, start=True, stop=True)
                ins.then_inc(s["centred"], 1)

            def xn_to_channels(p):
                pe.wait_ge(s["xn_tok"], p + 1)
                for t in range(TILES):
                    ins = pe.transpose(SA[:, t * P:(t + 1) * P], XNT[:, t, :], ident)
                ins.then_inc(s["xnT"], 1)

            def keys_values(p):
                pe.wait_ge(s["xn"], p + 1)
                if p == 0:
                    pe.wait_ge(s["ld_att"], LD_ATT)
                for h in range(2):
                    ins = mm(ps[0:C, h, :], WKV[:, :], XN[:, p % 2, h * HALF:(h + 1) * HALF], start=True, stop=True)
                ins.then_inc(s["kv_ps"], 1)

            def kv_to_tokens(p):
                pe.wait_ge(s["kexp"], p + 1)
                for t in range(TILES):
                    ins = pe.transpose(SA[:, t * C:(t + 1) * C], KV[:, t * P:(t + 1) * P], ident[0:C, 0:C])
                ins.then_inc(s["kvT_ps"], 1)

            def context(p):
                pe.wait_ge(s["kvT"], p + 1)
                for t in range(TILES):
                    ins = mm(ps[0:32, 1, 0:32], KVT[:, t, 0:32], KVT[:, t, 32:64], start=(t == 0), stop=(t == TILES - 1))
                ins.then_inc(s["ctx"], 1)

            def context_turned(p):
                pe.wait_ge(s["z"], 2 * (p + 1))
                mm(ps[:, 0, 0:32], Z[:, :, :].rearrange("p h e -> p (h e)"), ident[0:32, 0:32], start=True, stop=True)\
                    .then_inc(s["ctxT"], 1)

            def context_out(p):
                pe.wait_ge(s["bd"], p + 1)
                if p == 0:
                    pe.wait_ge(s["set_wocev"], 1)
                for i in range(2):
                    ins = mm(ps[:, 1, i * P:(i + 1) * P], BD[:, i].rearrange("p h d -> p (h d)"), WOC[:, :],
                             start=True, stop=True)
                ins.then_inc(s["m_ps"], 1)

            def queries(n):
                p, g = n // 4, n % 4
                q = ps[:, Q_BANK[n % 2], :]
                pe.wait_ge(s["xn"], p + 1)
                if n == 0:
                    pe.wait_ge(s["ld_att"], LD_ATT)
                    pe.wait_ge(s["set_dve"], SET_BQ)
                    pe.wait_ge(s["memsets"], 5)
                if n >= 2:
                    pe.wait_ge(s["qsub"], n - 1)
                mm(q, ones_r[:, :], BQR, start=True, stop=False)
                for j in range(UT_):
                    t = UT_ * g + j
                    ins = mm(q[:, j * 256:(j + 1) * 256], XN[:, p % 2, t * P:(t + 1) * P], WQB[:, :],
                             start=False, stop=(j == UT_ - 1))
                ins.then_inc(s["q_ps"], 1)

            def q_to_channels(n):
                pe.wait_ge(s["qnorm"], n + 1)
                if n >= 1:
                    pe.wait_ge(s["qT"], n)
                for r in range(4):
                    ins = pe.transpose(ps[:, QT_BANK, r * P:(r + 1) * P], QS[:, n % 2, r * P:(r + 1) * P], ident)
                ins.then_inc(s["qT_ps"], 1)

            def attend(n):
                p, g = n // 4, n % 4
                a = ps[:, AT_BANK[n % 2], :]
                pe.wait_ge(s["m"], p + 1)
                if n == 0:
                    pe.wait_ge(s["set_dve"], SET_BO)
                if n >= 2:
                    pe.wait_ge(s["u"], n - 1)
                mm(a, ones_r[:, :], BOR, start=True, stop=False)
                for j in range(UT_):
                    t = UT_ * g + j
                    mm(a[:, j * 256:(j + 1) * 256], XC[:, p, t * P:(t + 1) * P], ic, start=False, stop=False)
                pe.wait_ge(s["qT"], n + 1)
                for r in range(4):
                    ins = mm(a[:, r * P:(r + 1) * P], QT[:, n % 2, r, :], M[:, p % 2, r % 2, :],
                             start=False, stop=(r == 3))
                ins.then_inc(s["att"], 1)

            def u_to_channels(n):
                pe.wait_ge(s["ulo"], n + 1)
                if n >= 1:
                    pe.wait_ge(s["uT"], n)
                for r in range(4):
                    ins = pe.transpose(ps[:, UT_BANK, r * P:(r + 1) * P].bitcast(F32R),
                                       US[:, n % 2, r].rearrange("p k c -> p (k c)"), ident_r[:, :])
                ins.then_inc(s["uT_ps"], 1)

            pe.wait_ge(s["ld_const"], 16)
            pe.wait_ge(s["ld_att"], LD_ATT)
            mm(ps[:, 6, 0:P], WOUT[:, :], ic[0:C, 0:P], start=True, stop=True).then_inc(s["set_woc"], 1)
            mm(ps[0:C, 7, 0:P], BOUT2[:, :], ic[0:C, 0:P], start=True, stop=True).then_inc(s["set_bo"], 1)
            for i in range(-S1_LEAD, UNITS + 4):
                if (i - 1) % 4 == 0 and 0 <= (i - 1) // 4 < PAIRS:
                    context_turned((i - 1) // 4)
                    context_out((i - 1) // 4)
                if i % 4 == 0 and 0 <= i // 4 < PAIRS:
                    kv_to_tokens(i // 4)
                    context(i // 4)
                if (i + 3) % 4 == 0 and 0 <= (i + 3) // 4 < PAIRS:
                    centre((i + 3) // 4)
                if (i + 2) % 4 == 0 and 0 <= (i + 2) // 4 < PAIRS:
                    xn_to_channels((i + 2) // 4)
                if (i + 1) % 4 == 0 and 0 <= (i + 1) // 4 < PAIRS:
                    keys_values((i + 1) // 4)
                if 0 <= i + 1 < UNITS:
                    queries(i + 1)
                if 1 <= i <= UNITS:
                    q_to_channels(i - 1)
                    attend(i - 1)
                if 3 <= i <= UNITS + 2:
                    u_to_channels(i - 3)

            pe.wait_ge(s["ld_ffn0"], LD_FFN0)
            pe.wait_ge(s["qT"], UNITS)
            pe.wait_ge(s["qsub"], UNITS)
            for e in range(E):
                ins = mm(ps[:, Q_BANK[0], e * C:(e + 1) * C], W2TA[:, e, :], ic[0:C, C:P], start=True, stop=True)
            ins.then_inc(s["set_w2"], 1)
            mm(ps[0:E, Q_BANK[1], 0:C], B2TA[:, :], ic[0:C, C:P], start=True, stop=True).then_inc(s["set_w2"], 1)
            rp = steps_of(pe, s["router_pe"])
            r_ps = ps[:, QT_BANK, :]
            pe.wait_ge(s["router_dve"], RD_U8)
            rp.done(mm(r_ps[0:E, 0:E], u8[:, :], WR[:, :], start=True, stop=True))
            pe.wait_ge(s["router_dve"], RD_P1)
            rp.done(mm(r_ps[0:E, 0:E], ones[:, 0:E], R[:, 1, :], start=True, stop=True))
            pe.wait_ge(s["router_dve"], RD_WD)
            rp.done(pe.transpose(r_ps[0:E, 0:E], R[:, 12, :], ident[0:E, 0:E]))
            rp.done(mm(ps[:, UT_BANK, 0:4 * B], ones[:, :], D2[:, :, :].rearrange("p b k -> p (b k)"),
                       start=True, stop=True))
            pe.wait_ge(s["router_dve"], RD_WDT)
            pe.wait_ge(s["set_b2ev"], 1)
            rp.done(mm(r_ps[0:E, 0:C], wdT[:, :], B2A[:, :], start=True, stop=True))
            pe.wait_ge(s["router_dve"], RD_D1)
            rp.done(mm(r_ps[:, :], ones[:, :], D1[:, :, :].rearrange("p b c -> p (b c)"), start=True, stop=True))

            def a_hidden(b):
                pe.wait_ge(s["a_sel"], 2 * (b + 1))
                for n in range(4):
                    k, c = n // 2, n % 2
                    if n >= 2:
                        pe.wait_ge(s["a_gelu"], 4 * b + n - 1)
                    h = ps[:, A_BANK[n % 2], :]
                    for part in range(2):
                        ins = mm(h, W1S[:, k, part, :],
                                 UTR[:, bass.ds(b, 1), c * HALF:(c + 1) * HALF].rearrange("p a n -> p (a n)"),
                                 start=(part == 0), stop=(part == 1))
                    ins.then_inc(s["a_h"], 1)

            def a_output(b):
                pe.wait_ge(s["a_gelu"], 4 * b + 4)
                for t in range(TILES):
                    for k in range(2):
                        ins = mm(ps[:, A_BANK[0], t * C:(t + 1) * C], HA[:, k, t * P:(t + 1) * P], W2S[:, k, :],
                                 start=(k == 0), stop=(k == 1))
                ins.then_inc(s["a_z_ps"], 1)

            def a_to_channels(b):
                pe.wait_ge(s["a_vlo"], b + 1)
                for h in range(2):
                    for j in range(4):
                        ins = pe.transpose(ps[:, A_BANK[h], j * P:(j + 1) * P].bitcast(F32R),
                                           VS[:, 4 * h + j].rearrange("p k c -> p (k c)"), ident_r[:, :])
                    ins.then_inc(s["a_vT"], 1)

            def b_convolve(b, par):
                pe.wait_ge(s["a_img"], 2 * b + 2)
                for c in range(2):
                    for tap in range(TAPS):
                        dy, dx = tap // 3, tap % 3
                        ins = mm(ps[0:C, B_BANK[c], :], WC[:, tap, :],
                                 VP[:, par, 16 * c + dy:16 * c + dy + 16, dx:dx + W],
                                 start=(tap == 0), stop=(tap == TAPS - 1))
                    ins.then_inc(s["b_conv"], 1)

            def b_to_tokens(b):
                pe.wait_ge(s["b_cv"], 2 * (b + 1))
                for j in range(4):
                    ins = pe.transpose(ps[:, B_BANK[0], j * P:(j + 1) * P], CV[:, j * P:(j + 1) * P], ident)
                ins.then_inc(s["b_cvT"], 1)

            def b_to_channels(b):
                pe.wait_ge(s["b_elo"], b + 1)
                for h in range(2):
                    for j in range(4):
                        ins = pe.transpose(ps[:, B_BANK[h], j * P:(j + 1) * P].bitcast(F32R),
                                           ES[:, 4 * h + j].rearrange("p k c -> p (k c)"), ident_r[:, :])
                    ins.then_inc(s["b_eT"], 1)

            def b_gates(b, par):
                pe.wait_ge(s["b_et"], 2 * (b + 1))
                for t in range(TILES):
                    for part in range(2):
                        ins = mm(ps[:, B_BANK[0], t * E:(t + 1) * E], ET[:, par, t * P:(t + 1) * P], GW[:, part, :],
                                 start=(part == 0), stop=(part == 1))
                ins.then_inc(s["b_gate"], 1)

            def b_gates_turned(b):
                pe.wait_ge(s["b_cw"], 2 * (b + 1))
                for h in range(2):
                    for j in range(4):
                        ins = pe.transpose(ps[0:32, B_BANK[h], j * P:(j + 1) * P].bitcast(F32R),
                                           CWS[:, 4 * h + j].rearrange("p k e -> p (k e)"), ident_r[:, :])
                    ins.then_inc(s["b_cwT"], 1)

            acc = ps[:, ACC_BANK, :]

            def f_hidden(b, par, m):
                c, e = m // E, m % E
                if m == 0:
                    pe.wait_ge(s["b_cwt"], 2 * (b + 1))
                if m >= 2:
                    pe.wait_ge(s["f_gelu"], 16 * b + m - 1)
                for part in range(2):
                    ins = mm(ps[:, H_BANK[m % 2], :], W1B[:, e, part, :], ET[:, par, c * HALF:(c + 1) * HALF],
                             start=(part == 0), stop=(part == 1))
                ins.then_inc(s["f_h"], 1)

            def f_gate(b, par, m):
                c, e = m // E, m % E
                if m >= 1:
                    pe.wait_ge(s["f_hg"], 16 * b + m)
                mm(ps[:, CW_BANK, :], SEL[:, e, :], CWT[:, par, c * HALF:(c + 1) * HALF], start=True, stop=True)\
                    .then_inc(s["f_cw"], 1)

            def f_start(b, par, c):
                pe.wait_ge(s["f_out"], 2 * b + c + 1)
                mm(acc, B2B[:, :], CWT[:, par, c * HALF:(c + 1) * HALF], start=True, stop=False, skip_group_check=True)
                for j in range(4):
                    mm(acc[0:C, j * P:(j + 1) * P], TF[:, par, 4 * c + j, :], ident, start=False, stop=False,
                       skip_group_check=True)

            def f_output(b, m):
                pe.wait_ge(s["f_hg"], 16 * b + m + 2)
                last = m % E == E - 2
                for k in range(2):
                    ins = mm(acc[k * C:(k + 1) * C, :], W2B[:, (m + k) % E, :], HG[:, (m + k) % 4, :],
                             start=False, stop=last, skip_group_check=True)
                ins.then_inc(s["f_w2"], 1)

            def period(b, do_f, do_b, do_a, par):
                for j in range(9):
                    if do_f and j < 8:
                        f_hidden(b, par, 2 * j)
                    if do_a and j == 0:
                        a_hidden(b + 2)
                    if do_b and j == 0:
                        b_convolve(b + 1, 1 - par)
                    if do_f and j < 8:
                        f_gate(b, par, 2 * j)
                        if j:
                            f_output(b, 2 * j - 2)
                        if j % 4 == 0:
                            f_start(b, par, j // 4)
                        f_hidden(b, par, 2 * j + 1)
                        f_gate(b, par, 2 * j + 1)
                    elif do_f:
                        f_output(b, 14)
                    if do_a:
                        if j == 1:
                            a_output(b + 2)
                        if j == 6:
                            a_to_channels(b + 2)
                    if do_b:
                        if j == 1:
                            b_to_tokens(b + 1)
                        if j == 4:
                            b_to_channels(b + 1)
                        if j == 5:
                            b_gates(b + 1, 1 - par)
                        if j == 8:
                            b_gates_turned(b + 1)

            pe.wait_ge(s["router_act"], ROUTER_ACT)
            period(-2, False, False, True, 0)
            pe.wait_ge(s["set_dve"], SET_F1)
            period(-1, False, True, True, 1)
            with pe.Fori(0, (B - 2) // 2) as i:
                for par in range(2):
                    period(pe.snap(2 * i + par), True, True, True, par)
            period(B - 2, True, True, False, 0)
            period(B - 1, True, False, False, 1)

        @block.vector
        def _(vec):
            vr = vec.tensor_reduce
            tt = vec.tensor_tensor
            st = steps_of(vec, s["set_dve"])

            def split(hi, lo, whole):
                st.done(vec.tensor_copy(hi, whole))
                st.wait()
                st.done(tt(lo, whole, f32(hi), ALU.subtract))

            def bias_rows(rows, src):
                view = rows.rearrange("p (k n) -> p k n", n=P)
                src = src.unsqueeze(1).broadcast_to([C, 4, P])
                st.done(vec.tensor_copy(view, src))
                st.wait()
                st.done(tt(view[32:C], src[32:C], f32(view[32:C]), ALU.subtract))

            def set_attention():
                vec.wait_ge(s["ld_const"], 16)
                st.done(vec.tensor_copy(ident_r[:, :], ident))
                vec.wait_ge(s["ld_att"], LD_ATT)
                bias_rows(BQR, BQ2[:, :])
                assert st.n == SET_BQ
                vec.wait_ge(s["set_bo"], 1)
                bias_rows(BOR, ps[0:C, 7, 0:P])
                assert st.n == SET_BO

            def set_layer0():
                vec.wait_ge(s["ld_ffn0"], LD_FFN0)
                split(W1A[:, :, 0, :], W1A[:, :, 1, :], W1stage[:, :, :])
                assert st.n == SET_W1A

            def set_conv():
                vec.wait_ge(s["ld_conv"], 16)
                st.done(vec.tensor_scalar(WCstage, WCstage, 0.0, 2.0, ALU.is_gt, ALU.mult))
                st.wait()
                st.done(vec.tensor_scalar(WC[:, :, :], WCstage, -1.0, None, ALU.add))
                assert st.n == SET_SIGNS
                vec.wait_ge(s["ld_conv"], 32)
                st.done(vr(CSCALE[:, :], WCS, X, ALU.add, apply_absolute_value=True))
                st.wait()
                st.done(vec.tensor_scalar(CSCALE[:, :], CSCALE[:, :], 1.0 / (C * TAPS), None, ALU.mult))
                assert st.n == SET_CONV

            def set_layer1():
                vec.wait_ge(s["ld_w1b"], 16)
                split(W1B[:, :, 0, :], W1B[:, :, 1, :], W1stage[:, :, :])
                assert st.n == SET_W1B
                vec.wait_ge(s["ld_ffn1"], LD_FFN1)
                split(GW[:, 0, :], GW[:, 1, :], GWstage[:, :])
                split(B2hi[:, :], B2lo[:, :], B2stage[:, :])
                st.wait()
                vec.wait_ge(s["memsets"], 5)
                st.done(vec.tensor_scalar(B2lo[:, :], B2lo[:, :], hlmask[:, 1:2], None, ALU.mult))
                st.wait()
                st.done(vec.scalar_tensor_tensor(B2B[:, 0:C], f32(B2hi[:, :]), hlmask[:, 0:1], B2lo[:, :],
                                                 ALU.mult, ALU.add))
                vec.wait_ge(s["ld_sel"], 16)
                st.done(vec.tensor_copy(SEL[:, :, :], SELstage))
                assert st.n == SET_F1, st.n

            def variance(ss, var, eps, k, ss_sem, var_sem):
                vec.wait_ge(s[ss_sem], k)
                vec.tensor_scalar(var, ss, 1.0 / C, eps, ALU.mult, ALU.add).then_inc(s[var_sem], 1)

            def sum_squares1(p):
                vec.wait_ge(s["sq1"], p + 1)
                vr(ss1[:, :], SQ1[:, :, :].rearrange("p t (b c) -> p (t b) c", b=2), X, ALU.add).then_inc(s["ss1"], 1)
                variance(ss1[:, :], var1[:, :], LN_C_EPS, p + 1, "ss1", "var1")

            def normalise1(p):
                vec.wait_ge(s["rstd1"], p + 1)
                tt(XNT[:, :, :].rearrange("p t (b c) -> p (t b) c", b=2), SA.rearrange("p (t c) -> p t c", c=C),
                   rstd1[:, :].unsqueeze(2).broadcast_to([P, 2 * TILES, C]), ALU.mult).then_inc(s["xn_tok"], 1)

            def key_max(p):
                vec.wait_ge(s["kv"], p + 1)
                vr(nkmax[:, :], KV[0:32, :], X, ALU.max, negate=True).then_inc(s["kmax"], 1)

            def key_norm(p):
                vec.wait_ge(s["kexp"], p + 1)
                vec.reciprocal(rksum[:, :], ksum[:, :]).then_inc(s["rk"], 1)
                vec.wait_ge(s["rk"], 2 * p + 1)
                vec.tensor_scalar(r01[:, :], pairmask, rksum[:, 0:1], None, ALU.mult).then_inc(s["rk"], 1)

            def pick_context(p):
                vec.wait_ge(s["ctx"], p + 1)
                vec.wait_ge(s["rk"], 2 * p + 2)
                own = [ps[0:32, 1, i * KD:(i + 1) * KD].unsqueeze(1).broadcast_to([32, HEADS, KD]) for i in range(2)]
                vec.tensor_scalar(Z[:, :, :], own[0], r01[:, 0:1], None, ALU.mult).then_inc(s["z"], 1)
                vec.wait_ge(s["z"], 2 * p + 1)
                vec.scalar_tensor_tensor(Z[:, :, :], own[1], r01[:, 1:2], Z[:, :, :], ALU.mult, ALU.add)\
                    .then_inc(s["z"], 1)

            def block_diagonal(p):
                vec.wait_ge(s["ctxT"], p + 1)
                for i in range(2):
                    ins = tt(BD[:, i], ps[:, 0, i * KD:(i + 1) * KD].unsqueeze(1).broadcast_to([P, HEADS, KD]),
                             headmask.unsqueeze(2).broadcast_to([P, HEADS, KD]), ALU.mult)
                ins.then_inc(s["bd"], 1)

            def query_max(n):
                q = ps[:, Q_BANK[n % 2], :].rearrange("p (g d) -> p g d", d=KD)
                vec.wait_ge(s["q_ps"], n + 1)
                vr(qmax[:, :], q, X, ALU.max).then_inc(s["qmax"], 1)
                vec.wait_ge(s["qmax"], n + 1)
                if n >= 2:
                    vec.wait_ge(s["qT_ps"], n - 1)
                tt(QS[:, n % 2, :].rearrange("p (g d) -> p g d", d=KD), q,
                   qmax[:, :].unsqueeze(2).broadcast_to([P, 32, KD]), ALU.subtract).then_inc(s["qsub"], 1)

            def query_sum(n):
                vec.wait_ge(s["qexp"], n + 1)
                vr(qsum[:, :], QS[:, n % 2, :].rearrange("p (g d) -> p g d", d=KD), X, ALU.add).then_inc(s["qsum"], 1)
                vec.wait_ge(s["qsum"], n + 1)
                vec.reciprocal(rqsum[:, n % 2, :], qsum[:, :]).then_inc(s["rqsum"], 1)

            def sum_squares2(n):
                vec.wait_ge(s["sq2"], n + 1)
                vr(ss2[:, n % 2, :], SQ2[:, n % 2], X, ALU.add).then_inc(s["ss2"], 1)
                variance(ss2[:, n % 2, :], var2[:, n % 2, :], LN_T_EPS, n + 1, "ss2", "var2")

            def normalise2(n):
                p, g, k = n // 4, n % 4, n % 2
                a = ps[:, AT_BANK[k], :].rearrange("p (j b x c) -> p b j x c", j=UT_, b=2, x=2)
                r = rstd2[:, k, :].rearrange("p (j b) -> p b j", b=2)
                vec.wait_ge(s["rstd2"], n + 1)
                for i in range(2):
                    ins = tt(U[:, 2 * p + i, UT_ * g:UT_ * g + UT_, :], a[:, i, :, 1, :],
                             r[:, i].unsqueeze(2).broadcast_to([P, UT_, C]), ALU.mult)
                ins.then_inc(s["u"], 1)
                vec.wait_ge(s["u"], n + 1)
                if n >= 2:
                    vec.wait_ge(s["uT_ps"], n - 1)
                vec.tensor_copy(US[:, k, :, 0, :].rearrange("p (j b) c -> p b j c", b=2),
                                U[:, 2 * p:2 * p + 2, UT_ * g:UT_ * g + UT_, :]).then_inc(s["uhi"], 1)

            set_attention()
            for i in range(-S1_LEAD, UNITS + 4):
                if 0 <= i < UNITS:
                    query_max(i)
                if 1 <= i <= UNITS:
                    query_sum(i - 1)
                if (i - 1) % 4 == 0 and 0 <= (i - 1) // 4 < PAIRS:
                    block_diagonal((i - 1) // 4)
                if i % 4 == 0 and 0 <= i // 4 < PAIRS:
                    key_norm(i // 4)
                    pick_context(i // 4)
                if 2 <= i <= UNITS + 1:
                    sum_squares2(i - 2)
                if (i + 2) % 4 == 0 and 0 <= (i + 2) // 4 < PAIRS:
                    sum_squares1((i + 2) // 4)
                if 3 <= i <= UNITS + 2:
                    normalise2(i - 3)
                if (i + 2) % 4 == 0 and 0 <= (i + 2) // 4 < PAIRS:
                    normalise1((i + 2) // 4)
                if (i + 1) % 4 == 0 and 0 <= (i + 1) // 4 < PAIRS:
                    key_max((i + 1) // 4)
                if i == 3:
                    set_layer0()
                if i == 5:
                    set_conv()
                if i == 7:
                    set_layer1()

            rd = steps_of(vec, s["router_dve"])
            vec.wait_ge(s["uT"], UNITS)
            rd.done(vr(u8[:, :], usum[:, :, :], X, ALU.add))
            assert rd.n == RD_U8
            vec.wait_ge(s["router_pe"], 1)
            rd.done(vec.scalar_tensor_tensor(R[:, 0, :], ps[0:E, QT_BANK, 0:E], 1.0 / S, BR[:, :], ALU.mult, ALU.add))

            def softmax(src, dst, m, a_step):
                rd.wait()
                rd.done(vr(RV[:, m], R[:, src, :], X, ALU.max, negate=True))
                vec.wait_ge(s["router_act"], a_step)
                rd.done(vec.reciprocal(RV[:, m + 2], RV[:, m + 1]))
                rd.wait()
                rd.done(vec.tensor_scalar(R[:, dst, :], R[:, dst, :], RV[:, m + 2], None, ALU.mult))

            softmax(0, 1, 0, 1)
            assert rd.n == RD_P1
            vec.wait_ge(s["router_pe"], 2)
            rd.done(vec.tensor_scalar(R[:, 2, :], ps[0:E, QT_BANK, 0:E], float(S), None, ALU.mult))
            rd.wait()
            rd.done(vec.tensor_scalar(R[:, 3, :], R[:, 2, :], CAPACITY, None, ALU.max))
            rd.wait()
            rd.done(vec.reciprocal(R[:, 4, :], R[:, 3, :]))
            rd.wait()
            rd.done(vec.tensor_scalar(R[:, 4, :], R[:, 4, :], CAPACITY, -1.0, ALU.mult, ALU.add))
            rd.done(vec.tensor_scalar(R[:, 5, :], R[:, 2, :], CAPACITY, None, ALU.is_gt))
            rd.wait()
            rd.done(tt(R[:, 4, :], R[:, 4, :], R[:, 5, :], ALU.mult))
            rd.wait()
            rd.done(vec.scalar_tensor_tensor(R[:, 6, :], R[:, 4, :], 1.0, R[:, 1, :], ALU.add, ALU.mult))
            softmax(6, 7, 3, 2)
            top2(vec, rd, E, 1, R[:, 7:8, :], rev[0:E, :], RV[:, 6], R[:, 13:14, :], R[:, 14:15, :],
                 Rq[:, :, :], R[:, 8:9, :], R[:, 9:10, :], R[:, 10:11, :])
            rd.wait()
            rd.done(tt(R[:, 15, :], R[:, 8, :], R[:, 10, :], ALU.subtract))
            rd.wait()
            rd.done(tt(R[:, 16, :], R[:, 15, :], R[:, 7, :], ALU.mult))
            rd.wait()
            rd.done(vr(RV[:, 7], R[:, 16, :], X, ALU.add))
            assert rd.n == RD_DIFF, rd.n
            vec.wait_ge(s["router_act"], 3)
            rd.done(vec.tensor_scalar(RV[:, 9], RV[:, 8], 1.0, None, ALU.add))
            rd.wait()
            rd.done(vec.reciprocal(vals[:, 0:1], RV[:, 9]))
            rd.wait()
            rd.done(tt(vals[:, 1:2], RV[:, 8], vals[:, 0:1], ALU.mult))
            rd.done(vec.tensor_scalar(vals[:, 2:4], Rq[:, :, 0], -1.0, float(E), ALU.mult, ALU.add))
            rd.wait()
            rd.done(vec.tensor_scalar(R[:, 11, :], R[:, 8, :], vals[:, 0:1], None, ALU.mult))
            rd.wait()
            rd.done(vec.scalar_tensor_tensor(R[:, 12, :], R[:, 10, :], vals[:, 1:2], R[:, 11, :], ALU.mult, ALU.add))
            rd.done(tt(D2[:, :, :], vals[:, :].unsqueeze(1).broadcast_to([E, B, 4]),
                       ident[0:E, 0:B].unsqueeze(2).broadcast_to([E, B, 4]), ALU.mult))
            assert rd.n == RD_WD, rd.n
            vec.wait_ge(s["router_pe"], 4)
            rd.done(vec.tensor_copy(wdT[:, :], ps[0:E, QT_BANK, 0:E]))
            assert rd.n == RD_WDT, rd.n
            rd.done(vec.tensor_copy(WI[:, :, :].rearrange("p b k -> p (b k)"), ps[:, UT_BANK, 0:4 * B]))
            rd.wait()
            rd.done(vec.tensor_copy(IDX[:, :].rearrange("p (b k) -> p b k", k=2), WI[0:1, :, 2:4]))
            assert rd.n == RD_IDX, rd.n
            vec.wait_ge(s["router_pe"], 5)
            rd.done(vec.tensor_copy(b2row[:, :], ps[0:E, QT_BANK, 0:C]))
            rd.wait()
            rd.done(tt(D1[:, :, :], b2row[:, :].unsqueeze(1).broadcast_to([E, B, C]),
                       ident[0:E, 0:B].unsqueeze(2).broadcast_to([E, B, C]), ALU.mult))
            assert rd.n == RD_D1, rd.n

            def bcast(col):
                return col.unsqueeze(2).broadcast_to([P, TILES, C])

            def a_sum(b):
                vec.wait_ge(s["a_z_ps"], b + 1)
                vec.wait_ge(s["u_biased"], b + 1)
                tt(ZA[:, :, :], ps[:, A_BANK[0], :].rearrange("p (t c) -> p t c", c=C), image(U, b), ALU.add)\
                    .then_inc(s["a_z"], 1)

            def a_sum_squares(b, k):
                vec.wait_ge(s["a_sq"], 2 * b + k + 1)
                vr(ssA[:, :], SQA[:, :, :], X, ALU.add).then_inc(s["a_ss"], 1)
                variance(ssA[:, :], varA[:, :], (LN_T_EPS, LN_C_EPS)[k], 2 * b + k + 1, "a_ss", "a_var")

            def a_residual(b):
                vec.wait_ge(s["a_rstd"], 2 * b + 1)
                tt(ZN[:, :, :], ZA[:, :, :], bcast(rstdA[:, :]), ALU.mult).then_inc(s["a_zn"], 1)
                vec.wait_ge(s["a_zg"], b + 1)
                vec.wait_ge(s["t_beta"], b + 1)
                tt(TA[:, :, :], image(T, b), ZG[:, :, :], ALU.add).then_inc(s["a_t"], 1)
                vec.wait_ge(s["a_t"], b + 1)
                vr(sumA[:, :], TA[:, :, :], X, ALU.add).then_inc(s["a_sum"], 1)
                vec.wait_ge(s["a_sum"], b + 1)
                vec.scalar_tensor_tensor(XA[:, :, :], bcast(sumA[:, :]), -1.0 / C, TA[:, :, :], ALU.mult, ALU.add)\
                    .then_inc(s["a_xc"], 1)

            def a_normalise(b):
                vec.wait_ge(s["a_rstd"], 2 * b + 2)
                tt(V[:, :, :], XA[:, :, :], bcast(rstdA[:, :]), ALU.mult).then_inc(s["a_v"], 1)
                vec.wait_ge(s["a_v"], b + 1)
                vec.tensor_copy(VS[:, :, 0, :], V[:, :, :]).then_inc(s["a_vhi"], 1)

            def b_residual(b, par):
                vec.wait_ge(s["b_cvT"], b + 1)
                for h in range(2):
                    ins = tt(TF[:, par, 4 * h:4 * h + 4], TA[:, 4 * h:4 * h + 4, :],
                             ps[:, B_BANK[0], :].rearrange("p (j h c) -> p h j c", h=2, c=C)[:, h], ALU.add)
                ins\
                    .then_inc(s["b_t"], 1)
                vec.wait_ge(s["b_t"], b + 1)
                vr(sumB[:, :], TF[:, par], X, ALU.add).then_inc(s["b_sum"], 1)
                vec.wait_ge(s["b_sum"], b + 1)
                vec.scalar_tensor_tensor(XB[:, :, :], bcast(sumB[:, :]), -1.0 / C, TF[:, par], ALU.mult, ALU.add)\
                    .then_inc(s["b_xc"], 1)

            def b_sum_squares(b):
                vec.wait_ge(s["b_sq"], b + 1)
                vr(ssB[:, :], SQB[:, :, :], X, ALU.add).then_inc(s["b_ss"], 1)
                variance(ssB[:, :], varB[:, :], LN_T_EPS, b + 1, "b_ss", "b_var")

            def b_normalise(b):
                vec.wait_ge(s["b_rstd"], b + 1)
                tt(EN[:, :, :], XB[:, :, :], bcast(rstdB[:, :]), ALU.mult).then_inc(s["b_en"], 1)
                vec.wait_ge(s["b_en"], b + 1)
                vec.tensor_copy(ES[:, :, 0, :], EN[:, :, :]).then_inc(s["b_ehi"], 1)

            def b_logits(b):
                vec.wait_ge(s["b_gate"], b + 1)
                steps = steps_of(vec, s["b_lg"], 3 * b)
                steps.done(tt(G[:, 0], ps[:, B_BANK[0], 0:TILES * E].rearrange("p (t e) -> p t e", e=E), GBB[:, :, :],
                              ALU.add))
                steps.wait()
                steps.done(vr(gv[:, 0, :], G[:, 0], X, ALU.max))
                steps.wait()
                steps.done(tt(G[:, 1], G[:, 0], gv[:, 0, :].unsqueeze(2).broadcast_to([P, TILES, E]), ALU.subtract))

            def b_top2(b):
                vec.wait_ge(s["b_exp"], b + 1)
                steps = steps_of(vec, s["b_top"], (TOP2_STEPS + 5) * b)
                steps.done(vr(gv[:, 1, :], G[:, 1], X, ALU.add))
                steps.wait()
                steps.done(vec.reciprocal(gv[:, 2, :], gv[:, 1, :]))
                steps.wait()
                steps.done(tt(G[:, 2], G[:, 1], gv[:, 2, :].unsqueeze(2).broadcast_to([P, TILES, E]), ALU.mult))
                top2(vec, steps, P, TILES, G[:, 2], rev, gv[:, 3, :], G[:, 3], G[:, 4], gq, G[:, 5], G[:, 6], G[:, 7])
                steps.wait()
                steps.done(tt(G[:, 8], G[:, 5], G[:, 7], ALU.add))
                steps.wait()
                steps.done(tt(G[:, 9], G[:, 8], G[:, 2], ALU.mult))
                steps.wait()
                assert steps.n == TOP2_STEPS + 5
                cw = G[:, 9].unsqueeze(2).broadcast_to([P, TILES, 2, E])
                vec.tensor_copy(CWS[:, :, 0::2, :], cw).then_inc(s["b_cw"], 1)
                vec.wait_ge(s["b_cw"], 2 * b + 1)
                tt(CWS[:, :, 1::2, :], cw, f32(CWS[:, :, 0::2, :]), ALU.subtract).then_inc(s["b_cw"], 1)

            def f_gated(b, m):
                vec.wait_ge(s["f_gelu"], 16 * b + m + 1)
                vec.wait_ge(s["f_cw"], 16 * b + m + 1)
                if m >= 4:
                    vec.wait_ge(s["f_w2"], 8 * b + m // 2 - 1)
                tt(HG[:, m % 4, :], HB[:, m % 2, :], ps[:, CW_BANK, :], ALU.mult).then_inc(s["f_hg"], 1)

            def f_result(b, c):
                vec.wait_ge(s["f_odd"], 2 * b + c + 1)
                vec.wait_ge(s[f"f_stored{c}"], 16 * b + 16)
                tt(OUT[:, c, :], OO[:, :], ps[0:C, ACC_BANK, :], ALU.add).then_inc(s["f_out"], 1)

            def period(b, do_f, do_b, do_a, par):
                for j in range(9):
                    if do_f and j < 8:
                        f_gated(b, 2 * j)
                        if j == 4:
                            f_result(b, 0)
                        f_gated(b, 2 * j + 1)
                    if do_a:
                        if j == 1:
                            a_sum(b + 2)
                        if j == 2:
                            a_sum_squares(b + 2, 0)
                        if j == 3:
                            a_residual(b + 2)
                        if j == 4:
                            a_sum_squares(b + 2, 1)
                        if j == 5:
                            a_normalise(b + 2)
                    if do_b:
                        if j == 1:
                            b_residual(b + 1, 1 - par)
                        if j == 2:
                            b_sum_squares(b + 1)
                        if j == 3:
                            b_normalise(b + 1)
                        if j == 5:
                            b_logits(b + 1)
                        if j == 6:
                            b_top2(b + 1)
                    if do_f and j == 8:
                        f_result(b, 1)

            period(-2, False, False, True, 0)
            period(-1, False, True, True, 1)
            with vec.Fori(0, (B - 2) // 2) as i:
                for par in range(2):
                    period(vec.snap(2 * i + par), True, True, True, par)
            period(B - 2, True, True, False, 0)
            period(B - 1, True, False, False, 1)

        @block.scalar
        def _(act):
            av = act.activation

            def square1(p):
                act.wait_ge(s["centred"], p + 1)
                av(SQ1[:, :, :].rearrange("p t c -> p (t c)"), SA, ACT.Square).then_inc(s["sq1"], 1)

            def channels1(p):
                act.wait_ge(s["xnT"], p + 1)
                if p >= 2:
                    act.wait_ge(s["q_ps"], 4 * (p - 1))
                av(XN[:, p % 2, :], SA, ACT.Copy).then_inc(s["xn"], 1)

            def keys_values(p):
                act.wait_ge(s["kv_ps"], p + 1)
                if p >= 1:
                    act.wait_ge(s["kvT_ps"], p)
                av(KV[:, :], SA[0:C, :], ACT.Identity, bias=BKV[:, 0:1]).then_inc(s["kv"], 1)

            def key_exp(p):
                act.wait_ge(s["kmax"], p + 1)
                av(KV[0:32, :], KV[0:32, :], ACT.Exp, bias=nkmax[:, 0:1], accum_out=ksum[:, 0:1])\
                    .then_inc(s["kexp"], 1)

            def tokens_kv(p):
                act.wait_ge(s["kvT_ps"], p + 1)
                av(KVT[:, :, :].rearrange("p t c -> p (t c)"), SA[:, 0:TILES * C], ACT.Copy).then_inc(s["kvT"], 1)

            def outputs(p):
                act.wait_ge(s["m_ps"], p + 1)
                if p >= 2:
                    act.wait_ge(s["att"], 4 * (p - 1))
                av(M[:, p % 2].rearrange("p i n -> p (i n)"), ps[:, 1, 0:2 * P], ACT.Copy).then_inc(s["m"], 1)

            def query_exp(n):
                act.wait_ge(s["qsub"], n + 1)
                av(QS[:, n % 2, :], QS[:, n % 2, :], ACT.Exp).then_inc(s["qexp"], 1)

            def query_channels(n):
                act.wait_ge(s["qT_ps"], n + 1)
                if n >= 2:
                    act.wait_ge(s["att"], n - 1)
                av(QT[:, n % 2].rearrange("p r n -> p (r n)"), ps[:, QT_BANK, :], ACT.Copy).then_inc(s["qT"], 1)

            def residual(n):
                p, g, k = n // 4, n % 4, n % 2
                a = ps[:, AT_BANK[k], :].rearrange("p (j b x c) -> p j b x c", j=UT_, b=2, x=2)
                act.wait_ge(s["att"], n + 1)
                for i in range(2):
                    ins = av(T[:, 2 * p + i, UT_ * g:UT_ * g + UT_, :], a[:, :, i, 0, :], ACT.Copy)
                ins.then_inc(s["t_res"], 1)
                if n >= 2:
                    act.wait_ge(s["ss2"], n - 1)
                av(SQ2[:, k], ps[:, AT_BANK[k], :].rearrange("p (r x c) -> p r x c", x=2, c=C)[:, :, 1, :], ACT.Square)\
                    .then_inc(s["sq2"], 1)

            def u_channels(n):
                p, g = n // 4, n % 4
                act.wait_ge(s["uT_ps"], n + 1)
                src = ps[:, UT_BANK, :].rearrange("p (j b n) -> p j b n", j=UT_, b=2)
                for i in range(2):
                    ins = av(UTR[:, 2 * p + i, UT_ * g * P:UT_ * (g + 1) * P].rearrange("p (j n) -> p j n", n=P),
                             src[:, :, i, :], ACT.Copy, accum_out=usum[:, 2 * p + i, g:g + 1])
                ins.then_inc(s["uT"], 1)

            act.wait_ge(s["set_woc"], 1)
            av(WOC[:, :], ps[:, 6, 0:P], ACT.Copy).then_inc(s["set_wocev"], 1)
            for i in range(-S1_LEAD, UNITS + 4):
                if (i - 1) % 4 == 0 and 0 <= (i - 1) // 4 < PAIRS:
                    outputs((i - 1) // 4)
                if i % 4 == 0 and 0 <= i // 4 < PAIRS:
                    tokens_kv(i // 4)
                if (i + 3) % 4 == 0 and 0 <= (i + 3) // 4 < PAIRS:
                    square1((i + 3) // 4)
                if 0 <= i < UNITS:
                    query_exp(i)
                if 1 <= i <= UNITS:
                    query_channels(i - 1)
                    residual(i - 1)
                if (i + 2) % 4 == 0 and 0 <= (i + 2) // 4 < PAIRS:
                    channels1((i + 2) // 4)
                if (i + 1) % 4 == 0 and 0 <= (i + 1) // 4 < PAIRS:
                    keys_values((i + 1) // 4)
                    key_exp((i + 1) // 4)
                if 3 <= i <= UNITS + 2:
                    u_channels(i - 3)

            act.wait_ge(s["set_w2"], 2)
            av(W2A[:, :, :].rearrange("p e c -> p (e c)"), ps[:, Q_BANK[0], :], ACT.Copy).then_inc(s["set_w2ev"], 1)
            av(B2A[:, :], ps[0:E, Q_BANK[1], 0:C], ACT.Copy).then_inc(s["set_b2ev"], 1)
            act.wait_ge(s["router_dve"], RD_MAX1)
            av(R[:, 1, :], R[:, 0, :], ACT.Exp, bias=RV[:, 0], accum_out=RV[:, 1]).then_inc(s["router_act"], 1)
            act.wait_ge(s["router_dve"], RD_MAX2)
            av(R[:, 7, :], R[:, 6, :], ACT.Exp, bias=RV[:, 3], accum_out=RV[:, 4]).then_inc(s["router_act"], 1)
            act.wait_ge(s["router_dve"], RD_DIFF)
            av(RV[:, 8], RV[:, 7], ACT.Exp, scale=-1.0).then_inc(s["router_act"], 1)
            act.wait_ge(s["router_pe"], 6)
            av(B2A_b[:, :, :].rearrange("p b c -> p (b c)"), ps[:, QT_BANK, :], ACT.Copy).then_inc(s["router_act"], 1)

            def a_select(b):
                act.wait_ge(s["a_z_ps"], b)
                for k in range(2):
                    e = act.value_load(IDX[0:1, bass.ds(2 * b + k, 1)], min_val=0, max_val=E - 1)
                    av(W1S[:, k], f32(W1A[:, bass.ds(e, 1), :, :]).rearrange("p a k f -> p (a k) f"), ACT.Copy)
                    av(B1S[:, k:k + 1], B1A[:, bass.ds(e, 1)], ACT.Copy)
                    av(W2S[:, k, :], W2A[:, bass.ds(e, 1), :].rearrange("p a c -> p (a c)"), ACT.Copy,
                       scale=WI[:, bass.ds(b, 1), k:k + 1].rearrange("p a k -> p (a k)")).then_inc(s["a_sel"], 1)

            def a_gelu(b):
                for n in range(4):
                    k, c = n // 2, n % 2
                    if n == 0:
                        act.wait_ge(s["a_sel"], 2 * (b + 1))
                    act.wait_ge(s["a_h"], 4 * b + n + 1)
                    av(HA[:, k, c * HALF:(c + 1) * HALF], ps[:, A_BANK[n % 2], :], ACT.Gelu, bias=B1S[:, k:k + 1])\
                        .then_inc(s["a_gelu"], 1)

            def a_square(b, k):
                act.wait_ge(s[("a_z", "a_xc")[k]], b + 1)
                av(SQA[:, :, :], (ZA, XA)[k][:, :, :], ACT.Square).then_inc(s["a_sq"], 1)

            def a_image(b, par, first_image):
                for h in range(2):
                    act.wait_ge(s["a_vT"], 2 * b + h + 1)
                    if h == 0 and not first_image:
                        act.wait_ge(s["b_conv"], 2 * b - 2)
                    av(VP[:, par, 16 * h + 1:16 * h + 17, 1:W + 1],
                       ps[:, A_BANK[h], :].rearrange("p (y x) -> p y x", x=W), ACT.Copy).then_inc(s["a_img"], 1)

            def b_scale(b):
                for c in range(2):
                    act.wait_ge(s["b_conv"], 2 * b + c + 1)
                    av(CV[c * C:(c + 1) * C, :], ps[0:C, B_BANK[c], :], ACT.Copy, scale=CSCALE[:, 0:1])\
                        .then_inc(s["b_cv"], 1)

            def b_square(b):
                act.wait_ge(s["b_xc"], b + 1)
                av(SQB[:, :, :], XB[:, :, :], ACT.Square).then_inc(s["b_sq"], 1)

            def b_channels(b, par):
                for h in range(2):
                    act.wait_ge(s["b_eT"], 2 * b + h + 1)
                    av(ET[:, par, h * HALF:(h + 1) * HALF], ps[:, B_BANK[h], :], ACT.Copy).then_inc(s["b_et"], 1)

            def b_exp(b):
                act.wait_ge(s["b_lg"], 3 * b + 3)
                av(G[:, 1], G[:, 1], ACT.Exp).then_inc(s["b_exp"], 1)

            def b_gates(b, par):
                for h in range(2):
                    act.wait_ge(s["b_cwT"], 2 * b + h + 1)
                    av(CWT[:, par, h * HALF:(h + 1) * HALF], ps[0:32, B_BANK[h], :], ACT.Copy)\
                        .then_inc(s["b_cwt"], 1)

            def f_gelu(b, m):
                act.wait_ge(s["f_h"], 16 * b + m + 1)
                if m >= 2:
                    act.wait_ge(s["f_hg"], 16 * b + m - 1)
                av(HB[:, m % 2, :], ps[:, H_BANK[m % 2], :], ACT.Gelu, bias=B1B[:, m % E:m % E + 1])\
                    .then_inc(s["f_gelu"], 1)

            def f_odd(b, c):
                act.wait_ge(s["f_w2"], 8 * b + 4 * c + 4)
                av(OO[:, :], ps[C:P, ACC_BANK, :], ACT.Copy).then_inc(s["f_odd"], 1)

            def period(b, do_f, do_b, do_a, par):
                if do_a:
                    a_select(b + 2)
                for j in range(9):
                    if do_f and j < 8:
                        f_gelu(b, 2 * j)
                    if do_a and j == 0:
                        a_gelu(b + 2)
                    if do_b and j == 0:
                        b_scale(b + 1)
                    if do_f and j == 4:
                        f_odd(b, 0)
                    if do_f and j < 8:
                        f_gelu(b, 2 * j + 1)
                    if do_a:
                        if j == 1:
                            a_square(b + 2, 0)
                        if j == 3:
                            a_square(b + 2, 1)
                        if j == 6:
                            a_image(b + 2, par, not do_f)
                    if do_b:
                        if j == 1:
                            b_square(b + 1)
                        if j == 4:
                            b_channels(b + 1, 1 - par)
                        if j == 5:
                            b_exp(b + 1)
                        if j == 8:
                            b_gates(b + 1, 1 - par)
                    if do_f and j == 8:
                        f_odd(b, 1)

            act.wait_ge(s["router_dve"], RD_IDX)
            period(-2, False, False, True, 0)
            period(-1, False, True, True, 1)
            with act.Fori(0, (B - 2) // 2) as i:
                for par in range(2):
                    period(act.snap(2 * i + par), True, True, True, par)
            period(B - 2, True, True, False, 0)
            period(B - 1, True, False, False, 1)


S1_LEAD = 3
RD_U8, RD_MAX1, RD_P1 = 1, 3, 5
RD_MAX2 = 13
RD_DIFF = 15 + TOP2_STEPS + 3
RD_WD = RD_DIFF + 7
RD_WDT = RD_WD + 1
RD_IDX = RD_WDT + 2
RD_D1 = RD_IDX + 2
ROUTER_ACT = 4


def constants():
    k = np.zeros((P, K_N), np.float32)
    eye = np.eye(C, dtype=np.float32)
    c = eye - np.float32(1.0 / C)
    k[:, K_ID:K_ID + P] = np.eye(P)
    for i in range(2):
        rows = slice(i * C, (i + 1) * C)
        k[rows, K_CEN + i * C:K_CEN + (i + 1) * C] = c
        k[rows, K_IC + i * P:K_IC + i * P + C] = eye
        k[rows, K_IC + i * P + C:K_IC + (i + 1) * P] = c
        k[i * KD:(i + 1) * KD, K_PAIR + i] = 1.0
        k[i * KD:(i + 1) * KD, K_HL + i] = 1.0
    for h in range(HEADS):
        k[h * KD:(h + 1) * KD, K_HEAD + h] = 1.0
    k[:, K_REV:K_REV + E] = np.arange(E, 0, -1)
    sel = np.zeros((32, E, P), np.float32)
    for e in range(E):
        sel[e, e] = sel[E + e, e] = 1.0
    return k, sel


def kernel(**inputs):
    import concourse.bacc as bacc
    from concourse.bass_utils import run_bass_kernel_spmd

    a = {k: np.ascontiguousarray(v) for k, v in inputs.items()}
    k, sel = constants()
    wq, wk, wv = a["L0_conv_Wq"].T, a["L0_conv_Wk"].T, a["L0_conv_Wv"].T
    wqb = np.zeros((P, 256), np.float32)
    wkv = np.zeros((P, C), np.float32)
    bkv = np.zeros((C, 1), np.float32)
    for i in range(2):
        rows = slice(i * C, (i + 1) * C)
        wqb[rows, i * P:(i + 1) * P] = wq
        wkv[rows, i * KD:(i + 1) * KD] = wk
        wkv[rows, 32 + i * KD:32 + (i + 1) * KD] = wv
        bkv[i * KD:(i + 1) * KD, 0] = a["L0_conv_bk"]
        bkv[32 + i * KD:32 + (i + 1) * KD, 0] = a["L0_conv_bv"]
    bq2 = np.zeros((C, P), np.float32)
    bq2[0::32] = a["L0_conv_bq"]
    bout2 = np.zeros((C, C), np.float32)
    bout2[:, 0::32] = a["L0_conv_bout"][:, None]

    def twice(w):
        return np.concatenate([w, w])

    w = a["L1_conv_weight"]
    arrays = dict(
        x=a["x"].reshape(B, C, S), consts=k, wqb=wqb, bq2=bq2, wkv=wkv, bkv=bkv, wout=a["L0_conv_Wout"],
        bout2=bout2, wr=twice(a["L0_ffn_Wr"]), br=np.tile(a["L0_ffn_br"], (B, 1)),
        w1a=twice(a["L0_ffn_W1"].transpose(1, 0, 2)), b1a=a["L0_ffn_b1"].T,
        w2ta=a["L0_ffn_W2"].transpose(2, 0, 1), b2ta=a["L0_ffn_b2"].T,
        gammab=np.tile(a["L0_ffn_gamma"], (P, 1)), betab=np.tile(a["L0_ffn_beta"], (P, 1)),
        wconv=twice(w.transpose(1, 2, 3, 0).reshape(C, TAPS, C)), wcs=w.reshape(C, C * TAPS),
        gw=twice(a["L1_ffn_gate_w"]), gbb=np.tile(a["L1_ffn_gate_b"], (P, TILES, 1)),
        w1b=twice(a["L1_ffn_W1"].transpose(1, 0, 2)), b1b=a["L1_ffn_b1"].T,
        w2b=a["L1_ffn_W2"].transpose(1, 0, 2), b2b=np.tile(a["L1_ffn_b2"], (4, 1)), selb=sel,
    )
    nc = bacc.Bacc("TRN2", target_bir_lowering=False, num_devices=1)
    arrays = {f"in_{n}": np.ascontiguousarray(v) for n, v in arrays.items()}
    args = [nc.dram_tensor(n, v.shape, mybir.dt.from_np(v.dtype), kind="ExternalInput").ap()
            for n, v in arrays.items()]
    out = nc.dram_tensor("out", (B, C, S), F32, kind="ExternalOutput").ap()
    build(nc, *args, out)
    r = run_bass_kernel_spmd(nc, [arrays], core_ids=[0])
    return r.results[0]["out"].reshape(B, C, H, W)
```

```python
from contextlib import ExitStack

import numpy as np

import concourse.bass as bass
from concourse import mybir

F32 = mybir.dt.float32
F32R = mybir.dt.float32r
I32 = mybir.dt.int32
ALU = mybir.AluOpType
ACT = mybir.ActivationFunctionType
X = mybir.AxisListType.X

B, C, H, W = 8, 64, 32, 32
S = H * W
P = 128
TILES = S // P
PAIRS = B // 2
HEADS, KD = 8, 16
E, F = 8, 128
UNITS = 4 * PAIRS
UT_ = 2
HALF = S // 2
TAPS = 9
CAPACITY = float(-(-B * S * 5 // (4 * E)))
LN_C_EPS, LN_T_EPS = 1e-6, 1e-5

K_ID, K_CEN, K_IC, K_HEAD, K_REV, K_PAIR, K_HL = 0, 128, 256, 512, 520, 528, 530
K_N = 532


def steps_of(eng, sem, base=0):
    return Steps(eng, sem, base)


class Steps:
    def __init__(self, eng, sem, base):
        self.eng, self.sem, self.base, self.n = eng, sem, base, 0

    def done(self, instruction):
        instruction.then_inc(self.sem, 1)
        self.n += 1

    def wait(self):
        self.eng.wait_ge(self.sem, self.base + self.n)


def ge(eng, sem, value):
    if not isinstance(value, int) or value > 0:
        eng.wait_ge(sem, value)


SLOTS = 16
PLAN = dict(
    pool=(
        "a_zg+1 a_rstd1+1 a_vlo+1 b_rstd+1 b_elo+1 a_rstd0+2"
    ).split(),
    pe=(
        "f_gate14-1 b_conv0+1 a_hidden0+2 b_conv1+1 a_hidden1+2 f_gate15-1 f_hidden0 b_to_tokens+1 a_hidden2+2 "
        "f_output12-1 f_gate0 f_hidden1 a_hidden3+2 f_output14-1 f_gate1 f_hidden2 f_hidden3 f_gate2 a_output+2 "
        "f_gate3 f_hidden4 f_start0 f_output0 f_hidden5 b_to_channels0+1 b_to_channels1+1 f_gate4 f_hidden6 "
        "f_gate5 b_gates+1 f_hidden7 f_gate6 f_output2 f_gate7 f_hidden8 f_output4 f_output6 f_gate8 f_hidden9 "
        "f_hidden10 f_gate9 f_gate10 f_hidden11 f_start1 f_hidden12 f_gate11 f_hidden13 f_output8 a_vT0+2 "
        "f_gate12 f_hidden14 a_vT1+2 f_output10 b_gates_turned0+1 b_gates_turned1+1 f_gate13 f_hidden15"
    ).split(),
    vec=(
        "f_gated15-1 b_residual+1 b_centre+1 f_gated0 b_ss+1 f_gated1 f_result1-1 f_gated2 b_normalise+1 a_sum+2 "
        "f_gated3 a_ss0+2 f_gated4 a_zn+2 f_gated5 b_logits+1 a_residual+2 a_centre+2 f_gated6 f_gated7 b_probs+1 "
        "a_ss1+2 f_gated8 f_result0 f_gated9 a_normalise+2 b_first+1 f_gated10 b_second+1 f_gated11 b_weights+1 "
        "f_gated12 f_gated13 f_gated14"
    ).split(),
    act=(
        "a_select+2 b_scale0+1 f_gelu14-1 a_hidden0+2 f_gelu15-1 b_scale1+1 a_hidden1+2 a_hidden2+2 f_gelu0 "
        "f_gelu1 a_hidden3+2 b_square+1 f_odd1-1 f_gelu2 f_gelu3 f_gelu4 a_square0+2 b_channels0+1 b_channels1+1 "
        "f_gelu5 f_gelu6 f_gelu7 b_exp+1 a_square1+2 f_gelu8 f_odd0 f_gelu9 f_gelu10 f_gelu11 f_gelu12 a_image0+2 "
        "a_image1+2 f_gelu13 b_gates_out0+1 b_gates_out1+1"
    ).split(),
)
MOST_AHEAD = 2


def parts_of(plan):
    for token in plan:
        name = token.rstrip("0123456789").rstrip("+-") if "+" in token or "-" in token else token
        yield name, int(token[len(name):] or 0)


def period(b, par, plan, parts, live):
    for name, ahead in parts_of(plan):
        if live(b, ahead):
            parts[name](b + ahead, (par + ahead) % 2)


def periods(eng, plan, parts):
    def image_exists(b, ahead):
        return 0 <= b + ahead < B

    assert sorted(parts) == sorted(name for name, _ in parts_of(plan))
    for b in range(-MOST_AHEAD, MOST_AHEAD):
        period(b, b % 2, plan, parts, image_exists)
    with eng.Fori(0, (B - 2 * MOST_AHEAD) // 2) as i:
        for par in range(2):
            period(eng.snap(2 * i + (MOST_AHEAD + par)), par, plan, parts, lambda b, ahead: True)
    for b in range(B - MOST_AHEAD, B + MOST_AHEAD):
        period(b, b % 2, plan, parts, image_exists)


def largest(vec, steps, p, n, vals, rev, m, eq, rank, q, onehot):
    wide = [p, n, E]
    steps.wait()
    steps.done(vec.tensor_reduce(m, vals, X, ALU.max))
    steps.wait()
    steps.done(vec.tensor_tensor(eq, vals, m.unsqueeze(2).broadcast_to(wide), ALU.is_equal))
    steps.wait()
    steps.done(vec.tensor_tensor(rank, eq, rev.unsqueeze(1).broadcast_to(wide), ALU.mult))
    steps.wait()
    steps.done(vec.tensor_reduce(q, rank, X, ALU.max))
    steps.wait()
    steps.done(vec.tensor_tensor(onehot, rank, q.unsqueeze(2).broadcast_to(wide), ALU.is_equal))


def without(vec, steps, rest, first, probs):
    steps.wait()
    steps.done(vec.scalar_tensor_tensor(rest, first, -2.0, probs, ALU.mult, ALU.add))


def build(nc, x, consts, wqb, bq2, wkv, bkv, wout, bout2, wr, br, w1a, b1a, w2ta, b2ta, gammab, betab,
          wconv, wcs, gw, gbb, w1b, b1b, w2b, b2b, selb, out):
    ctx = ExitStack()
    with ctx:
        def sb(name, shape, dt=F32):
            return ctx.enter_context(nc.sbuf_tensor(name, shape, dt))

        def tiles(ap):
            return ap.rearrange("p (t c) -> p t c", c=C)

        def sem(name):
            return ctx.enter_context(nc.semaphore(name))

        K = sb("K", [P, K_N])
        ident = K[:, K_ID:K_ID + P]
        cen = K[:, K_CEN:K_CEN + P]
        ic = K[:, K_IC:K_IC + 256]
        headmask = K[:, K_HEAD:K_HEAD + HEADS]
        rev = K[:, K_REV:K_REV + E]
        pairmask = K[0:32, K_PAIR:K_PAIR + 2]
        hlmask = K[0:32, K_HL:K_HL + 2]
        ident_r = sb("ident_r", [P, P], F32R)
        ones_r = sb("ones_r", [C, P], F32R)
        ones = sb("ones", [E, P])
        WQB = sb("WQB", [P, 256])
        BQ2 = sb("BQ2", [C, P])
        CWTB = sb("CWTB", [C, 2 * S], F32R)
        BQR = CWTB[:, 0:512]
        WKV = sb("WKV", [P, C])
        BKV = sb("BKV", [C, 1])
        WOUT = sb("WOUT", [C, P])
        BOUT2 = sb("BOUT2", [C, C])
        WOC = sb("WOC", [P, P])
        BOR = CWTB[:, 512:1024]
        WR = sb("WR", [P, E])
        BR = sb("BR", [E, E])
        W1stage = sb("W1stage", [P, E, F])
        W1A = sb("W1A", [P, E, 2, F], F32R)
        B1A = sb("B1A", [F, E])
        HB = sb("HB", [F, 2, HALF])
        W2TA = HB[0:C, :, :].rearrange("p a (e f) -> p (a e) f", f=F)
        W2A = sb("W2A", [F, E, C])
        B2TA = sb("B2TA", [C, E])
        B2A = sb("B2A", [E, C])
        GAMMA = sb("GAMMA", [P, C])
        BETA = sb("BETA", [P, C])
        WCstage = W1stage[:, 0:5, :].rearrange("p a n -> p (a n)")[:, 0:TAPS * C].rearrange("p (t c) -> p t c", c=C)
        WC = sb("WC", [P, TAPS, C], F32R)
        WCS = W1stage[0:C, 0:5, :].rearrange("p a n -> p (a n)")[:, 0:C * TAPS]
        CSCALE = sb("CSCALE", [C, 1])
        GWstage = sb("GWstage", [P, E])
        GW = sb("GW", [P, 2, E], F32R)
        GBB = sb("GBB", [P, TILES, E])
        W1B = sb("W1B", [P, E, 2, F], F32R)
        B1B = sb("B1B", [F, E])
        W2B = sb("W2B", [F, E, C])
        B2stage = sb("B2stage", [32, C])
        B2hi = sb("B2hi", [32, C], F32R)
        B2lo = sb("B2lo", [32, C])
        B2B = sb("B2B", [32, P], F32R)
        SELstage = W1stage[0:32, :, :]
        SEL = sb("SEL", [32, E, P], F32R)
        XC = sb("XC", [P, PAIRS, S])
        T = sb("T", [P, B, TILES, C])
        U = sb("U", [P, B, TILES, C])
        UTR = sb("UTR", [P, B, S], F32R)
        usum = sb("usum", [P, B, 4])
        SQ1 = sb("SQ1", [P, TILES, P])
        ss1 = sb("ss1", [P, 2 * TILES])
        var1 = sb("var1", [P, 2 * TILES])
        rstd1 = sb("rstd1", [P, 2 * TILES])
        XNT = sb("XNT", [P, TILES, P])
        XN = sb("XN", [P, 2, S])
        KV = sb("KV", [C, S])
        nkmax = sb("nkmax", [32, 1])
        ksum = sb("ksum", [32, 1])
        rksum = sb("rksum", [32, 1])
        r01 = sb("r01", [32, 2])
        KVT = sb("KVT", [P, TILES, C])
        Z = sb("Z", [32, HEADS, KD])
        BD = sb("BD", [P, 2, HEADS, KD])
        M = sb("M", [P, 2, 2, P])
        qmax = sb("qmax", [P, 32])
        QS = sb("QS", [P, 2, 512])
        qsum = sb("qsum", [P, 32])
        rqsum = sb("rqsum", [P, 2, 32])
        QT = sb("QT", [P, 2, 4, P])
        SQ2 = sb("SQ2", [P, 2, 4, C])
        ss2 = sb("ss2", [P, 2, 4])
        var2 = sb("var2", [P, 2, 4])
        rstd2 = sb("rstd2", [P, 2, 4])
        US = sb("US", [P, 2, 4, 2, C], F32R)
        pow_half = sb("pow_half", [P, 2 * TILES])
        u8 = sb("u8", [P, E])
        R = sb("R", [E, 32, E])
        RV = sb("RV", [E, 16, 1])
        Rq = sb("Rq", [E, 2, 1])
        vals = sb("vals", [E, 4])
        D1 = KV[0:E, 0:B * C].rearrange("p (b c) -> p b c", c=C)
        D2 = sb("D2", [E, B, 4])
        wdT = sb("wdT", [E, E])
        b2row = sb("b2row", [E, C])
        WI = sb("WI", [P, B, 4])
        IDX = sb("IDX", [1, B * 2], I32)
        B2A_b = SQ2[:, :, :, :].rearrange("p k r c -> p (k r) c")
        W1S = sb("W1S", [P, 2, 2, F], F32R)
        B1S = sb("B1S", [F, 2])
        W2S = sb("W2S", [F, 2, C])
        HA = XC[:, 0:2, :]
        ZA, SQA, ZN, ZG = (tiles(XN[:, k // 2, (k % 2) * HALF:(k % 2 + 1) * HALF]) for k in range(4))
        ssA = sb("ssA", [P, TILES])
        varA = sb("varA", [P, TILES])
        rstdA = sb("rstdA", [P, TILES])
        sumA = sb("sumA", [P, TILES])
        TA = sb("TA", [P, TILES, C])
        XA = XNT[:, :, 0:C]
        V = XNT[:, :, C:P]
        VS = US[:, :, :, :, :].rearrange("p k r a c -> p (k r) a c")
        VP = sb("VP", [P, 2, H + 2, W + 2], F32R)
        CV = sb("CV", [P, HALF])
        TF = QT[:, :, :, :].rearrange("p k r (a c) -> p k (r a) c", c=C)
        sumB = sb("sumB", [P, TILES])
        XB = SQ1[:, :, 0:C]
        SQB = SQ1[:, :, C:P]
        ssB = sb("ssB", [P, TILES])
        varB = sb("varB", [P, TILES])
        rstdB = sb("rstdB", [P, TILES])
        EN = tiles(QS[:, 0, :])
        ES = sb("ES", [P, TILES, 2, C], F32R)
        ET = sb("ET", [P, 2, S], F32R)
        G = sb("G", [P, 10, TILES, E])
        gv = sb("gv", [P, 4, TILES])
        gq = sb("gq", [P, 2, TILES])
        CWS = sb("CWS", [P, TILES, 4, E], F32R)
        CWT = CWTB[0:32, :].rearrange("p (k n) -> p k n", k=2)
        HG = XC[:, 2:4, :].rearrange("p a (k n) -> p (a k) n", k=2)
        OO = QS[0:C, 1, :]
        OUT = W1stage[0:C, :, :].rearrange("p (c a) n -> p c (a n)", c=2)

        ps = ctx.enter_context(nc.psum_tensor("ps", [P, 8, HALF], F32))

        s = {name: sem(name) for name in (
            "ld_const", "ld_x0", "ld_x", "ld_att", "ld_ffn0", "ld_conv", "ld_ffn1", "ld_w1b", "ld_sel", "memsets", "set_dve", "set_w2",
            "set_woc", "set_bo", "set_wocev", "set_w2ev", "set_b2ev",
            "centred", "sq1", "ss1", "var1", "rstd1", "xn_tok", "xnT", "xn", "kv_ps", "kv", "kmax", "kexp",
            "rk", "kvT_ps", "kvT", "ctx", "z", "ctxT", "bd", "m_ps", "m",
            "q_ps", "qmax", "qsub", "qexp", "qsum", "rqsum", "qnorm", "qT_ps", "qT", "att", "t_res", "sq2",
            "ss2", "var2", "rstd2", "u", "uhi", "ulo", "uT_ps", "uT",
            "router_dve", "router_pe", "router_act", "u_biased", "t_beta",
            "a_sel", "a_h", "a_gelu", "a_z_ps", "a_z", "a_sq", "a_ss", "a_var", "a_rstd", "a_zn", "a_zg", "a_t",
            "a_sum", "a_xc", "a_v", "a_vhi", "a_vlo", "a_vT", "a_img",
            "b_conv", "b_cv", "b_cvT", "b_t", "b_sum", "b_xc", "b_sq", "b_ss", "b_var", "b_rstd", "b_en", "b_ehi",
            "b_elo", "b_eT", "b_et", "b_gate", "b_lg", "b_exp", "b_top", "b_cw", "b_cwT", "b_cwt",
            "f_h", "f_gelu", "f_cw", "f_hg", "f_w2", "f_acc", "f_odd", "f_out", "f_stored0", "f_stored1",
        )}
        block = ctx.enter_context(nc.Block())

        SA = ps[:, 0:2, :].rearrange("p a n -> p (a n)")
        Q_BANK, QT_BANK, AT_BANK, UT_BANK = (2, 3), 4, (5, 6), 7
        A_BANK, B_BANK, H_BANK, CW_BANK, ACC_BANK = 0, (1, 2), (3, 4), (5, 6), 7

        def image(tile, b):
            return tile[:, bass.ds(b, 1), :, :].rearrange("p a t c -> p (a t) c")

        def f32(ap):
            return ap.bitcast(F32)

        SET_BQ, SET_BO, SET_W1A, SET_SIGNS, SET_CONV, SET_W1B, SET_F1 = 3, 5, 7, 9, 11, 13, 20
        LD_ATT, LD_FFN0, LD_FFN1 = 6 * 16, 8 * 16, 5 * 16

        @block.sync
        def _(sp):
            xp = x.rearrange("(q i) c n -> q (i c) n", i=2)
            sp.dma_start(K[:, :], consts).then_inc(s["ld_const"], 16)
            sp.dma_start(XC[:, 0, :], xp[0]).then_inc(s["ld_x0"], 16)
            for dst, src in ((WKV[:, :], wkv), (BKV[:, :], bkv), (WQB[:, :], wqb), (BQ2[:, :], bq2),
                             (WOUT[:, :], wout), (BOUT2[:, :], bout2)):
                sp.dma_start(dst, src).then_inc(s["ld_att"], 16)
            sp.dma_start(XC[:, 1:PAIRS, :], xp[1:PAIRS].rearrange("q p n -> p q n")).then_inc(s["ld_x"], 16)
            for dst, src in ((WR[:, :], wr), (BR[:, :], br), (W1stage[:, :, :], w1a), (B1A[:, :], b1a),
                             (W2TA[:, :, :], w2ta), (B2TA[:, :], b2ta), (GAMMA[:, :], gammab), (BETA[:, :], betab)):
                sp.dma_start(dst, src).then_inc(s["ld_ffn0"], 16)
            for dst, src in ((GWstage[:, :], gw), (GBB[:, :, :], gbb), (B1B[:, :], b1b),
                             (W2B[:, :, :], w2b), (B2stage[:, :], b2b)):
                sp.dma_start(dst, src).then_inc(s["ld_ffn1"], 16)
            for dst, src, step, sig in ((WCstage, wconv, SET_W1A, "ld_conv"), (WCS, wcs, SET_SIGNS, "ld_conv"),
                                        (W1stage[:, :, :], w1b, SET_CONV, "ld_w1b"),
                                        (SELstage, selb, SET_W1B, "ld_sel")):
                sp.wait_ge(s["set_dve"], step)
                sp.dma_start(dst, src).then_inc(s[sig], 16)

            def store(b):
                for c in range(2):
                    sp.wait_ge(s["f_out"], 2 * b + c + 1)
                    sp.dma_start(out[bass.ds(b, 1), :, c * HALF:(c + 1) * HALF].rearrange("a c n -> c (a n)"),
                                 OUT[:, c, :]).then_inc(s[f"f_stored{c}"], 16)

            with sp.Fori(0, B) as b:
                store(b)
            for c in range(2):
                sp.wait_ge(s[f"f_stored{c}"], 16 * B)

        @block.gpsimd
        def _(pool):
            for tile, value in ((pow_half[:, :], -0.5), (ones[:, :], 1.0), (f32(ones_r[:, :]), 1.0),
                                (f32(VP[:, :, :, :]), 0.0), (f32(B2B[:, :]), 0.0)):
                pool.memset(tile, value).then_inc(s["memsets"], 1)

            def rstd(var, out_, n, k, var_sem, rstd_sem):
                pool.wait_ge(s[var_sem], k)
                pool.tensor_tensor(out_, var, pow_half[:, 0:n], ALU.pow).then_inc(s[rstd_sem], 1)

            def qnorm(n):
                pool.wait_ge(s["rqsum"], n + 1)
                q = QS[:, n % 2, :].rearrange("p (g d) -> p g d", d=KD)
                pool.tensor_tensor(q, q, rqsum[:, n % 2, :].unsqueeze(2).broadcast_to([P, 32, KD]), ALU.mult)\
                    .then_inc(s["qnorm"], 1)

            def ulo(n):
                p, g, k = n // 4, n % 4, n % 2
                pool.wait_ge(s["uhi"], n + 1)
                hi = f32(US[:, k, :, 0, :]).rearrange("p (j b) c -> p b j c", b=2)
                lo = US[:, k, :, 1, :].rearrange("p (j b) c -> p b j c", b=2)
                for i in range(2):
                    ins = pool.tensor_tensor(lo[:, i], U[:, 2 * p + i, UT_ * g:UT_ * g + UT_, :], hi[:, i],
                                             ALU.subtract)
                ins.then_inc(s["ulo"], 1)

            pool.wait_ge(s["memsets"], 1)
            for i in range(-S1_LEAD, UNITS + 4):
                if 1 <= i <= UNITS:
                    qnorm(i - 1)
                if 2 <= i <= UNITS + 1:
                    n = i - 2
                    rstd(var2[:, n % 2, :], rstd2[:, n % 2, :], 4, n + 1, "var2", "rstd2")
                if 3 <= i <= UNITS + 2:
                    ulo(i - 3)
                if (i + 2) % 4 == 0 and 0 <= (i + 2) // 4 < PAIRS:
                    rstd(var1[:, :], rstd1[:, :], 2 * TILES, (i + 2) // 4 + 1, "var1", "rstd1")

            pool.wait_ge(s["router_act"], ROUTER_ACT)
            pool.wait_ge(s["ld_ffn0"], LD_FFN0)
            pool.wait_ge(s["t_res"], UNITS)
            with pool.Fori(0, B) as b:
                pool.tensor_tensor(image(U, b), image(U, b),
                                   B2A_b[:, bass.ds(b, 1), :].broadcast_to([P, TILES, C]),
                                   ALU.add).then_inc(s["u_biased"], 1)
                pool.tensor_tensor(image(T, b), image(T, b), BETA[:, :].unsqueeze(1).broadcast_to([P, TILES, C]),
                                   ALU.add).then_inc(s["t_beta"], 1)

            def lo_part(whole, parts, have, b, sig):
                pool.wait_ge(s[have], b + 1)
                pool.tensor_tensor(parts[:, :, 1, :], whole[:, :, :], f32(parts[:, :, 0, :]), ALU.subtract)\
                    .then_inc(s[sig], 1)

            def a_rstd(k):
                return lambda b, par: rstd(varA[:, :], rstdA[:, :], TILES, 2 * b + k + 1, "a_var", "a_rstd")

            def a_zg(b, par):
                pool.wait_ge(s["a_zn"], b + 1)
                pool.tensor_tensor(ZG, ZN, GAMMA[:, :].unsqueeze(1).broadcast_to([P, TILES, C]), ALU.mult)\
                    .then_inc(s["a_zg"], 1)

            def b_rstd(b, par):
                rstd(varB[:, :], rstdB[:, :], TILES, b + 1, "b_var", "b_rstd")

            def a_vlo(b, par):
                lo_part(V, VS, "a_vhi", b, "a_vlo")

            def b_elo(b, par):
                lo_part(EN, ES, "b_ehi", b, "b_elo")

            periods(pool, PLAN["pool"], dict(
                [("a_rstd0", a_rstd(0)), ("a_rstd1", a_rstd(1)), ("a_zg", a_zg), ("b_rstd", b_rstd),
                           ("a_vlo", a_vlo), ("b_elo", b_elo)]))

        @block.tensor
        def _(pe):
            mm = pe.matmul

            def centre(p):
                if p == 0:
                    pe.wait_ge(s["ld_const"], 16)
                    pe.wait_ge(s["ld_x0"], 16)
                else:
                    pe.wait_ge(s["ld_x"], 16)
                    pe.wait_ge(s["m"], p)
                for t in range(TILES):
                    ins = mm(SA[:, t * P:(t + 1) * P], XC[:, p, t * P:(t + 1) * P], cen, start=True, stop=True)
                ins.then_inc(s["centred"], 1)

            def xn_to_channels(p):
                pe.wait_ge(s["xn_tok"], p + 1)
                for t in range(TILES):
                    ins = pe.transpose(SA[:, t * P:(t + 1) * P], XNT[:, t, :], ident)
                ins.then_inc(s["xnT"], 1)

            def keys_values(p):
                pe.wait_ge(s["xn"], p + 1)
                if p == 0:
                    pe.wait_ge(s["ld_att"], LD_ATT)
                for h in range(2):
                    ins = mm(ps[0:C, h, :], WKV[:, :], XN[:, p % 2, h * HALF:(h + 1) * HALF], start=True, stop=True)
                ins.then_inc(s["kv_ps"], 1)

            def kv_to_tokens(p):
                pe.wait_ge(s["kexp"], p + 1)
                for t in range(TILES):
                    ins = pe.transpose(SA[:, t * C:(t + 1) * C], KV[:, t * P:(t + 1) * P], ident[0:C, 0:C])
                ins.then_inc(s["kvT_ps"], 1)

            def context(p):
                pe.wait_ge(s["kvT"], p + 1)
                for t in range(TILES):
                    ins = mm(ps[0:32, 1, 0:32], KVT[:, t, 0:32], KVT[:, t, 32:64], start=(t == 0), stop=(t == TILES - 1))
                ins.then_inc(s["ctx"], 1)

            def context_turned(p):
                pe.wait_ge(s["z"], 2 * (p + 1))
                mm(ps[:, 0, 0:32], Z[:, :, :].rearrange("p h e -> p (h e)"), ident[0:32, 0:32], start=True, stop=True)\
                    .then_inc(s["ctxT"], 1)

            def context_out(p):
                pe.wait_ge(s["bd"], p + 1)
                if p == 0:
                    pe.wait_ge(s["set_wocev"], 1)
                for i in range(2):
                    ins = mm(ps[:, 1, i * P:(i + 1) * P], BD[:, i].rearrange("p h d -> p (h d)"), WOC[:, :],
                             start=True, stop=True)
                ins.then_inc(s["m_ps"], 1)

            def queries(n):
                p, g = n // 4, n % 4
                q = ps[:, Q_BANK[n % 2], :]
                pe.wait_ge(s["xn"], p + 1)
                if n == 0:
                    pe.wait_ge(s["ld_att"], LD_ATT)
                    pe.wait_ge(s["set_dve"], SET_BQ)
                    pe.wait_ge(s["memsets"], 5)
                if n >= 2:
                    pe.wait_ge(s["qsub"], n - 1)
                mm(q, ones_r[:, :], BQR, start=True, stop=False)
                for j in range(UT_):
                    t = UT_ * g + j
                    ins = mm(q[:, j * 256:(j + 1) * 256], XN[:, p % 2, t * P:(t + 1) * P], WQB[:, :],
                             start=False, stop=(j == UT_ - 1))
                ins.then_inc(s["q_ps"], 1)

            def q_to_channels(n):
                pe.wait_ge(s["qnorm"], n + 1)
                if n >= 1:
                    pe.wait_ge(s["qT"], n)
                for r in range(4):
                    ins = pe.transpose(ps[:, QT_BANK, r * P:(r + 1) * P], QS[:, n % 2, r * P:(r + 1) * P], ident)
                ins.then_inc(s["qT_ps"], 1)

            def attend(n):
                p, g = n // 4, n % 4
                a = ps[:, AT_BANK[n % 2], :]
                pe.wait_ge(s["m"], p + 1)
                if n == 0:
                    pe.wait_ge(s["set_dve"], SET_BO)
                if n >= 2:
                    pe.wait_ge(s["u"], n - 1)
                mm(a, ones_r[:, :], BOR, start=True, stop=False)
                for j in range(UT_):
                    t = UT_ * g + j
                    mm(a[:, j * 256:(j + 1) * 256], XC[:, p, t * P:(t + 1) * P], ic, start=False, stop=False)
                pe.wait_ge(s["qT"], n + 1)
                for r in range(4):
                    ins = mm(a[:, r * P:(r + 1) * P], QT[:, n % 2, r, :], M[:, p % 2, r % 2, :],
                             start=False, stop=(r == 3))
                ins.then_inc(s["att"], 1)

            def u_to_channels(n):
                pe.wait_ge(s["ulo"], n + 1)
                if n >= 1:
                    pe.wait_ge(s["uT"], n)
                for r in range(4):
                    ins = pe.transpose(ps[:, UT_BANK, r * P:(r + 1) * P].bitcast(F32R),
                                       US[:, n % 2, r].rearrange("p k c -> p (k c)"), ident_r[:, :])
                ins.then_inc(s["uT_ps"], 1)

            pe.wait_ge(s["ld_const"], 16)
            pe.wait_ge(s["ld_att"], LD_ATT)
            mm(ps[:, 6, 0:P], WOUT[:, :], ic[0:C, 0:P], start=True, stop=True).then_inc(s["set_woc"], 1)
            mm(ps[0:C, 7, 0:P], BOUT2[:, :], ic[0:C, 0:P], start=True, stop=True).then_inc(s["set_bo"], 1)
            for i in range(-S1_LEAD, UNITS + 4):
                if (i - 1) % 4 == 0 and 0 <= (i - 1) // 4 < PAIRS:
                    context_turned((i - 1) // 4)
                    context_out((i - 1) // 4)
                if i % 4 == 0 and 0 <= i // 4 < PAIRS:
                    kv_to_tokens(i // 4)
                    context(i // 4)
                if (i + 3) % 4 == 0 and 0 <= (i + 3) // 4 < PAIRS:
                    centre((i + 3) // 4)
                if (i + 2) % 4 == 0 and 0 <= (i + 2) // 4 < PAIRS:
                    xn_to_channels((i + 2) // 4)
                if (i + 1) % 4 == 0 and 0 <= (i + 1) // 4 < PAIRS:
                    keys_values((i + 1) // 4)
                if 0 <= i + 1 < UNITS:
                    queries(i + 1)
                if 1 <= i <= UNITS:
                    q_to_channels(i - 1)
                    attend(i - 1)
                if 3 <= i <= UNITS + 2:
                    u_to_channels(i - 3)

            pe.wait_ge(s["ld_ffn0"], LD_FFN0)
            pe.wait_ge(s["qT"], UNITS)
            pe.wait_ge(s["qsub"], UNITS)
            for e in range(E):
                ins = mm(ps[:, Q_BANK[0], e * C:(e + 1) * C], W2TA[:, e, :], ic[0:C, C:P], start=True, stop=True)
            ins.then_inc(s["set_w2"], 1)
            mm(ps[0:E, Q_BANK[1], 0:C], B2TA[:, :], ic[0:C, C:P], start=True, stop=True).then_inc(s["set_w2"], 1)
            rp = steps_of(pe, s["router_pe"])
            r_ps = ps[:, QT_BANK, :]
            pe.wait_ge(s["router_dve"], RD_U8)
            rp.done(mm(r_ps[0:E, 0:E], u8[:, :], WR[:, :], start=True, stop=True))
            pe.wait_ge(s["router_dve"], RD_P1)
            rp.done(mm(r_ps[0:E, 0:E], ones[:, 0:E], R[:, 1, :], start=True, stop=True))
            pe.wait_ge(s["router_dve"], RD_WD)
            rp.done(pe.transpose(r_ps[0:E, 0:E], R[:, 12, :], ident[0:E, 0:E]))
            rp.done(mm(ps[:, UT_BANK, 0:4 * B], ones[:, :], D2[:, :, :].rearrange("p b k -> p (b k)"),
                       start=True, stop=True))
            pe.wait_ge(s["router_dve"], RD_WDT)
            pe.wait_ge(s["set_b2ev"], 1)
            rp.done(mm(r_ps[0:E, 0:C], wdT[:, :], B2A[:, :], start=True, stop=True))
            pe.wait_ge(s["router_dve"], RD_D1)
            rp.done(mm(r_ps[:, :], ones[:, :], D1[:, :, :].rearrange("p b c -> p (b c)"), start=True, stop=True))

            def a_hidden(n):
                def part(b, par):
                    k, c = n // 2, n % 2
                    if n == 0:
                        pe.wait_ge(s["a_sel"], 2 * (b + 1))
                        ge(pe, s["a_img"], 2 * b)
                    else:
                        pe.wait_ge(s["a_gelu"], 4 * b + n)
                    for w in range(2):
                        ins = mm(ps[:, A_BANK, :], W1S[:, k, w, :],
                                 UTR[:, bass.ds(b, 1), c * HALF:(c + 1) * HALF].rearrange("p a n -> p (a n)"),
                                 start=(w == 0), stop=(w == 1))
                    ins.then_inc(s["a_h"], 1)
                return part

            def a_output(b, par):
                pe.wait_ge(s["a_gelu"], 4 * b + 4)
                for t in range(TILES):
                    for k in range(2):
                        ins = mm(ps[:, A_BANK, t * C:(t + 1) * C], HA[:, k, t * P:(t + 1) * P], W2S[:, k, :],
                                 start=(k == 0), stop=(k == 1))
                ins.then_inc(s["a_z_ps"], 1)

            def a_vT(h):
                def part(b, par):
                    pe.wait_ge(s["a_vlo"], b + 1)
                    if h == 1:
                        pe.wait_ge(s["a_img"], 2 * b + 1)
                    for j in range(4):
                        ins = pe.transpose(ps[:, A_BANK, j * P:(j + 1) * P].bitcast(F32R),
                                           VS[:, 4 * h + j].rearrange("p k c -> p (k c)"), ident_r[:, :])
                    ins.then_inc(s["a_vT"], 1)
                return part

            def b_conv(c):
                def part(b, par):
                    if c == 0:
                        pe.wait_ge(s["a_img"], 2 * b + 2)
                        ge(pe, s["b_cwt"], 2 * b)
                    for tap in range(TAPS):
                        dy, dx = tap // 3, tap % 3
                        ins = mm(ps[0:C, B_BANK[c], :], WC[:, tap, :],
                                 VP[:, par, 16 * c + dy:16 * c + dy + 16, dx:dx + W],
                                 start=(tap == 0), stop=(tap == TAPS - 1))
                    ins.then_inc(s["b_conv"], 1)
                return part

            def b_to_tokens(b, par):
                pe.wait_ge(s["b_cv"], 2 * (b + 1))
                for j in range(4):
                    ins = pe.transpose(ps[:, B_BANK[0], j * P:(j + 1) * P], CV[:, j * P:(j + 1) * P], ident)
                ins.then_inc(s["b_cvT"], 1)

            def b_to_channels(h):
                def part(b, par):
                    pe.wait_ge(s["b_elo"], b + 1)
                    for j in range(4):
                        ins = pe.transpose(ps[:, B_BANK[h], j * P:(j + 1) * P].bitcast(F32R),
                                           ES[:, 4 * h + j].rearrange("p k c -> p (k c)"), ident_r[:, :])
                    ins.then_inc(s["b_eT"], 1)
                return part

            def b_gates(b, par):
                pe.wait_ge(s["b_et"], 2 * (b + 1))
                for t in range(TILES):
                    for part in range(2):
                        ins = mm(ps[:, B_BANK[0], t * E:(t + 1) * E], ET[:, par, t * P:(t + 1) * P], GW[:, part, :],
                                 start=(part == 0), stop=(part == 1))
                ins.then_inc(s["b_gate"], 1)

            def b_gates_turned(h):
                def part(b, par):
                    pe.wait_ge(s["b_cw"], 2 * (b + 1))
                    for j in range(4):
                        ins = pe.transpose(ps[0:32, B_BANK[h], j * P:(j + 1) * P].bitcast(F32R),
                                           CWS[:, 4 * h + j].rearrange("p k e -> p (k e)"), ident_r[:, :])
                    ins.then_inc(s["b_cwT"], 1)
                return part

            acc = ps[:, ACC_BANK, :]

            def f_hidden(m):
                c, e = m // E, m % E

                def part(b, par):
                    if m == 0:
                        pe.wait_ge(s["b_cwt"], 2 * (b + 1))
                    ge(pe, s["f_gelu"], 16 * b + m - 1)
                    for w in range(2):
                        ins = mm(ps[:, H_BANK[m % 2], :], W1B[:, e, w, :], ET[:, par, c * HALF:(c + 1) * HALF],
                                 start=(w == 0), stop=(w == 1))
                    ins.then_inc(s["f_h"], 1)
                return part

            def f_gate(m):
                c, e = m // E, m % E

                def part(b, par):
                    ge(pe, s["f_hg"], 16 * b + m - 1)
                    mm(ps[:, CW_BANK[m % 2], :], SEL[:, e, :], CWT[:, par, c * HALF:(c + 1) * HALF],
                       start=True, stop=True).then_inc(s["f_cw"], 1)
                return part

            def f_start(c):
                def part(b, par):
                    ge(pe, s["f_out"], 2 * b + c)
                    mm(acc, B2B[:, :], CWT[:, par, c * HALF:(c + 1) * HALF], start=True, stop=False,
                       skip_group_check=True)
                    for j in range(4):
                        mm(acc[0:C, j * P:(j + 1) * P], TF[:, par, 4 * c + j, :], ident, start=False, stop=False,
                           skip_group_check=True)
                return part

            def f_output(m):
                def part(b, par):
                    pe.wait_ge(s["f_hg"], 16 * b + m + 2)
                    for k in range(2):
                        ins = mm(acc[k * C:(k + 1) * C, :], W2B[:, (m + k) % E, :], HG[:, (m + k) % 4, :],
                                 start=False, stop=(m % E == E - 2), skip_group_check=True)
                    ins.then_inc(s["f_w2"], 1)
                return part

            pe.wait_ge(s["router_act"], ROUTER_ACT)
            pe.wait_ge(s["set_dve"], SET_F1)
            every = range(SLOTS)
            periods(pe, PLAN["pe"], dict(
                [(f"f_hidden{m}", f_hidden(m)) for m in every]
                    + [(f"a_hidden{n}", a_hidden(n)) for n in range(4)]
                    + [("a_output", a_output), ("a_vT0", a_vT(0)), ("a_vT1", a_vT(1)), ("b_conv0", b_conv(0)),
                       ("b_conv1", b_conv(1)), ("b_to_tokens", b_to_tokens), ("b_to_channels0", b_to_channels(0)),
                       ("b_to_channels1", b_to_channels(1)), ("b_gates", b_gates),
                       ("b_gates_turned0", b_gates_turned(0)), ("b_gates_turned1", b_gates_turned(1))]
                    + [(f"f_gate{m}", f_gate(m)) for m in every]
                    + [(f"f_start{c}", f_start(c)) for c in range(2)]
                    + [(f"f_output{m}", f_output(m)) for m in range(0, SLOTS, 2)]))

        @block.vector
        def _(vec):
            vr = vec.tensor_reduce
            tt = vec.tensor_tensor
            st = steps_of(vec, s["set_dve"])

            def split(hi, lo, whole):
                st.done(vec.tensor_copy(hi, whole))
                st.wait()
                st.done(tt(lo, whole, f32(hi), ALU.subtract))

            def bias_rows(rows, src):
                view = rows.rearrange("p (k n) -> p k n", n=P)
                src = src.unsqueeze(1).broadcast_to([C, 4, P])
                st.done(vec.tensor_copy(view, src))
                st.wait()
                st.done(tt(view[32:C], src[32:C], f32(view[32:C]), ALU.subtract))

            def set_attention():
                vec.wait_ge(s["ld_const"], 16)
                st.done(vec.tensor_copy(ident_r[:, :], ident))
                vec.wait_ge(s["ld_att"], LD_ATT)
                bias_rows(BQR, BQ2[:, :])
                assert st.n == SET_BQ
                vec.wait_ge(s["set_bo"], 1)
                bias_rows(BOR, ps[0:C, 7, 0:P])
                assert st.n == SET_BO

            def set_layer0():
                vec.wait_ge(s["ld_ffn0"], LD_FFN0)
                split(W1A[:, :, 0, :], W1A[:, :, 1, :], W1stage[:, :, :])
                assert st.n == SET_W1A

            def set_conv():
                vec.wait_ge(s["ld_conv"], 16)
                st.done(vec.tensor_scalar(WCstage, WCstage, 0.0, 2.0, ALU.is_gt, ALU.mult))
                st.wait()
                st.done(vec.tensor_scalar(WC[:, :, :], WCstage, -1.0, None, ALU.add))
                assert st.n == SET_SIGNS
                vec.wait_ge(s["ld_conv"], 32)
                st.done(vr(CSCALE[:, :], WCS, X, ALU.add, apply_absolute_value=True))
                st.wait()
                st.done(vec.tensor_scalar(CSCALE[:, :], CSCALE[:, :], 1.0 / (C * TAPS), None, ALU.mult))
                assert st.n == SET_CONV

            def set_layer1():
                vec.wait_ge(s["ld_w1b"], 16)
                split(W1B[:, :, 0, :], W1B[:, :, 1, :], W1stage[:, :, :])
                assert st.n == SET_W1B
                vec.wait_ge(s["ld_ffn1"], LD_FFN1)
                split(GW[:, 0, :], GW[:, 1, :], GWstage[:, :])
                split(B2hi[:, :], B2lo[:, :], B2stage[:, :])
                st.wait()
                vec.wait_ge(s["memsets"], 5)
                st.done(vec.tensor_scalar(B2lo[:, :], B2lo[:, :], hlmask[:, 1:2], None, ALU.mult))
                st.wait()
                st.done(vec.scalar_tensor_tensor(B2B[:, 0:C], f32(B2hi[:, :]), hlmask[:, 0:1], B2lo[:, :],
                                                 ALU.mult, ALU.add))
                vec.wait_ge(s["ld_sel"], 16)
                st.done(vec.tensor_copy(SEL[:, :, :], SELstage))
                assert st.n == SET_F1, st.n

            def variance(ss, var, eps, k, ss_sem, var_sem):
                vec.wait_ge(s[ss_sem], k)
                vec.tensor_scalar(var, ss, 1.0 / C, eps, ALU.mult, ALU.add).then_inc(s[var_sem], 1)

            def sum_squares1(p):
                vec.wait_ge(s["sq1"], p + 1)
                vr(ss1[:, :], SQ1[:, :, :].rearrange("p t (b c) -> p (t b) c", b=2), X, ALU.add).then_inc(s["ss1"], 1)
                variance(ss1[:, :], var1[:, :], LN_C_EPS, p + 1, "ss1", "var1")

            def normalise1(p):
                vec.wait_ge(s["rstd1"], p + 1)
                tt(XNT[:, :, :].rearrange("p t (b c) -> p (t b) c", b=2), SA.rearrange("p (t c) -> p t c", c=C),
                   rstd1[:, :].unsqueeze(2).broadcast_to([P, 2 * TILES, C]), ALU.mult).then_inc(s["xn_tok"], 1)

            def key_max(p):
                vec.wait_ge(s["kv"], p + 1)
                vr(nkmax[:, :], KV[0:32, :], X, ALU.max, negate=True).then_inc(s["kmax"], 1)

            def key_norm(p):
                vec.wait_ge(s["kexp"], p + 1)
                vec.reciprocal(rksum[:, :], ksum[:, :]).then_inc(s["rk"], 1)
                vec.wait_ge(s["rk"], 2 * p + 1)
                vec.tensor_scalar(r01[:, :], pairmask, rksum[:, 0:1], None, ALU.mult).then_inc(s["rk"], 1)

            def pick_context(p):
                vec.wait_ge(s["ctx"], p + 1)
                vec.wait_ge(s["rk"], 2 * p + 2)
                own = [ps[0:32, 1, i * KD:(i + 1) * KD].unsqueeze(1).broadcast_to([32, HEADS, KD]) for i in range(2)]
                vec.tensor_scalar(Z[:, :, :], own[0], r01[:, 0:1], None, ALU.mult).then_inc(s["z"], 1)
                vec.wait_ge(s["z"], 2 * p + 1)
                vec.scalar_tensor_tensor(Z[:, :, :], own[1], r01[:, 1:2], Z[:, :, :], ALU.mult, ALU.add)\
                    .then_inc(s["z"], 1)

            def block_diagonal(p):
                vec.wait_ge(s["ctxT"], p + 1)
                for i in range(2):
                    ins = tt(BD[:, i], ps[:, 0, i * KD:(i + 1) * KD].unsqueeze(1).broadcast_to([P, HEADS, KD]),
                             headmask.unsqueeze(2).broadcast_to([P, HEADS, KD]), ALU.mult)
                ins.then_inc(s["bd"], 1)

            def query_max(n):
                q = ps[:, Q_BANK[n % 2], :].rearrange("p (g d) -> p g d", d=KD)
                vec.wait_ge(s["q_ps"], n + 1)
                vr(qmax[:, :], q, X, ALU.max).then_inc(s["qmax"], 1)
                vec.wait_ge(s["qmax"], n + 1)
                if n >= 2:
                    vec.wait_ge(s["qT_ps"], n - 1)
                tt(QS[:, n % 2, :].rearrange("p (g d) -> p g d", d=KD), q,
                   qmax[:, :].unsqueeze(2).broadcast_to([P, 32, KD]), ALU.subtract).then_inc(s["qsub"], 1)

            def query_sum(n):
                vec.wait_ge(s["qexp"], n + 1)
                vr(qsum[:, :], QS[:, n % 2, :].rearrange("p (g d) -> p g d", d=KD), X, ALU.add).then_inc(s["qsum"], 1)
                vec.wait_ge(s["qsum"], n + 1)
                vec.reciprocal(rqsum[:, n % 2, :], qsum[:, :]).then_inc(s["rqsum"], 1)

            def sum_squares2(n):
                vec.wait_ge(s["sq2"], n + 1)
                vr(ss2[:, n % 2, :], SQ2[:, n % 2], X, ALU.add).then_inc(s["ss2"], 1)
                variance(ss2[:, n % 2, :], var2[:, n % 2, :], LN_T_EPS, n + 1, "ss2", "var2")

            def normalise2(n):
                p, g, k = n // 4, n % 4, n % 2
                a = ps[:, AT_BANK[k], :].rearrange("p (j b x c) -> p b j x c", j=UT_, b=2, x=2)
                r = rstd2[:, k, :].rearrange("p (j b) -> p b j", b=2)
                vec.wait_ge(s["rstd2"], n + 1)
                for i in range(2):
                    ins = tt(U[:, 2 * p + i, UT_ * g:UT_ * g + UT_, :], a[:, i, :, 1, :],
                             r[:, i].unsqueeze(2).broadcast_to([P, UT_, C]), ALU.mult)
                ins.then_inc(s["u"], 1)
                vec.wait_ge(s["u"], n + 1)
                if n >= 2:
                    vec.wait_ge(s["uT_ps"], n - 1)
                vec.tensor_copy(US[:, k, :, 0, :].rearrange("p (j b) c -> p b j c", b=2),
                                U[:, 2 * p:2 * p + 2, UT_ * g:UT_ * g + UT_, :]).then_inc(s["uhi"], 1)

            set_attention()
            for i in range(-S1_LEAD, UNITS + 4):
                if 0 <= i < UNITS:
                    query_max(i)
                if 1 <= i <= UNITS:
                    query_sum(i - 1)
                if (i - 1) % 4 == 0 and 0 <= (i - 1) // 4 < PAIRS:
                    block_diagonal((i - 1) // 4)
                if i % 4 == 0 and 0 <= i // 4 < PAIRS:
                    key_norm(i // 4)
                    pick_context(i // 4)
                if 2 <= i <= UNITS + 1:
                    sum_squares2(i - 2)
                if (i + 2) % 4 == 0 and 0 <= (i + 2) // 4 < PAIRS:
                    sum_squares1((i + 2) // 4)
                if 3 <= i <= UNITS + 2:
                    normalise2(i - 3)
                if (i + 2) % 4 == 0 and 0 <= (i + 2) // 4 < PAIRS:
                    normalise1((i + 2) // 4)
                if (i + 1) % 4 == 0 and 0 <= (i + 1) // 4 < PAIRS:
                    key_max((i + 1) // 4)
                if i == 3:
                    set_layer0()
                if i == 5:
                    set_conv()
                if i == 7:
                    set_layer1()

            rd = steps_of(vec, s["router_dve"])
            vec.wait_ge(s["uT"], UNITS)
            rd.done(vr(u8[:, :], usum[:, :, :], X, ALU.add))
            assert rd.n == RD_U8
            vec.wait_ge(s["router_pe"], 1)
            rd.done(vec.scalar_tensor_tensor(R[:, 0, :], ps[0:E, QT_BANK, 0:E], 1.0 / S, BR[:, :], ALU.mult, ALU.add))

            def softmax(src, dst, m, a_step):
                rd.wait()
                rd.done(vr(RV[:, m], R[:, src, :], X, ALU.max, negate=True))
                vec.wait_ge(s["router_act"], a_step)
                rd.done(vec.reciprocal(RV[:, m + 2], RV[:, m + 1]))
                rd.wait()
                rd.done(vec.tensor_scalar(R[:, dst, :], R[:, dst, :], RV[:, m + 2], None, ALU.mult))

            softmax(0, 1, 0, 1)
            assert rd.n == RD_P1
            vec.wait_ge(s["router_pe"], 2)
            rd.done(vec.tensor_scalar(R[:, 2, :], ps[0:E, QT_BANK, 0:E], float(S), None, ALU.mult))
            rd.wait()
            rd.done(vec.tensor_scalar(R[:, 3, :], R[:, 2, :], CAPACITY, None, ALU.max))
            rd.wait()
            rd.done(vec.reciprocal(R[:, 4, :], R[:, 3, :]))
            rd.wait()
            rd.done(vec.tensor_scalar(R[:, 4, :], R[:, 4, :], CAPACITY, -1.0, ALU.mult, ALU.add))
            rd.done(vec.tensor_scalar(R[:, 5, :], R[:, 2, :], CAPACITY, None, ALU.is_gt))
            rd.wait()
            rd.done(tt(R[:, 4, :], R[:, 4, :], R[:, 5, :], ALU.mult))
            rd.wait()
            rd.done(vec.scalar_tensor_tensor(R[:, 6, :], R[:, 4, :], 1.0, R[:, 1, :], ALU.add, ALU.mult))
            softmax(6, 7, 3, 2)
            largest(vec, rd, E, 1, R[:, 7:8, :], rev[0:E, :], RV[:, 6], R[:, 13:14, :], R[:, 14:15, :],
                    Rq[:, 0, :], R[:, 8:9, :])
            without(vec, rd, R[:, 9:10, :], R[:, 8:9, :], R[:, 7:8, :])
            largest(vec, rd, E, 1, R[:, 9:10, :], rev[0:E, :], RV[:, 6], R[:, 13:14, :], R[:, 14:15, :],
                    Rq[:, 1, :], R[:, 10:11, :])
            rd.wait()
            rd.done(tt(R[:, 15, :], R[:, 8, :], R[:, 10, :], ALU.subtract))
            rd.wait()
            rd.done(tt(R[:, 16, :], R[:, 15, :], R[:, 7, :], ALU.mult))
            rd.wait()
            rd.done(vr(RV[:, 7], R[:, 16, :], X, ALU.add))
            assert rd.n == RD_DIFF, rd.n
            vec.wait_ge(s["router_act"], 3)
            rd.done(vec.tensor_scalar(RV[:, 9], RV[:, 8], 1.0, None, ALU.add))
            rd.wait()
            rd.done(vec.reciprocal(vals[:, 0:1], RV[:, 9]))
            rd.wait()
            rd.done(tt(vals[:, 1:2], RV[:, 8], vals[:, 0:1], ALU.mult))
            rd.done(vec.tensor_scalar(vals[:, 2:4], Rq[:, :, 0], -1.0, float(E), ALU.mult, ALU.add))
            rd.wait()
            rd.done(vec.tensor_scalar(R[:, 11, :], R[:, 8, :], vals[:, 0:1], None, ALU.mult))
            rd.wait()
            rd.done(vec.scalar_tensor_tensor(R[:, 12, :], R[:, 10, :], vals[:, 1:2], R[:, 11, :], ALU.mult, ALU.add))
            rd.done(tt(D2[:, :, :], vals[:, :].unsqueeze(1).broadcast_to([E, B, 4]),
                       ident[0:E, 0:B].unsqueeze(2).broadcast_to([E, B, 4]), ALU.mult))
            assert rd.n == RD_WD, rd.n
            vec.wait_ge(s["router_pe"], 4)
            rd.done(vec.tensor_copy(wdT[:, :], ps[0:E, QT_BANK, 0:E]))
            assert rd.n == RD_WDT, rd.n
            rd.done(vec.tensor_copy(WI[:, :, :].rearrange("p b k -> p (b k)"), ps[:, UT_BANK, 0:4 * B]))
            rd.wait()
            rd.done(vec.tensor_copy(IDX[:, :].rearrange("p (b k) -> p b k", k=2), WI[0:1, :, 2:4]))
            assert rd.n == RD_IDX, rd.n
            vec.wait_ge(s["router_pe"], 5)
            rd.done(vec.tensor_copy(b2row[:, :], ps[0:E, QT_BANK, 0:C]))
            rd.wait()
            rd.done(tt(D1[:, :, :], b2row[:, :].unsqueeze(1).broadcast_to([E, B, C]),
                       ident[0:E, 0:B].unsqueeze(2).broadcast_to([E, B, C]), ALU.mult))
            assert rd.n == RD_D1, rd.n

            def bcast(col):
                return col.unsqueeze(2).broadcast_to([P, TILES, C])

            def a_sum(b, par):
                vec.wait_ge(s["a_z_ps"], b + 1)
                vec.wait_ge(s["u_biased"], b + 1)
                tt(ZA[:, :, :], ps[:, A_BANK, :].rearrange("p (t c) -> p t c", c=C), image(U, b), ALU.add)\
                    .then_inc(s["a_z"], 1)

            def a_sum_squares(k):
                def part(b, par):
                    vec.wait_ge(s["a_sq"], 2 * b + k + 1)
                    vr(ssA[:, :], SQA[:, :, :], X, ALU.add).then_inc(s["a_ss"], 1)
                    variance(ssA[:, :], varA[:, :], (LN_T_EPS, LN_C_EPS)[k], 2 * b + k + 1, "a_ss", "a_var")
                return part

            def a_zn(b, par):
                vec.wait_ge(s["a_rstd"], 2 * b + 1)
                tt(ZN[:, :, :], ZA[:, :, :], bcast(rstdA[:, :]), ALU.mult).then_inc(s["a_zn"], 1)

            def a_residual(b, par):
                vec.wait_ge(s["a_zg"], b + 1)
                vec.wait_ge(s["t_beta"], b + 1)
                tt(TA[:, :, :], image(T, b), ZG[:, :, :], ALU.add).then_inc(s["a_t"], 1)

            def a_centre(b, par):
                vec.wait_ge(s["a_t"], b + 1)
                vr(sumA[:, :], TA[:, :, :], X, ALU.add).then_inc(s["a_sum"], 1)
                vec.wait_ge(s["a_sum"], b + 1)
                vec.scalar_tensor_tensor(XA[:, :, :], bcast(sumA[:, :]), -1.0 / C, TA[:, :, :], ALU.mult, ALU.add)\
                    .then_inc(s["a_xc"], 1)

            def a_normalise(b, par):
                vec.wait_ge(s["a_rstd"], 2 * b + 2)
                tt(V[:, :, :], XA[:, :, :], bcast(rstdA[:, :]), ALU.mult).then_inc(s["a_v"], 1)
                vec.wait_ge(s["a_v"], b + 1)
                ge(vec, s["a_vT"], 2 * b)
                vec.tensor_copy(VS[:, :, 0, :], V[:, :, :]).then_inc(s["a_vhi"], 1)

            def b_residual(b, par):
                vec.wait_ge(s["b_cvT"], b + 1)
                for h in range(2):
                    ins = tt(TF[:, par, 4 * h:4 * h + 4], TA[:, 4 * h:4 * h + 4, :],
                             ps[:, B_BANK[0], :].rearrange("p (j h c) -> p h j c", h=2, c=C)[:, h], ALU.add)
                ins.then_inc(s["b_t"], 1)

            def b_centre(b, par):
                vec.wait_ge(s["b_t"], b + 1)
                vr(sumB[:, :], TF[:, par], X, ALU.add).then_inc(s["b_sum"], 1)
                vec.wait_ge(s["b_sum"], b + 1)
                vec.scalar_tensor_tensor(XB[:, :, :], bcast(sumB[:, :]), -1.0 / C, TF[:, par], ALU.mult, ALU.add)\
                    .then_inc(s["b_xc"], 1)

            def b_sum_squares(b, par):
                vec.wait_ge(s["b_sq"], b + 1)
                vr(ssB[:, :], SQB[:, :, :], X, ALU.add).then_inc(s["b_ss"], 1)
                variance(ssB[:, :], varB[:, :], LN_T_EPS, b + 1, "b_ss", "b_var")

            def b_normalise(b, par):
                vec.wait_ge(s["b_rstd"], b + 1)
                tt(EN[:, :, :], XB[:, :, :], bcast(rstdB[:, :]), ALU.mult).then_inc(s["b_en"], 1)
                vec.wait_ge(s["b_en"], b + 1)
                ge(vec, s["b_eT"], 2 * b)
                vec.tensor_copy(ES[:, :, 0, :], EN[:, :, :]).then_inc(s["b_ehi"], 1)

            def b_logits(b, par):
                vec.wait_ge(s["b_gate"], b + 1)
                steps = steps_of(vec, s["b_lg"], 3 * b)
                steps.done(tt(G[:, 0], ps[:, B_BANK[0], 0:TILES * E].rearrange("p (t e) -> p t e", e=E), GBB[:, :, :],
                              ALU.add))
                steps.wait()
                steps.done(vr(gv[:, 0, :], G[:, 0], X, ALU.max))
                steps.wait()
                steps.done(tt(G[:, 1], G[:, 0], gv[:, 0, :].unsqueeze(2).broadcast_to([P, TILES, E]), ALU.subtract))

            def b_probs(b, par):
                vec.wait_ge(s["b_exp"], b + 1)
                steps = steps_of(vec, s["b_top"], 16 * b)
                steps.done(vr(gv[:, 1, :], G[:, 1], X, ALU.add))
                steps.wait()
                steps.done(vec.reciprocal(gv[:, 2, :], gv[:, 1, :]))
                steps.wait()
                steps.done(tt(G[:, 2], G[:, 1], gv[:, 2, :].unsqueeze(2).broadcast_to([P, TILES, E]), ALU.mult))

            def b_first(b, par):
                steps = steps_of(vec, s["b_top"], 16 * b + 3)
                largest(vec, steps, P, TILES, G[:, 2], rev, gv[:, 3, :], G[:, 3], G[:, 4], gq[:, 0, :], G[:, 5])
                without(vec, steps, G[:, 6], G[:, 5], G[:, 2])

            def b_second(b, par):
                steps = steps_of(vec, s["b_top"], 16 * b + 9)
                largest(vec, steps, P, TILES, G[:, 6], rev, gv[:, 3, :], G[:, 3], G[:, 4], gq[:, 1, :], G[:, 7])

            def b_weights(b, par):
                steps = steps_of(vec, s["b_top"], 16 * b + 14)
                steps.wait()
                steps.done(tt(G[:, 8], G[:, 5], G[:, 7], ALU.add))
                steps.wait()
                steps.done(tt(G[:, 9], G[:, 8], G[:, 2], ALU.mult))
                steps.wait()
                cw = G[:, 9].unsqueeze(2).broadcast_to([P, TILES, 2, E])
                ge(vec, s["b_cwT"], 2 * b)
                vec.tensor_copy(CWS[:, :, 0::2, :], cw).then_inc(s["b_cw"], 1)
                vec.wait_ge(s["b_cw"], 2 * b + 1)
                tt(CWS[:, :, 1::2, :], cw, f32(CWS[:, :, 0::2, :]), ALU.subtract).then_inc(s["b_cw"], 1)

            def f_gated(m):
                def part(b, par):
                    vec.wait_ge(s["f_gelu"], 16 * b + m + 1)
                    vec.wait_ge(s["f_cw"], 16 * b + m + 1)
                    ge(vec, s["f_w2"], 8 * b + m // 2 - 1)
                    tt(HG[:, m % 4, :], HB[:, m % 2, :], ps[:, CW_BANK[m % 2], :], ALU.mult).then_inc(s["f_hg"], 1)
                return part

            def f_result(c):
                def part(b, par):
                    vec.wait_ge(s["f_odd"], 2 * b + c + 1)
                    ge(vec, s[f"f_stored{c}"], 16 * b)
                    tt(OUT[:, c, :], OO[:, :], ps[0:C, ACC_BANK, :], ALU.add).then_inc(s["f_out"], 1)
                return part

            periods(vec, PLAN["vec"], dict(
                [(f"f_gated{m}", f_gated(m)) for m in range(SLOTS)]
                    + [("f_result0", f_result(0)), ("f_result1", f_result(1)), ("b_residual", b_residual), ("b_centre", b_centre),
                       ("b_ss", b_sum_squares), ("b_normalise", b_normalise), ("b_logits", b_logits),
                       ("b_probs", b_probs), ("b_first", b_first), ("b_second", b_second),
                       ("b_weights", b_weights), ("a_sum", a_sum), ("a_ss0", a_sum_squares(0)), ("a_zn", a_zn),
                       ("a_residual", a_residual), ("a_centre", a_centre), ("a_ss1", a_sum_squares(1)), ("a_normalise", a_normalise)]))

        @block.scalar
        def _(act):
            av = act.activation

            def square1(p):
                act.wait_ge(s["centred"], p + 1)
                av(SQ1[:, :, :].rearrange("p t c -> p (t c)"), SA, ACT.Square).then_inc(s["sq1"], 1)

            def channels1(p):
                act.wait_ge(s["xnT"], p + 1)
                if p >= 2:
                    act.wait_ge(s["q_ps"], 4 * (p - 1))
                av(XN[:, p % 2, :], SA, ACT.Copy).then_inc(s["xn"], 1)

            def keys_values(p):
                act.wait_ge(s["kv_ps"], p + 1)
                if p >= 1:
                    act.wait_ge(s["kvT_ps"], p)
                av(KV[:, :], SA[0:C, :], ACT.Identity, bias=BKV[:, 0:1]).then_inc(s["kv"], 1)

            def key_exp(p):
                act.wait_ge(s["kmax"], p + 1)
                av(KV[0:32, :], KV[0:32, :], ACT.Exp, bias=nkmax[:, 0:1], accum_out=ksum[:, 0:1])\
                    .then_inc(s["kexp"], 1)

            def tokens_kv(p):
                act.wait_ge(s["kvT_ps"], p + 1)
                av(KVT[:, :, :].rearrange("p t c -> p (t c)"), SA[:, 0:TILES * C], ACT.Copy).then_inc(s["kvT"], 1)

            def outputs(p):
                act.wait_ge(s["m_ps"], p + 1)
                if p >= 2:
                    act.wait_ge(s["att"], 4 * (p - 1))
                av(M[:, p % 2].rearrange("p i n -> p (i n)"), ps[:, 1, 0:2 * P], ACT.Copy).then_inc(s["m"], 1)

            def query_exp(n):
                act.wait_ge(s["qsub"], n + 1)
                av(QS[:, n % 2, :], QS[:, n % 2, :], ACT.Exp).then_inc(s["qexp"], 1)

            def query_channels(n):
                act.wait_ge(s["qT_ps"], n + 1)
                if n >= 2:
                    act.wait_ge(s["att"], n - 1)
                av(QT[:, n % 2].rearrange("p r n -> p (r n)"), ps[:, QT_BANK, :], ACT.Copy).then_inc(s["qT"], 1)

            def residual(n):
                p, g, k = n // 4, n % 4, n % 2
                a = ps[:, AT_BANK[k], :].rearrange("p (j b x c) -> p j b x c", j=UT_, b=2, x=2)
                act.wait_ge(s["att"], n + 1)
                for i in range(2):
                    ins = av(T[:, 2 * p + i, UT_ * g:UT_ * g + UT_, :], a[:, :, i, 0, :], ACT.Copy)
                ins.then_inc(s["t_res"], 1)
                if n >= 2:
                    act.wait_ge(s["ss2"], n - 1)
                av(SQ2[:, k], ps[:, AT_BANK[k], :].rearrange("p (r x c) -> p r x c", x=2, c=C)[:, :, 1, :], ACT.Square)\
                    .then_inc(s["sq2"], 1)

            def u_channels(n):
                p, g = n // 4, n % 4
                act.wait_ge(s["uT_ps"], n + 1)
                src = ps[:, UT_BANK, :].rearrange("p (j b n) -> p j b n", j=UT_, b=2)
                for i in range(2):
                    ins = av(UTR[:, 2 * p + i, UT_ * g * P:UT_ * (g + 1) * P].rearrange("p (j n) -> p j n", n=P),
                             src[:, :, i, :], ACT.Copy, accum_out=usum[:, 2 * p + i, g:g + 1])
                ins.then_inc(s["uT"], 1)

            act.wait_ge(s["set_woc"], 1)
            av(WOC[:, :], ps[:, 6, 0:P], ACT.Copy).then_inc(s["set_wocev"], 1)
            for i in range(-S1_LEAD, UNITS + 4):
                if (i - 1) % 4 == 0 and 0 <= (i - 1) // 4 < PAIRS:
                    outputs((i - 1) // 4)
                if i % 4 == 0 and 0 <= i // 4 < PAIRS:
                    tokens_kv(i // 4)
                if (i + 3) % 4 == 0 and 0 <= (i + 3) // 4 < PAIRS:
                    square1((i + 3) // 4)
                if 0 <= i < UNITS:
                    query_exp(i)
                if 1 <= i <= UNITS:
                    query_channels(i - 1)
                    residual(i - 1)
                if (i + 2) % 4 == 0 and 0 <= (i + 2) // 4 < PAIRS:
                    channels1((i + 2) // 4)
                if (i + 1) % 4 == 0 and 0 <= (i + 1) // 4 < PAIRS:
                    keys_values((i + 1) // 4)
                    key_exp((i + 1) // 4)
                if 3 <= i <= UNITS + 2:
                    u_channels(i - 3)

            act.wait_ge(s["set_w2"], 2)
            av(W2A[:, :, :].rearrange("p e c -> p (e c)"), ps[:, Q_BANK[0], :], ACT.Copy).then_inc(s["set_w2ev"], 1)
            av(B2A[:, :], ps[0:E, Q_BANK[1], 0:C], ACT.Copy).then_inc(s["set_b2ev"], 1)
            act.wait_ge(s["router_dve"], RD_MAX1)
            av(R[:, 1, :], R[:, 0, :], ACT.Exp, bias=RV[:, 0], accum_out=RV[:, 1]).then_inc(s["router_act"], 1)
            act.wait_ge(s["router_dve"], RD_MAX2)
            av(R[:, 7, :], R[:, 6, :], ACT.Exp, bias=RV[:, 3], accum_out=RV[:, 4]).then_inc(s["router_act"], 1)
            act.wait_ge(s["router_dve"], RD_DIFF)
            av(RV[:, 8], RV[:, 7], ACT.Exp, scale=-1.0).then_inc(s["router_act"], 1)
            act.wait_ge(s["router_pe"], 6)
            av(B2A_b[:, :, :].rearrange("p b c -> p (b c)"), ps[:, QT_BANK, :], ACT.Copy).then_inc(s["router_act"], 1)

            def a_select(b, par):
                ge(act, s["a_z_ps"], b)
                for k in range(2):
                    e = act.value_load(IDX[0:1, bass.ds(2 * b + k, 1)], min_val=0, max_val=E - 1)
                    av(W1S[:, k], f32(W1A[:, bass.ds(e, 1), :, :]).rearrange("p a k f -> p (a k) f"), ACT.Copy)
                    av(B1S[:, k:k + 1], B1A[:, bass.ds(e, 1)], ACT.Copy)
                    av(W2S[:, k, :], W2A[:, bass.ds(e, 1), :].rearrange("p a c -> p (a c)"), ACT.Copy,
                       scale=WI[:, bass.ds(b, 1), k:k + 1].rearrange("p a k -> p (a k)")).then_inc(s["a_sel"], 1)

            def a_gelu(n):
                def part(b, par):
                    k, c = n // 2, n % 2
                    if n == 0:
                        act.wait_ge(s["a_sel"], 2 * (b + 1))
                    act.wait_ge(s["a_h"], 4 * b + n + 1)
                    av(HA[:, k, c * HALF:(c + 1) * HALF], ps[:, A_BANK, :], ACT.Gelu, bias=B1S[:, k:k + 1])\
                        .then_inc(s["a_gelu"], 1)
                return part

            def a_square(k):
                def part(b, par):
                    act.wait_ge(s[("a_z", "a_xc")[k]], b + 1)
                    av(SQA[:, :, :], (ZA, XA)[k][:, :, :], ACT.Square).then_inc(s["a_sq"], 1)
                return part

            def a_image(h):
                def part(b, par):
                    act.wait_ge(s["a_vT"], 2 * b + h + 1)
                    if h == 0:
                        ge(act, s["b_conv"], 2 * b - 2)
                    av(VP[:, par, 16 * h + 1:16 * h + 17, 1:W + 1],
                       ps[:, A_BANK, :].rearrange("p (y x) -> p y x", x=W), ACT.Copy).then_inc(s["a_img"], 1)
                return part

            def b_scale(c):
                def part(b, par):
                    act.wait_ge(s["b_conv"], 2 * b + c + 1)
                    av(CV[c * C:(c + 1) * C, :], ps[0:C, B_BANK[c], :], ACT.Copy, scale=CSCALE[:, 0:1])\
                        .then_inc(s["b_cv"], 1)
                return part

            def b_square(b, par):
                act.wait_ge(s["b_xc"], b + 1)
                av(SQB[:, :, :], XB[:, :, :], ACT.Square).then_inc(s["b_sq"], 1)

            def b_channels(h):
                def part(b, par):
                    act.wait_ge(s["b_eT"], 2 * b + h + 1)
                    av(ET[:, par, h * HALF:(h + 1) * HALF], ps[:, B_BANK[h], :], ACT.Copy).then_inc(s["b_et"], 1)
                return part

            def b_exp(b, par):
                act.wait_ge(s["b_lg"], 3 * b + 3)
                av(G[:, 1], G[:, 1], ACT.Exp).then_inc(s["b_exp"], 1)

            def b_gates_out(h):
                def part(b, par):
                    act.wait_ge(s["b_cwT"], 2 * b + h + 1)
                    av(CWT[:, par, h * HALF:(h + 1) * HALF], ps[0:32, B_BANK[h], :], ACT.Copy)\
                        .then_inc(s["b_cwt"], 1)
                return part

            def f_gelu(m):
                def part(b, par):
                    act.wait_ge(s["f_h"], 16 * b + m + 1)
                    ge(act, s["f_hg"], 16 * b + m - 1)
                    av(HB[:, m % 2, :], ps[:, H_BANK[m % 2], :], ACT.Gelu, bias=B1B[:, m % E:m % E + 1])\
                        .then_inc(s["f_gelu"], 1)
                return part

            def f_odd(c):
                def part(b, par):
                    act.wait_ge(s["f_w2"], 8 * b + 4 * c + 4)
                    ge(act, s["f_out"], 2 * b + c)
                    av(OO[:, :], ps[C:P, ACC_BANK, :], ACT.Copy).then_inc(s["f_odd"], 1)
                return part

            act.wait_ge(s["router_dve"], RD_IDX)
            periods(act, PLAN["act"], dict(
                [(f"f_gelu{m}", f_gelu(m)) for m in range(SLOTS)]
                    + [("f_odd0", f_odd(0)), ("f_odd1", f_odd(1))]
                    + [("a_select", a_select)]
                    + [(f"a_hidden{n}", a_gelu(n)) for n in range(4)]
                    + [("a_square0", a_square(0)), ("a_square1", a_square(1)), ("a_image0", a_image(0)),
                       ("a_image1", a_image(1)), ("b_scale0", b_scale(0)), ("b_scale1", b_scale(1)),
                       ("b_square", b_square), ("b_channels0", b_channels(0)),
                       ("b_channels1", b_channels(1)), ("b_exp", b_exp),
                       ("b_gates_out0", b_gates_out(0)), ("b_gates_out1", b_gates_out(1))]))


S1_LEAD = 3
RD_U8, RD_MAX1, RD_P1 = 1, 3, 5
RD_MAX2 = 13
RD_DIFF = 15 + 11 + 3
RD_WD = RD_DIFF + 7
RD_WDT = RD_WD + 1
RD_IDX = RD_WDT + 2
RD_D1 = RD_IDX + 2
ROUTER_ACT = 4


def constants():
    k = np.zeros((P, K_N), np.float32)
    eye = np.eye(C, dtype=np.float32)
    c = eye - np.float32(1.0 / C)
    k[:, K_ID:K_ID + P] = np.eye(P)
    for i in range(2):
        rows = slice(i * C, (i + 1) * C)
        k[rows, K_CEN + i * C:K_CEN + (i + 1) * C] = c
        k[rows, K_IC + i * P:K_IC + i * P + C] = eye
        k[rows, K_IC + i * P + C:K_IC + (i + 1) * P] = c
        k[i * KD:(i + 1) * KD, K_PAIR + i] = 1.0
        k[i * KD:(i + 1) * KD, K_HL + i] = 1.0
    for h in range(HEADS):
        k[h * KD:(h + 1) * KD, K_HEAD + h] = 1.0
    k[:, K_REV:K_REV + E] = np.arange(E, 0, -1)
    sel = np.zeros((32, E, P), np.float32)
    for e in range(E):
        sel[e, e] = sel[E + e, e] = 1.0
    return k, sel


def kernel(**inputs):
    import concourse.bacc as bacc
    from concourse.bass_utils import run_bass_kernel_spmd

    a = {k: np.ascontiguousarray(v) for k, v in inputs.items()}
    k, sel = constants()
    wq, wk, wv = a["L0_conv_Wq"].T, a["L0_conv_Wk"].T, a["L0_conv_Wv"].T
    wqb = np.zeros((P, 256), np.float32)
    wkv = np.zeros((P, C), np.float32)
    bkv = np.zeros((C, 1), np.float32)
    for i in range(2):
        rows = slice(i * C, (i + 1) * C)
        wqb[rows, i * P:(i + 1) * P] = wq
        wkv[rows, i * KD:(i + 1) * KD] = wk
        wkv[rows, 32 + i * KD:32 + (i + 1) * KD] = wv
        bkv[i * KD:(i + 1) * KD, 0] = a["L0_conv_bk"]
        bkv[32 + i * KD:32 + (i + 1) * KD, 0] = a["L0_conv_bv"]
    bq2 = np.zeros((C, P), np.float32)
    bq2[0::32] = a["L0_conv_bq"]
    bout2 = np.zeros((C, C), np.float32)
    bout2[:, 0::32] = a["L0_conv_bout"][:, None]

    def twice(w):
        return np.concatenate([w, w])

    w = a["L1_conv_weight"]
    arrays = dict(
        x=a["x"].reshape(B, C, S), consts=k, wqb=wqb, bq2=bq2, wkv=wkv, bkv=bkv, wout=a["L0_conv_Wout"],
        bout2=bout2, wr=twice(a["L0_ffn_Wr"]), br=np.tile(a["L0_ffn_br"], (B, 1)),
        w1a=twice(a["L0_ffn_W1"].transpose(1, 0, 2)), b1a=a["L0_ffn_b1"].T,
        w2ta=a["L0_ffn_W2"].transpose(2, 0, 1), b2ta=a["L0_ffn_b2"].T,
        gammab=np.tile(a["L0_ffn_gamma"], (P, 1)), betab=np.tile(a["L0_ffn_beta"], (P, 1)),
        wconv=twice(w.transpose(1, 2, 3, 0).reshape(C, TAPS, C)), wcs=w.reshape(C, C * TAPS),
        gw=twice(a["L1_ffn_gate_w"]), gbb=np.tile(a["L1_ffn_gate_b"], (P, TILES, 1)),
        w1b=twice(a["L1_ffn_W1"].transpose(1, 0, 2)), b1b=a["L1_ffn_b1"].T,
        w2b=a["L1_ffn_W2"].transpose(1, 0, 2), b2b=np.tile(a["L1_ffn_b2"], (4, 1)), selb=sel,
    )
    nc = bacc.Bacc("TRN2", target_bir_lowering=False, num_devices=1)
    arrays = {f"in_{n}": np.ascontiguousarray(v) for n, v in arrays.items()}
    args = [nc.dram_tensor(n, v.shape, mybir.dt.from_np(v.dtype), kind="ExternalInput").ap()
            for n, v in arrays.items()]
    out = nc.dram_tensor("out", (B, C, S), F32, kind="ExternalOutput").ap()
    build(nc, *args, out)
    r = run_bass_kernel_spmd(nc, [arrays], core_ids=[0])
    return r.results[0]["out"].reshape(B, C, H, W)
```

```python
from contextlib import ExitStack

import numpy as np

import concourse.bass as bass
from concourse import mybir

F32 = mybir.dt.float32
F32R = mybir.dt.float32r
I32 = mybir.dt.int32
ALU = mybir.AluOpType
ACT = mybir.ActivationFunctionType
X = mybir.AxisListType.X

B, C, H, W = 8, 64, 32, 32
S = H * W
P = 128
TILES = S // P
PAIRS = B // 2
HEADS, KD = 8, 16
E, F = 8, 128
UNITS = 4 * PAIRS
UT_ = 2
HALF = S // 2
TAPS = 9
CAPACITY = float(-(-B * S * 5 // (4 * E)))
LN_C_EPS, LN_T_EPS = 1e-6, 1e-5

K_ID, K_CEN, K_IC, K_HEAD, K_REV, K_PAIR, K_HL = 0, 128, 256, 512, 520, 528, 530
K_N = 532


def steps_of(eng, sem, base=0):
    return Steps(eng, sem, base)


class Steps:
    def __init__(self, eng, sem, base):
        self.eng, self.sem, self.base, self.n = eng, sem, base, 0

    def done(self, instruction):
        instruction.then_inc(self.sem, 1)
        self.n += 1

    def wait(self):
        self.eng.wait_ge(self.sem, self.base + self.n)


def ge(eng, sem, value):
    if not isinstance(value, int) or value > 0:
        eng.wait_ge(sem, value)


SLOTS = 16
PLAN = dict(
    pool=(
        "a_rstd1+1 a_rstd0+2 b_rstd+1"
    ).split(),
    pe=(
        "f_hidden4-1 f_gate3-1 f_hidden5-1 f_output0-1 f_gate4-1 f_output1-1 a_hidden0+2 f_hidden6-1 "
        "b_to_channels0 f_gate5-1 f_gate6-1 a_hidden1+2 b_to_channels1 f_hidden7-1 f_hidden8-1 a_hidden2+2 "
        "b_gates f_gate7-1 a_hidden3+2 f_output2-1 f_gate8-1 f_hidden9-1 f_hidden10-1 f_gate9-1 f_output3-1 "
        "a_output+2 a_vT0+1 f_gate10-1 f_hidden11-1 f_hidden12-1 a_vT1+1 a_z_turned+2 f_gate11-1 f_output4-1 "
        "f_hidden13-1 f_gate12-1 f_hidden14-1 b_gates_turned0 f_gate13-1 f_output5-1 b_gates_turned1 f_hidden15-1 "
        "f_gate14-1 f_gate15-1 b_conv0+1 b_conv1+1 f_output6-1 b_to_tokens+1 f_hidden0 f_hidden1 f_output7-1 "
        "f_gate0 f_hidden2 f_gate1 f_hidden3 f_start f_gate2"
    ).split(),
    vec=(
        "a_normalise+1 b_probs f_gated9-1 b_first f_gated10-1 b_second b_weights f_gated11-1 a_sum+2 f_gated12-1 "
        "f_gated13-1 a_ss0+2 f_gated14-1 f_gated15-1 a_zn+2 b_residual+1 b_centre+1 f_gated0 f_gated1 b_ss+1 "
        "a_residual+2 f_gated2 f_gated3 b_normalise+1 f_gated4 a_centre+2 f_gated5 f_gated6 a_ss1+2 b_logits+1 "
        "f_gated7 f_gated8"
    ).split(),
    act=(
        "a_select+2 f_gelu4-1 f_gelu5-1 a_hidden0+2 b_channels0 f_gelu6-1 a_hidden1+2 b_channels1 a_square1+1 "
        "a_hidden2+2 f_gelu7-1 f_gelu8-1 a_hidden3+2 b_exp f_gelu9-1 f_gelu10-1 a_z_copy+2 a_image0+1 a_image1+1 "
        "f_gelu11-1 f_gelu12-1 b_gates_out0 f_gelu13-1 a_square0+2 b_gates_out1 f_gelu14-1 f_gelu15-1 b_scale+1 "
        "f_gelu0 f_gelu1 f_result-1 b_square+1 f_gelu2 f_gelu3"
    ).split(),
)
ATTENTION_PLAN = dict(
    pool=(
        "qnorm0 rstd2_2-1 qnorm1 ulo2-1 rstd2_3-1 rstd1_0+1 ulo3-1 rstd1_1+1 rstd2_0 qnorm2 ulo0 rstd2_1 qnorm3 "
        "ulo1"
    ).split(),
    pe=(
        "set_outputs+1 residual0 attend0 q_to_channels1 residual1 u_to_channels2-1 xn_to_channels0+1 attend1 "
        "queries0+1 xn_to_channels1+1 u_to_channels3-1 keys_values0+1 q_to_channels2 keys_values1+1 residual2 "
        "attend2 queries1+1 u_to_channels0 q_to_channels3 residual3 kv_to_tokens+1 queries2+1 context+1 "
        "queries3+1 context_turned+1 attend3 centre0+2 context_out+1 u_to_channels1 q_to_channels0+1 centre1+2"
    ).split(),
    vec=(
        "sum_squares2_0 normalise1_1+1 query_max3 order_rows0+2 normalise2_0 set_bo+1 order_rows1+2 query_max0+1 "
        "sum_squares2_1 query_sum3 key_max+1 normalise2_1 query_max1+1 query_sum0+1 key_norm+1 sum_squares2_2 "
        "query_sum1+1 pick_context+1 normalise2_2 block_diagonal+1 set_layer0+1 set_layer1-1 set_conv "
        "sum_squares2_3 sum_squares1_0+2 query_max2+1 normalise2_3 sum_squares1_1+2 normalise1_0+2 set_bq+2 "
        "query_sum2+1"
    ).split(),
    act=(
        "channels1_1+1 query_channels2 keys_values0+1 keys_values1+1 u_channels3-1 residual2 query_exp0+1 "
        "key_exp+1 query_channels3 query_exp1+1 tokens_kv+1 set_outputs+1 square1_0+2 u_channels0 residual3 "
        "outputs+1 u_channels1 query_channels0+1 square1_1+2 query_exp2+1 residual0+1 query_channels1+1 "
        "channels1_0+2 u_channels2 residual1+1 query_exp3+1"
    ).split(),
)
MOST_AHEAD = 2


def parts_of(plan):
    for token in plan:
        name = token.rstrip("0123456789").rstrip("+-") if "+" in token or "-" in token else token
        yield name, int(token[len(name):] or 0)


def period(b, par, plan, parts, live):
    for name, ahead in parts_of(plan):
        if live(name, b, ahead):
            parts[name](b + ahead, (par + ahead) % 2)


def periods(eng, plan, parts):
    def image_exists(name, b, ahead):
        return 0 <= b + ahead < B

    assert sorted(parts) == sorted(name for name, _ in parts_of(plan))
    for b in range(-MOST_AHEAD, MOST_AHEAD):
        period(b, b % 2, plan, parts, image_exists)
    with eng.Fori(0, (B - 2 * MOST_AHEAD) // 2) as i:
        for par in range(2):
            period(eng.snap(2 * i + (MOST_AHEAD + par)), par, plan, parts, lambda name, b, ahead: True)
    for b in range(B - MOST_AHEAD, B + MOST_AHEAD):
        period(b, b % 2, plan, parts, image_exists)


def pair_periods(name, parts):
    parts, plan = dict(parts), ATTENTION_PLAN[name]
    assert sorted(parts) == sorted(name for name, _ in parts_of(plan))
    for p in range(-MOST_AHEAD, PAIRS + MOST_AHEAD):
        period(p, p % 2, plan, parts,
               lambda name, p, ahead: p + ahead == 0 or 0 < p + ahead < PAIRS and not name.startswith("set_"))


def largest(vec, steps, p, n, vals, rev, m, eq, rank, q, onehot):
    wide = [p, n, E]
    steps.wait()
    steps.done(vec.tensor_reduce(m, vals, X, ALU.max))
    steps.wait()
    if n == 1:
        steps.done(vec.scalar_tensor_tensor(rank, vals, m, rev.unsqueeze(1), ALU.is_equal, ALU.mult))
    else:
        steps.done(vec.tensor_tensor(eq, vals, m.unsqueeze(2).broadcast_to(wide), ALU.is_equal))
        steps.wait()
        steps.done(vec.tensor_tensor(rank, eq, rev.unsqueeze(1).broadcast_to(wide), ALU.mult))
    steps.wait()
    steps.done(vec.tensor_reduce(q, rank, X, ALU.max))
    steps.wait()
    steps.done(vec.tensor_tensor(onehot, rank, q.unsqueeze(2).broadcast_to(wide), ALU.is_equal))


def without(vec, steps, rest, first, probs):
    steps.wait()
    steps.done(vec.scalar_tensor_tensor(rest, first, -2.0, probs, ALU.mult, ALU.add))


def build(nc, x, consts, wqb, bq2, wkv, bkv, wout, bout2, wr, br, w1a, b1a, w2ta, b2ta, gammab, betab,
          wconv, wcs, gw, gbb, w1b, b1b, w2b, b2b, selb, out):
    ctx = ExitStack()
    with ctx:
        def sb(name, shape, dt=F32):
            return ctx.enter_context(nc.sbuf_tensor(name, shape, dt))

        def tiles(ap):
            return ap.rearrange("p (t c) -> p t c", c=C)

        def sem(name):
            return ctx.enter_context(nc.semaphore(name))

        K = sb("K", [P, K_N])
        ident = K[:, K_ID:K_ID + P]
        cen = K[:, K_CEN:K_CEN + P]
        ic = K[:, K_IC:K_IC + 256]
        headmask = K[:, K_HEAD:K_HEAD + HEADS]
        rev = K[:, K_REV:K_REV + E]
        pairmask = K[0:32, K_PAIR:K_PAIR + 2]
        hlmask = K[0:32, K_HL:K_HL + 2]
        ident_r = sb("ident_r", [P, P], F32R)
        ones_r = sb("ones_r", [C, P], F32R)
        ones = sb("ones", [E, P])
        WQB = sb("WQB", [P, 256])
        BQ2 = sb("BQ2", [C, P])
        CWTB = sb("CWTB", [C, 2 * S], F32R)
        BQR = CWTB[:, 0:512]
        WKV = sb("WKV", [P, C])
        BKV = sb("BKV", [C, 1])
        WOUT = sb("WOUT", [C, P])
        BOUT2 = sb("BOUT2", [C, C])
        WOC = sb("WOC", [P, P])
        BOR = CWTB[:, 512:1024]
        WR = sb("WR", [P, E])
        BR = sb("BR", [E, E])
        W1stage = sb("W1stage", [P, E, F])
        W1A = sb("W1A", [P, E, 2, F], F32R)
        B1A = sb("B1A", [F, E])
        HB = sb("HB", [F, 2, HALF])
        W2TA = HB[0:C, :, :].rearrange("p a (e f) -> p (a e) f", f=F)
        W2A = sb("W2A", [F, E, C])
        B2TA = sb("B2TA", [C, E])
        B2A = sb("B2A", [E, C])
        GAMMA = sb("GAMMA", [P, C])
        BETA = sb("BETA", [P, C])
        WCstage = W1stage[:, 0:5, :].rearrange("p a n -> p (a n)")[:, 0:TAPS * C].rearrange("p (t c) -> p t c", c=C)
        WC = sb("WC", [P, 3, 5, C], F32R)
        WCS = W1stage[:, 0:5, :].rearrange("p a n -> p (a n)")[:, 0:C * TAPS]
        CSCALE = sb("CSCALE", [P, 1])
        GWstage = sb("GWstage", [P, E])
        GW = sb("GW", [P, 2, E], F32R)
        GBB = sb("GBB", [P, TILES, E])
        W1B = sb("W1B", [P, E, 2, F], F32R)
        B1B = sb("B1B", [F, E])
        W2B = sb("W2B", [F, E, C])
        B2stage = sb("B2stage", [32, C])
        B2hi = sb("B2hi", [32, C], F32R)
        B2lo = sb("B2lo", [32, C])
        B2B = sb("B2B", [32, 3 * C], F32R)
        SELstage = W1stage[0:32, :, :]
        SEL = sb("SEL", [32, E, P], F32R)
        XC = sb("XC", [P, PAIRS, S])
        T = sb("T", [P, B, TILES, C])
        U = sb("U", [P, B, TILES, C])
        UTR = sb("UTR", [P, B, S], F32R)
        XR = T[:, :, :, :].rearrange("p (q i) t c -> p q (i t c)", i=2)
        usum = sb("usum", [P, B, 4])
        SQ1 = sb("SQ1", [P, TILES, P])
        ss1 = sb("ss1", [P, 2 * TILES])
        var1 = sb("var1", [P, 2 * TILES])
        rstd1_ = sb("rstd1", [P, 2 * TILES])
        XNT = sb("XNT", [P, TILES, P])
        XN = sb("XN", [P, 2, S])
        KV = sb("KV", [C, S])
        nkmax = sb("nkmax", [32, 1])
        ksum = sb("ksum", [32, 1])
        rksum = sb("rksum", [32, 1])
        r01 = sb("r01", [32, 2])
        KVT = sb("KVT", [P, TILES, C])
        Z = sb("Z", [32, HEADS, KD])
        BD = sb("BD", [P, 2, HEADS, KD])
        M = sb("M", [P, 2, 2, P])
        qmax = sb("qmax", [P, 32])
        QS = sb("QS", [P, 2, 512])
        qsum = sb("qsum", [P, 32])
        rqsum = sb("rqsum", [P, 2, 32])
        QT = sb("QT", [P, 2, 4, P])
        SQ2 = sb("SQ2", [P, 2, 4, C])
        ss2 = sb("ss2", [P, 2, 4])
        var2 = sb("var2", [P, 2, 4])
        rstd2 = sb("rstd2", [P, 2, 4])
        US = sb("US", [P, 2, 4, 2, C], F32R)
        pow_half = sb("pow_half", [P, 2 * TILES])
        u8 = sb("u8", [P, E])
        R = sb("R", [E, 32, E])
        RV = sb("RV", [E, 16, 1])
        Rq = sb("Rq", [E, 2, 1])
        vals = sb("vals", [E, 4])
        D1 = KV[0:E, 0:B * C].rearrange("p (b c) -> p b c", c=C)
        D2 = sb("D2", [E, B, 4])
        wdT = sb("wdT", [E, E])
        b2row = sb("b2row", [E, C])
        WI = sb("WI", [P, B, 4])
        IDX = sb("IDX", [1, B * 2], I32)
        B2A_b = SQ2[:, :, :, :].rearrange("p k r c -> p (k r) c")
        gelu_table = sb("gelu_table", [E, 1])
        W1S = sb("W1S", [P, 2, 2, F], F32R)
        B1S = sb("B1S", [F, 2])
        W2S = sb("W2S", [F, 2, C])
        HA = XC[:, 0:2, :]
        ZA, SQA, ZN, ZG = (tiles(XN[:, k // 2, (k % 2) * HALF:(k % 2 + 1) * HALF]) for k in range(4))
        ssA = sb("ssA", [P, TILES])
        varA = sb("varA", [P, TILES])
        rstdA = sb("rstdA", [P, TILES])
        sumA = sb("sumA", [P, TILES])
        TA = sb("TA", [P, TILES, C])
        XA = XNT[:, :, 0:C]
        V = XNT[:, :, C:P]
        VS = US[:, :, :, :, :].rearrange("p k r a c -> p (k r) a c")
        VP = sb("VP", [P, 2, H + 2, W + 2], F32R)
        CV = sb("CV", [P, HALF])
        TF = QT[:, :, :, :].rearrange("p k r (h c) -> p k r h c", c=C)
        sumB = sb("sumB", [P, TILES])
        XB = SQ1[:, :, 0:C]
        SQB = SQ1[:, :, C:P]
        ssB = sb("ssB", [P, TILES])
        varB = sb("varB", [P, TILES])
        rstdB = sb("rstdB", [P, TILES])
        EN = tiles(QS[:, 0, :])
        ES = sb("ES", [P, TILES, 2, C], F32R)
        ET = sb("ET", [P, 2, S], F32R)
        G = sb("G", [P, 10, TILES, E])
        gv = sb("gv", [P, 4, TILES])
        gq = sb("gq", [P, 2, TILES])
        CWS = sb("CWS", [P, TILES, 4, E], F32R)
        CWT = CWTB[0:32, :].rearrange("p (k n) -> p k n", k=2)
        HG = XC[:, 2:4, :].rearrange("p a (k n) -> p (a k) n", k=2)
        ZC = QS[:, 1, :]
        OUT = W1stage[0:C, :, :].rearrange("p a n -> p (a n)")

        ps = ctx.enter_context(nc.psum_tensor("ps", [P, 8, HALF], F32))

        s = {name: sem(name) for name in (
            "ld_const", "ld_x0", "ld_x", "ld_att", "ld_ffn0", "ld_conv", "ld_ffn1", "ld_w1b", "ld_sel", "memsets", "set_dve", "set_w2",
            "set_woc", "set_bo", "set_wocev", "set_w2ev", "set_b2ev",
            "x", "centred", "sq1", "ss1", "var1", "rstd1", "xn_tok", "xnT", "xn", "kv_ps", "kv", "kmax", "kexp",
            "rk", "kvT_ps", "kvT", "ctx", "z", "ctxT", "bd", "m_ps", "m",
            "q_ps", "qmax", "qsub", "qexp", "qsum", "rqsum", "qnorm", "qT_ps", "qT", "at_open", "att", "t_res", "sq2",
            "ss2", "var2", "rstd2", "u", "uhi", "ulo", "uT_ps", "uT",
            "router_dve", "router_pe", "router_act", "u_biased", "t_beta",
            "a_sel", "a_h", "a_gelu", "a_z_ps", "a_zc", "a_zT", "a_z", "a_sq", "a_ss", "a_var", "a_rstd", "a_zn", "a_zg", "a_t",
            "a_sum", "a_xc", "a_v", "a_vhi", "a_vlo", "a_vT", "a_img",
            "b_conv", "b_cv", "b_cvT", "b_t", "b_sum", "b_xc", "b_sq", "b_ss", "b_var", "b_rstd", "b_en", "b_ehi",
            "b_elo", "b_eT", "b_et", "b_gate", "b_lg", "b_exp", "b_top", "b_cw", "b_cwT", "b_cwt",
            "f_h", "f_gelu", "f_cw", "f_hg", "f_start", "f_w2", "f_out", "f_stored",
        )}
        block = ctx.enter_context(nc.Block())

        SA = ps[:, 0:2, :].rearrange("p a n -> p (a n)")
        Q_BANK, QT_BANK, AT_BANK, UT_BANK = (2, 3), 4, (5, 6), 7
        A_BANK, B_BANK, V_BANK, H_BANK, CW_BANK, ACC_BANK = 0, 1, 2, (3, 4), (5, 6), 7

        def image(tile, b):
            return tile[:, bass.ds(b, 1), :, :].rearrange("p a t c -> p (a t) c")

        def f32(ap):
            return ap.bitcast(F32)

        SET_BQ, SET_BO, SET_W1A, SET_SIGNS, SET_CONV, SET_W1B, SET_F1 = 3, 5, 7, 9, 11, 13, 20
        LD_ATT, LD_FFN0, LD_FFN1 = 6 * 16, 8 * 16, 5 * 16

        @block.sync
        def _(sp):
            xp = x.rearrange("(q i) c n -> q (i c) n", i=2)
            sp.dma_start(K[:, :], consts).then_inc(s["ld_const"], 16)
            sp.dma_start(XR[:, 0, :], xp[0]).then_inc(s["ld_x0"], 16)
            for dst, src in ((WKV[:, :], wkv), (BKV[:, :], bkv), (WQB[:, :], wqb), (BQ2[:, :], bq2),
                             (WOUT[:, :], wout), (BOUT2[:, :], bout2)):
                sp.dma_start(dst, src).then_inc(s["ld_att"], 16)
            sp.dma_start(XR[:, 1:PAIRS, :], xp[1:PAIRS].rearrange("q p n -> p q n")).then_inc(s["ld_x"], 16)
            for dst, src in ((WR[:, :], wr), (BR[:, :], br), (W1stage[:, :, :], w1a), (B1A[:, :], b1a),
                             (W2TA[:, :, :], w2ta), (B2TA[:, :], b2ta), (GAMMA[:, :], gammab), (BETA[:, :], betab)):
                sp.dma_start(dst, src).then_inc(s["ld_ffn0"], 16)
            for dst, src in ((GWstage[:, :], gw), (GBB[:, :, :], gbb), (B1B[:, :], b1b),
                             (W2B[:, :, :], w2b), (B2stage[:, :], b2b)):
                sp.dma_start(dst, src).then_inc(s["ld_ffn1"], 16)
            for dst, src, step, sig in ((WCstage, wconv, SET_W1A, "ld_conv"), (WCS, wcs, SET_SIGNS, "ld_conv"),
                                        (W1stage[:, :, :], w1b, SET_CONV, "ld_w1b"),
                                        (SELstage, selb, SET_W1B, "ld_sel")):
                sp.wait_ge(s["set_dve"], step)
                sp.dma_start(dst, src).then_inc(s[sig], 16)

            with sp.Fori(0, B) as b:
                sp.wait_ge(s["f_out"], b + 1)
                sp.dma_start(out[bass.ds(b, 1), :, :].rearrange("a c n -> c (a n)"), OUT).then_inc(s["f_stored"], 16)
            sp.wait_ge(s["f_stored"], 16 * B)

        @block.gpsimd
        def _(pool):
            for tile, value in ((pow_half[:, :], -0.5), (ones[:, :], 1.0), (f32(ones_r[:, :]), 1.0),
                                (f32(VP[:, :, :, :]), 0.0), (f32(B2B[:, :]), 0.0), (f32(WC[:, :, :, :]), 0.0)):
                pool.memset(tile, value).then_inc(s["memsets"], 1)

            def rstd(var, out_, n, k, var_sem, rstd_sem):
                pool.wait_ge(s[var_sem], k)
                pool.tensor_tensor(out_, var, pow_half[:, 0:n], ALU.pow).then_inc(s[rstd_sem], 1)

            def rstd1(h):
                def part(p, par):
                    cols = slice(h * TILES, (h + 1) * TILES)
                    rstd(var1[:, cols], rstd1_[:, cols], TILES, 2 * p + h + 1, "var1", "rstd1")
                return part

            def qnorm(g):
                def part(p, par):
                    n = 4 * p + g
                    pool.wait_ge(s["rqsum"], n + 1)
                    q = QS[:, n % 2, :].rearrange("p (g d) -> p g d", d=KD)
                    pool.tensor_tensor(q, q, rqsum[:, n % 2, :].unsqueeze(2).broadcast_to([P, 32, KD]), ALU.mult)\
                        .then_inc(s["qnorm"], 1)
                return part

            def rstd2_(g):
                def part(p, par):
                    n = 4 * p + g
                    rstd(var2[:, n % 2, :], rstd2[:, n % 2, :], 4, n + 1, "var2", "rstd2")
                return part

            def ulo(g):
                def part(p, par):
                    n, k = 4 * p + g, g % 2
                    pool.wait_ge(s["uhi"], n + 1)
                    hi = f32(US[:, k, :, 0, :]).rearrange("p (j b) c -> p b j c", b=2)
                    lo = US[:, k, :, 1, :].rearrange("p (j b) c -> p b j c", b=2)
                    for i in range(2):
                        ins = pool.tensor_tensor(lo[:, i], U[:, 2 * p + i, UT_ * g:UT_ * g + UT_, :], hi[:, i],
                                                 ALU.subtract)
                    ins.then_inc(s["ulo"], 1)
                return part

            pool.wait_ge(s["memsets"], 1)
            pair_periods("pool", [(f"rstd1_{h}", rstd1(h)) for h in range(2)]
                         + [(f"{name}{g}", part(g)) for g in range(4)
                            for name, part in (("qnorm", qnorm), ("rstd2_", rstd2_), ("ulo", ulo))])

            pool.wait_ge(s["ld_ffn0"], LD_FFN0)
            pool.wait_ge(s["t_res"], UNITS)
            with pool.Fori(0, B) as b:
                pool.tensor_tensor(image(T, b), image(T, b), BETA[:, :].unsqueeze(1).broadcast_to([P, TILES, C]),
                                   ALU.add).then_inc(s["t_beta"], 1)
            pool.wait_ge(s["router_dve"], RD_B2)
            with pool.Fori(0, B) as b:
                pool.tensor_tensor(image(U, b), image(U, b),
                                   B2A_b[:, bass.ds(b, 1), :].broadcast_to([P, TILES, C]),
                                   ALU.add).then_inc(s["u_biased"], 1)

            def a_rstd(k):
                return lambda b, par: rstd(varA[:, :], rstdA[:, :], TILES, 2 * b + k + 1, "a_var", "a_rstd")

            def b_rstd(b, par):
                rstd(varB[:, :], rstdB[:, :], TILES, b + 1, "b_var", "b_rstd")

            periods(pool, PLAN["pool"], dict(
                [("a_rstd0", a_rstd(0)), ("a_rstd1", a_rstd(1)), ("b_rstd", b_rstd)]))

        @block.tensor
        def _(pe):
            mm = pe.matmul

            def centre(h):
                def part(p, par):
                    pe.wait_ge(s["x"], 2 * p + h + 1)
                    if p == 0:
                        pe.wait_ge(s["ld_const"], 16)
                    else:
                        pe.wait_ge(s[("bd", "m")[h]], p)
                    for t in range(4 * h, 4 * h + 4):
                        ins = mm(SA[:, t * P:(t + 1) * P], XC[:, p, t * P:(t + 1) * P], cen, start=True, stop=True)
                    ins.then_inc(s["centred"], 1)
                return part

            def xn_to_channels(h):
                def part(p, par):
                    pe.wait_ge(s["xn_tok"], 2 * p + h + 1)
                    for t in range(4 * h, 4 * h + 4):
                        ins = pe.transpose(SA[:, t * P:(t + 1) * P], XNT[:, t, :], ident)
                    ins.then_inc(s["xnT"], 1)
                return part

            def keys_values(h):
                def part(p, par):
                    pe.wait_ge(s["xn"], 2 * p + h + 1)
                    if p == 0:
                        pe.wait_ge(s["ld_att"], LD_ATT)
                    mm(ps[0:C, h, :], WKV[:, :], XN[:, p % 2, h * HALF:(h + 1) * HALF], start=True, stop=True)\
                        .then_inc(s["kv_ps"], 1)
                return part

            def kv_to_tokens(p, par):
                pe.wait_ge(s["kexp"], p + 1)
                for t in range(TILES):
                    ins = pe.transpose(SA[:, t * C:(t + 1) * C], KV[:, t * P:(t + 1) * P], ident[0:C, 0:C])
                ins.then_inc(s["kvT_ps"], 1)

            def context(p, par):
                pe.wait_ge(s["kvT"], p + 1)
                for t in range(TILES):
                    ins = mm(ps[0:32, 1, 0:32], KVT[:, t, 0:32], KVT[:, t, 32:64], start=(t == 0), stop=(t == TILES - 1))
                ins.then_inc(s["ctx"], 1)

            def context_turned(p, par):
                pe.wait_ge(s["z"], 2 * (p + 1))
                mm(ps[:, 0, 0:32], Z[:, :, :].rearrange("p h e -> p (h e)"), ident[0:32, 0:32], start=True, stop=True)\
                    .then_inc(s["ctxT"], 1)

            def context_out(p, par):
                pe.wait_ge(s["bd"], p + 1)
                if p == 0:
                    pe.wait_ge(s["set_wocev"], 1)
                for i in range(2):
                    ins = mm(ps[:, 1, i * P:(i + 1) * P], BD[:, i].rearrange("p h d -> p (h d)"), WOC[:, :],
                             start=True, stop=True)
                ins.then_inc(s["m_ps"], 1)

            def queries(g):
                def part(p, par):
                    n = 4 * p + g
                    q = ps[:, Q_BANK[n % 2], :]
                    pe.wait_ge(s["xn"], 2 * p + g // 2 + 1)
                    if n == 0:
                        pe.wait_ge(s["ld_att"], LD_ATT)
                        pe.wait_ge(s["set_dve"], SET_BQ)
                        pe.wait_ge(s["memsets"], 5)
                    if n >= 2:
                        pe.wait_ge(s["qsub"], n - 1)
                    mm(q, ones_r[:, :], BQR, start=True, stop=False)
                    for j in range(UT_):
                        t = UT_ * g + j
                        ins = mm(q[:, j * 256:(j + 1) * 256], XN[:, p % 2, t * P:(t + 1) * P], WQB[:, :],
                                 start=False, stop=(j == UT_ - 1))
                    ins.then_inc(s["q_ps"], 1)
                return part

            def q_to_channels(g):
                def part(p, par):
                    n = 4 * p + g
                    pe.wait_ge(s["qnorm"], n + 1)
                    if n >= 1:
                        pe.wait_ge(s["qT"], n)
                    for r in range(4):
                        ins = pe.transpose(ps[:, QT_BANK, r * P:(r + 1) * P], QS[:, n % 2, r * P:(r + 1) * P], ident)
                    ins.then_inc(s["qT_ps"], 1)
                return part

            def residual(g):
                def part(p, par):
                    n = 4 * p + g
                    a = ps[:, AT_BANK[n % 2], :]
                    if n == 0:
                        pe.wait_ge(s["set_dve"], SET_BO)
                        pe.wait_ge(s["set_wocev"], 1)
                    if n >= 2:
                        pe.wait_ge(s["u"], n - 1)
                    mm(a, ones_r[:, :], BOR, start=True, stop=False, skip_group_check=True)
                    for j in range(UT_):
                        t = UT_ * g + j
                        ins = mm(a[:, j * 256:(j + 1) * 256], XC[:, p, t * P:(t + 1) * P], ic, start=False, stop=False,
                                 skip_group_check=True)
                    ins.then_inc(s["at_open"], 1)
                return part

            def attend(g):
                def part(p, par):
                    n = 4 * p + g
                    a = ps[:, AT_BANK[n % 2], :]
                    pe.wait_ge(s["m"], p + 1)
                    pe.wait_ge(s["qT"], n + 1)
                    for r in range(4):
                        ins = mm(a[:, r * P:(r + 1) * P], QT[:, n % 2, r, :], M[:, p % 2, r % 2, :],
                                 start=False, stop=(r == 3), skip_group_check=True)
                    ins.then_inc(s["att"], 1)
                return part

            def u_to_channels(g):
                def part(p, par):
                    n = 4 * p + g
                    pe.wait_ge(s["ulo"], n + 1)
                    if n >= 1:
                        pe.wait_ge(s["uT"], n)
                    for r in range(4):
                        ins = pe.transpose(ps[:, UT_BANK, r * P:(r + 1) * P].bitcast(F32R),
                                           US[:, n % 2, r].rearrange("p k c -> p (k c)"), ident_r[:, :])
                    ins.then_inc(s["uT_ps"], 1)
                return part

            def set_outputs(p, par):
                pe.wait_ge(s["ld_const"], 16)
                pe.wait_ge(s["ld_att"], LD_ATT)
                mm(ps[:, 6, 0:P], WOUT[:, :], ic[0:C, 0:P], start=True, stop=True).then_inc(s["set_woc"], 1)
                mm(ps[0:C, 7, 0:P], BOUT2[:, :], ic[0:C, 0:P], start=True, stop=True).then_inc(s["set_bo"], 1)

            pair_periods("pe", [("set_outputs", set_outputs)] + [(f"{name}{h}", part(h)) for h in range(2) for name, part in (
                                    ("centre", centre), ("xn_to_channels", xn_to_channels),
                                    ("keys_values", keys_values))]
                         + [("kv_to_tokens", kv_to_tokens), ("context", context), ("context_turned", context_turned),
                            ("context_out", context_out)]
                         + [(f"{name}{g}", part(g)) for g in range(4) for name, part in (
                             ("queries", queries), ("q_to_channels", q_to_channels), ("residual", residual),
                             ("attend", attend), ("u_to_channels", u_to_channels))])

            pe.wait_ge(s["ld_ffn0"], LD_FFN0)
            pe.wait_ge(s["qT"], UNITS)
            pe.wait_ge(s["qsub"], UNITS)
            for e in range(E):
                ins = mm(ps[:, Q_BANK[0], e * C:(e + 1) * C], W2TA[:, e, :], ic[0:C, C:P], start=True, stop=True)
            ins.then_inc(s["set_w2"], 1)
            mm(ps[0:E, Q_BANK[1], 0:C], B2TA[:, :], ic[0:C, C:P], start=True, stop=True).then_inc(s["set_w2"], 1)
            rp = steps_of(pe, s["router_pe"])
            r_ps = ps[:, QT_BANK, :]
            pe.wait_ge(s["router_dve"], RD_U8)
            rp.done(mm(r_ps[0:E, 0:E], u8[:, :], WR[:, :], start=True, stop=True))
            pe.wait_ge(s["router_dve"], RD_P1)
            rp.done(mm(r_ps[0:E, 0:E], ones[:, 0:E], R[:, 1, :], start=True, stop=True))
            pe.wait_ge(s["router_dve"], RD_D2)
            rp.done(mm(ps[:, UT_BANK, 0:4 * B], ones[:, :], D2[:, :, :].rearrange("p b k -> p (b k)"),
                       start=True, stop=True))
            pe.wait_ge(s["router_dve"], RD_WD)
            rp.done(pe.transpose(r_ps[0:E, 0:E], R[:, 12, :], ident[0:E, 0:E]))
            pe.wait_ge(s["router_dve"], RD_WDT)
            pe.wait_ge(s["set_b2ev"], 1)
            rp.done(mm(r_ps[0:E, 0:C], wdT[:, :], B2A[:, :], start=True, stop=True))
            pe.wait_ge(s["router_dve"], RD_D1)
            rp.done(mm(r_ps[:, :], ones[:, :], D1[:, :, :].rearrange("p b c -> p (b c)"), start=True, stop=True))

            def a_hidden(n):
                def part(b, par):
                    k, c = n // 2, n % 2
                    if n == 0:
                        pe.wait_ge(s["a_sel"], 2 * (b + 1))
                        ge(pe, s["a_z"], b)
                    else:
                        pe.wait_ge(s["a_gelu"], 4 * b + n)
                    for w in range(2):
                        ins = mm(ps[:, A_BANK, :], W1S[:, k, w, :],
                                 UTR[:, bass.ds(b, 1), c * HALF:(c + 1) * HALF].rearrange("p a n -> p (a n)"),
                                 start=(w == 0), stop=(w == 1))
                    ins.then_inc(s["a_h"], 1)
                return part

            def a_output(b, par):
                pe.wait_ge(s["a_gelu"], 4 * b + 4)
                for k in range(2):
                    for c in range(2):
                        ins = mm(ps[c * C:(c + 1) * C, A_BANK, :], W2S[:, k, :], HA[:, k, c * HALF:(c + 1) * HALF],
                                 start=(k == 0), stop=(k == 1), skip_group_check=True)
                ins.then_inc(s["a_z_ps"], 1)

            def a_z_turned(b, par):
                pe.wait_ge(s["a_zc"], b + 1)
                for j in range(4):
                    ins = pe.transpose(ps[:, A_BANK, j * P:(j + 1) * P], ZC[:, j * P:(j + 1) * P], ident)
                ins.then_inc(s["a_zT"], 1)

            def a_vT(h):
                def part(b, par):
                    pe.wait_ge(s["a_vlo"], b + 1)
                    ge(pe, s["a_img"], 2 * b + h)
                    for j in range(4):
                        ins = pe.transpose(ps[:, V_BANK, j * P:(j + 1) * P].bitcast(F32R),
                                           VS[:, 4 * h + j].rearrange("p k c -> p (k c)"), ident_r[:, :])
                    ins.then_inc(s["a_vT"], 1)
                return part

            def b_conv(k):
                def part(b, par):
                    if k == 0:
                        pe.wait_ge(s["a_img"], 2 * b + 2)
                        ge(pe, s["b_cwt"], 2 * b)
                    for r in range(2 * k, 2 * k + 2):
                        for dx in range(3):
                            ins = mm(ps[:, B_BANK, :],
                                     WC[:, dx, 3 - r:5 - r, :].rearrange("p k c -> p (k c)"),
                                     VP[:, par, r:r + H - 1:2, dx:dx + W], start=(r == 0 and dx == 0),
                                     stop=(r == 3 and dx == 2), skip_group_check=True)
                    if k == 1:
                        ins.then_inc(s["b_conv"], 1)
                return part

            def b_to_tokens(b, par):
                pe.wait_ge(s["b_cv"], b + 1)
                for j in range(4):
                    ins = pe.transpose(ps[:, B_BANK, j * P:(j + 1) * P], CV[:, j * P:(j + 1) * P], ident)
                ins.then_inc(s["b_cvT"], 1)

            def b_to_channels(h):
                def part(b, par):
                    pe.wait_ge(s["b_elo"], b + 1)
                    if h == 1:
                        pe.wait_ge(s["b_et"], 2 * b + 1)
                    for j in range(4):
                        ins = pe.transpose(ps[:, B_BANK, j * P:(j + 1) * P].bitcast(F32R),
                                           ES[:, 2 * j + h].rearrange("p k c -> p (k c)"), ident_r[:, :])
                    ins.then_inc(s["b_eT"], 1)
                return part

            def b_gates(b, par):
                pe.wait_ge(s["b_et"], 2 * (b + 1))
                for t in range(TILES):
                    ins = mm(ps[:, B_BANK, t * 2 * E:(t + 1) * 2 * E], ET[:, par, t * P:(t + 1) * P],
                             GW[:, :, :].rearrange("p k e -> p (k e)"), start=True, stop=True)
                ins.then_inc(s["b_gate"], 1)

            def b_gates_turned(h):
                def part(b, par):
                    pe.wait_ge(s["b_cw"], 2 * (b + 1))
                    if h == 1:
                        pe.wait_ge(s["b_cwt"], 2 * b + 1)
                    for j in range(4):
                        ins = pe.transpose(ps[0:32, B_BANK, j * P:(j + 1) * P].bitcast(F32R),
                                           CWS[:, 4 * h + j].rearrange("p k e -> p (k e)"), ident_r[:, :])
                    ins.then_inc(s["b_cwT"], 1)
                return part

            acc = ps[:, ACC_BANK, :]

            def f_hidden(m):
                e, c = m // 2, m % 2

                def part(b, par):
                    if m == 0:
                        pe.wait_ge(s["b_cwt"], 2 * (b + 1))
                    ge(pe, s["f_gelu"], 16 * b + m - 1)
                    for w in range(2):
                        ins = mm(ps[:, H_BANK[m % 2], :], W1B[:, e, w, :], ET[:, par, c * HALF:(c + 1) * HALF],
                                 start=(w == 0), stop=(w == 1))
                    ins.then_inc(s["f_h"], 1)
                return part

            def f_gate(m):
                e, c = m // 2, m % 2

                def part(b, par):
                    ge(pe, s["f_hg"], 16 * b + m - 1)
                    mm(ps[:, CW_BANK[m % 2], :], SEL[:, e, :], CWT[:, par, c * HALF:(c + 1) * HALF],
                       start=True, stop=True).then_inc(s["f_cw"], 1)
                return part

            def f_start(b, par):
                ge(pe, s["f_out"], b)
                for c in range(2):
                    mm(acc, B2B[:, (1 - c) * C:(3 - c) * C], CWT[:, par, c * HALF:(c + 1) * HALF],
                       start=(c == 0), stop=False, skip_group_check=True)
                for j in range(4):
                    ins = mm(acc[:, j * P:(j + 1) * P], TF[:, par, j].rearrange("p h c -> p (h c)"), ident,
                             start=False, stop=False, skip_group_check=True)
                ins.then_inc(s["f_start"], 1)

            def f_output(e):
                def part(b, par):
                    pe.wait_ge(s["f_hg"], 16 * b + 2 * e + 2)
                    for c in range(2):
                        ins = mm(acc[c * C:(c + 1) * C, :], W2B[:, e, :], HG[:, (2 * e + c) % 4, :],
                                 start=False, stop=(e == E - 1), skip_group_check=True)
                    ins.then_inc(s["f_w2"], 1)
                return part

            pe.wait_ge(s["set_dve"], SET_F1)
            every = range(SLOTS)
            periods(pe, PLAN["pe"], dict(
                [(f"f_hidden{m}", f_hidden(m)) for m in every]
                    + [(f"a_hidden{n}", a_hidden(n)) for n in range(4)]
                    + [("a_output", a_output), ("a_z_turned", a_z_turned), ("a_vT0", a_vT(0)), ("a_vT1", a_vT(1)),
                       ("b_conv0", b_conv(0)), ("b_conv1", b_conv(1)), ("b_to_tokens", b_to_tokens), ("b_to_channels0", b_to_channels(0)),
                       ("b_to_channels1", b_to_channels(1)), ("b_gates", b_gates),
                       ("b_gates_turned0", b_gates_turned(0)), ("b_gates_turned1", b_gates_turned(1))]
                    + [(f"f_gate{m}", f_gate(m)) for m in every]
                    + [("f_start", f_start)]
                    + [(f"f_output{e}", f_output(e)) for e in range(E)]))

        @block.vector
        def _(vec):
            vr = vec.tensor_reduce
            tt = vec.tensor_tensor
            st = steps_of(vec, s["set_dve"])

            def split(hi, lo, whole):
                st.done(vec.tensor_copy(hi, whole))
                st.wait()
                st.done(tt(lo, whole, f32(hi), ALU.subtract))

            def bias_rows(rows, src):
                view = rows.rearrange("p (k n) -> p k n", n=P)
                src = src.unsqueeze(1).broadcast_to([C, 4, P])
                st.done(vec.tensor_copy(view, src))
                st.wait()
                st.done(tt(view[32:C], src[32:C], f32(view[32:C]), ALU.subtract))

            def set_bq(p, par):
                vec.wait_ge(s["ld_const"], 16)
                st.done(vec.tensor_copy(ident_r[:, :], ident))
                vec.wait_ge(s["ld_att"], LD_ATT)
                bias_rows(BQR, BQ2[:, :])
                assert st.n == SET_BQ

            def set_bo(p, par):
                vec.wait_ge(s["set_bo"], 1)
                bias_rows(BOR, ps[0:C, 7, 0:P])
                assert st.n == SET_BO

            def set_layer0(p, par):
                vec.wait_ge(s["ld_ffn0"], LD_FFN0)
                split(W1A[:, :, 0, :], W1A[:, :, 1, :], W1stage[:, :, :])
                assert st.n == SET_W1A

            def set_conv(p, par):
                vec.wait_ge(s["ld_conv"], 16)
                st.done(vec.tensor_scalar(WCstage, WCstage, 0.0, 2.0, ALU.is_gt, ALU.mult))
                st.wait()
                vec.wait_ge(s["memsets"], 6)
                st.done(vec.tensor_scalar(WC[:, :, 1:4, :], WCstage.rearrange("p (x y) c -> p x y c", x=3), -1.0, None,
                                          ALU.add))
                assert st.n == SET_SIGNS
                vec.wait_ge(s["ld_conv"], 32)
                st.done(vr(CSCALE[:, :], WCS, X, ALU.add, apply_absolute_value=True))
                st.wait()
                st.done(vec.tensor_scalar(CSCALE[:, :], CSCALE[:, :], 1.0 / (C * TAPS), None, ALU.mult))
                assert st.n == SET_CONV

            def set_layer1(p, par):
                vec.wait_ge(s["ld_w1b"], 16)
                split(W1B[:, :, 0, :], W1B[:, :, 1, :], W1stage[:, :, :])
                assert st.n == SET_W1B
                vec.wait_ge(s["ld_ffn1"], LD_FFN1)
                split(GW[:, 0, :], GW[:, 1, :], GWstage[:, :])
                split(B2hi[:, :], B2lo[:, :], B2stage[:, :])
                st.wait()
                vec.wait_ge(s["memsets"], 5)
                st.done(vec.tensor_scalar(B2lo[:, :], B2lo[:, :], hlmask[:, 1:2], None, ALU.mult))
                st.wait()
                st.done(vec.scalar_tensor_tensor(B2B[:, C:2 * C], f32(B2hi[:, :]), hlmask[:, 0:1], B2lo[:, :],
                                                 ALU.mult, ALU.add))
                vec.wait_ge(s["ld_sel"], 16)
                st.done(vec.tensor_copy(SEL[:, :, :], SELstage))
                assert st.n == SET_F1, st.n

            def variance(ss, var, eps, k, ss_sem, var_sem):
                vec.wait_ge(s[ss_sem], k)
                vec.tensor_scalar(var, ss, 1.0 / C, eps, ALU.mult, ALU.add).then_inc(s[var_sem], 1)

            def order_rows(h):
                def part(p, par):
                    vec.wait_ge(s["ld_x0" if p == 0 else "ld_x"], 16)
                    vec.tensor_copy(XC[:, p, h * HALF:(h + 1) * HALF].rearrange("p (y x) -> p y x", x=W),
                                    XR[:, p, :].rearrange("p (y h x) -> p h y x", h=2, x=W)[:, h])\
                        .then_inc(s["x"], 1)
                return part

            def sum_squares1(h):
                def part(p, par):
                    vec.wait_ge(s["sq1"], 2 * p + h + 1)
                    cols = slice(h * TILES, (h + 1) * TILES)
                    vr(ss1[:, cols], SQ1[:, 4 * h:4 * h + 4, :].rearrange("p t (b c) -> p (t b) c", b=2), X, ALU.add)\
                        .then_inc(s["ss1"], 1)
                    variance(ss1[:, cols], var1[:, cols], LN_C_EPS, 2 * p + h + 1, "ss1", "var1")
                return part

            def normalise1(h):
                def part(p, par):
                    vec.wait_ge(s["rstd1"], 2 * p + h + 1)
                    tt(XNT[:, 4 * h:4 * h + 4, :].rearrange("p t (b c) -> p (t b) c", b=2), tiles(ps[:, h, :]),
                       rstd1_[:, h * TILES:(h + 1) * TILES].unsqueeze(2).broadcast_to([P, TILES, C]), ALU.mult)\
                        .then_inc(s["xn_tok"], 1)
                return part

            def key_max(p, par):
                vec.wait_ge(s["kv"], 2 * p + 2)
                vr(nkmax[:, :], KV[0:32, :], X, ALU.max, negate=True).then_inc(s["kmax"], 1)

            def key_norm(p, par):
                vec.wait_ge(s["kexp"], p + 1)
                vec.reciprocal(rksum[:, :], ksum[:, :]).then_inc(s["rk"], 1)
                vec.wait_ge(s["rk"], 2 * p + 1)
                vec.tensor_scalar(r01[:, :], pairmask, rksum[:, 0:1], None, ALU.mult).then_inc(s["rk"], 1)

            def pick_context(p, par):
                vec.wait_ge(s["ctx"], p + 1)
                vec.wait_ge(s["rk"], 2 * p + 2)
                own = [ps[0:32, 1, i * KD:(i + 1) * KD].unsqueeze(1).broadcast_to([32, HEADS, KD]) for i in range(2)]
                vec.tensor_scalar(Z[:, :, :], own[0], r01[:, 0:1], None, ALU.mult).then_inc(s["z"], 1)
                vec.wait_ge(s["z"], 2 * p + 1)
                vec.scalar_tensor_tensor(Z[:, :, :], own[1], r01[:, 1:2], Z[:, :, :], ALU.mult, ALU.add)\
                    .then_inc(s["z"], 1)

            def block_diagonal(p, par):
                vec.wait_ge(s["ctxT"], p + 1)
                for i in range(2):
                    ins = tt(BD[:, i], ps[:, 0, i * KD:(i + 1) * KD].unsqueeze(1).broadcast_to([P, HEADS, KD]),
                             headmask.unsqueeze(2).broadcast_to([P, HEADS, KD]), ALU.mult)
                ins.then_inc(s["bd"], 1)

            def query_max(g):
                def part(p, par):
                    n = 4 * p + g
                    q = ps[:, Q_BANK[n % 2], :].rearrange("p (g d) -> p g d", d=KD)
                    vec.wait_ge(s["q_ps"], n + 1)
                    ge(vec, s["qsub"], n)
                    vr(qmax[:, :], q, X, ALU.max).then_inc(s["qmax"], 1)
                    vec.wait_ge(s["qmax"], n + 1)
                    if n >= 2:
                        vec.wait_ge(s["qT_ps"], n - 1)
                    tt(QS[:, n % 2, :].rearrange("p (g d) -> p g d", d=KD), q,
                       qmax[:, :].unsqueeze(2).broadcast_to([P, 32, KD]), ALU.subtract).then_inc(s["qsub"], 1)
                return part

            def query_sum(g):
                def part(p, par):
                    n = 4 * p + g
                    vec.wait_ge(s["qexp"], n + 1)
                    ge(vec, s["rqsum"], n)
                    vr(qsum[:, :], QS[:, n % 2, :].rearrange("p (g d) -> p g d", d=KD), X, ALU.add)\
                        .then_inc(s["qsum"], 1)
                    vec.wait_ge(s["qsum"], n + 1)
                    vec.reciprocal(rqsum[:, n % 2, :], qsum[:, :]).then_inc(s["rqsum"], 1)
                return part

            def sum_squares2(g):
                def part(p, par):
                    n = 4 * p + g
                    vec.wait_ge(s["sq2"], n + 1)
                    vr(ss2[:, n % 2, :], SQ2[:, n % 2], X, ALU.add).then_inc(s["ss2"], 1)
                    variance(ss2[:, n % 2, :], var2[:, n % 2, :], LN_T_EPS, n + 1, "ss2", "var2")
                return part

            def normalise2(g):
                def part(p, par):
                    n, k = 4 * p + g, g % 2
                    a = ps[:, AT_BANK[k], :].rearrange("p (j b x c) -> p b j x c", j=UT_, b=2, x=2)
                    r = rstd2[:, k, :].rearrange("p (j b) -> p b j", b=2)
                    vec.wait_ge(s["rstd2"], n + 1)
                    vec.wait_ge(s["t_res"], n + 1)
                    for i in range(2):
                        ins = tt(U[:, 2 * p + i, UT_ * g:UT_ * g + UT_, :], a[:, i, :, 1, :],
                                 r[:, i].unsqueeze(2).broadcast_to([P, UT_, C]), ALU.mult)
                    ins.then_inc(s["u"], 1)
                    vec.wait_ge(s["u"], n + 1)
                    if n >= 2:
                        vec.wait_ge(s["uT_ps"], n - 1)
                    vec.tensor_copy(US[:, k, :, 0, :].rearrange("p (j b) c -> p b j c", b=2),
                                    U[:, 2 * p:2 * p + 2, UT_ * g:UT_ * g + UT_, :]).then_inc(s["uhi"], 1)
                return part

            pair_periods("vec", [(f"{name}{h}", part(h)) for h in range(2) for name, part in (
                                     ("order_rows", order_rows), ("sum_squares1_", sum_squares1), ("normalise1_", normalise1))]
                         + [("key_max", key_max), ("key_norm", key_norm), ("pick_context", pick_context),
                            ("block_diagonal", block_diagonal), ("set_bq", set_bq), ("set_bo", set_bo),
                            ("set_layer0", set_layer0), ("set_conv", set_conv),
                            ("set_layer1", set_layer1)]
                         + [(f"{name}{g}", part(g)) for g in range(4) for name, part in (
                             ("query_max", query_max), ("query_sum", query_sum), ("sum_squares2_", sum_squares2),
                             ("normalise2_", normalise2))])

            rd = steps_of(vec, s["router_dve"])
            vec.wait_ge(s["uT"], UNITS)
            rd.done(vr(u8[:, :], usum[:, :, :], X, ALU.add))
            assert rd.n == RD_U8
            vec.wait_ge(s["router_pe"], 1)
            rd.done(vec.scalar_tensor_tensor(R[:, 0, :], ps[0:E, QT_BANK, 0:E], 1.0 / S, BR[:, :], ALU.mult, ALU.add))

            def softmax(src, dst, m, a_step):
                rd.wait()
                rd.done(vr(RV[:, m], R[:, src, :], X, ALU.max, negate=True))
                vec.wait_ge(s["router_act"], a_step)
                rd.done(vec.reciprocal(RV[:, m + 2], RV[:, m + 1]))
                rd.wait()
                rd.done(vec.tensor_scalar(R[:, dst, :], R[:, dst, :], RV[:, m + 2], None, ALU.mult))

            softmax(0, 1, 0, 1)
            assert rd.n == RD_P1
            vec.wait_ge(s["router_pe"], 2)
            rd.done(vec.tensor_scalar(R[:, 3, :], ps[0:E, QT_BANK, 0:E], float(S), CAPACITY, ALU.mult, ALU.max))
            rd.done(vec.tensor_scalar(R[:, 5, :], ps[0:E, QT_BANK, 0:E], float(S), CAPACITY, ALU.mult, ALU.is_gt))
            rd.wait()
            rd.done(vec.reciprocal(R[:, 4, :], R[:, 3, :]))
            rd.wait()
            rd.done(vec.tensor_scalar(R[:, 4, :], R[:, 4, :], CAPACITY, -1.0, ALU.mult, ALU.add))
            rd.wait()
            rd.done(tt(R[:, 4, :], R[:, 4, :], R[:, 5, :], ALU.mult))
            rd.wait()
            rd.done(vec.scalar_tensor_tensor(R[:, 6, :], R[:, 4, :], 1.0, R[:, 1, :], ALU.add, ALU.mult))
            softmax(6, 7, 3, 2)
            largest(vec, rd, E, 1, R[:, 7:8, :], rev[0:E, :], RV[:, 6], R[:, 13:14, :], R[:, 14:15, :],
                    Rq[:, 0, :], R[:, 8:9, :])
            without(vec, rd, R[:, 9:10, :], R[:, 8:9, :], R[:, 7:8, :])
            largest(vec, rd, E, 1, R[:, 9:10, :], rev[0:E, :], RV[:, 7], R[:, 13:14, :], R[:, 14:15, :],
                    Rq[:, 1, :], R[:, 10:11, :])
            rd.wait()
            rd.done(tt(RV[:, 10], RV[:, 6], RV[:, 7], ALU.subtract))
            assert rd.n == RD_DIFF, rd.n
            vec.wait_ge(s["router_act"], 3)
            rd.done(vec.tensor_scalar(RV[:, 9], RV[:, 8], 1.0, None, ALU.add))
            rd.wait()
            rd.done(vec.reciprocal(vals[:, 0:1], RV[:, 9]))
            rd.wait()
            rd.done(tt(vals[:, 1:2], RV[:, 8], vals[:, 0:1], ALU.mult))
            rd.done(vec.tensor_scalar(vals[:, 2:4], Rq[:, :, 0], -1.0, float(E), ALU.mult, ALU.add))
            rd.wait()
            rd.done(tt(D2[:, :, :], vals[:, :].unsqueeze(1).broadcast_to([E, B, 4]),
                       ident[0:E, 0:B].unsqueeze(2).broadcast_to([E, B, 4]), ALU.mult))
            assert rd.n == RD_D2, rd.n
            rd.done(vec.tensor_scalar(R[:, 11, :], R[:, 8, :], vals[:, 0:1], None, ALU.mult))
            rd.wait()
            rd.done(vec.scalar_tensor_tensor(R[:, 12, :], R[:, 10, :], vals[:, 1:2], R[:, 11, :], ALU.mult, ALU.add))
            assert rd.n == RD_WD, rd.n
            vec.wait_ge(s["router_pe"], 3)
            rd.done(vec.tensor_copy(WI[:, :, :].rearrange("p b k -> p (b k)"), ps[:, UT_BANK, 0:4 * B]))
            rd.wait()
            rd.done(vec.tensor_copy(IDX[:, :].rearrange("p (b k) -> p b k", k=2), WI[0:1, :, 2:4]))
            assert rd.n == RD_IDX, rd.n
            vec.wait_ge(s["router_pe"], 4)
            rd.done(vec.tensor_copy(wdT[:, :], ps[0:E, QT_BANK, 0:E]))
            assert rd.n == RD_WDT, rd.n
            vec.wait_ge(s["router_pe"], 5)
            rd.done(vec.tensor_copy(b2row[:, :], ps[0:E, QT_BANK, 0:C]))
            rd.wait()
            rd.done(tt(D1[:, :, :], b2row[:, :].unsqueeze(1).broadcast_to([E, B, C]),
                       ident[0:E, 0:B].unsqueeze(2).broadcast_to([E, B, C]), ALU.mult))
            assert rd.n == RD_D1, rd.n
            vec.wait_ge(s["router_pe"], 6)
            rd.done(vec.tensor_copy(B2A_b[:, :, :].rearrange("p b c -> p (b c)"), ps[:, QT_BANK, :]))
            assert rd.n == RD_B2, rd.n

            def bcast(col):
                return col.unsqueeze(2).broadcast_to([P, TILES, C])

            def paired(bank):
                return bank.rearrange("p (j h c) -> p j h c", h=2, c=C)

            def by_pairs(tile):
                return tile.rearrange("p (h j) c -> p j h c", h=2)

            def split_tokens(whole, parts, b, hi, lo, read):
                ge(vec, s[read], 2 * b)
                vec.tensor_copy(parts[:, :, 0, :], whole[:, :, :]).then_inc(s[hi], 1)
                vec.wait_ge(s[hi], b + 1)
                tt(parts[:, :, 1, :], whole[:, :, :], f32(parts[:, :, 0, :]), ALU.subtract).then_inc(s[lo], 1)

            def a_sum(b, par):
                vec.wait_ge(s["a_zT"], b + 1)
                vec.wait_ge(s["u_biased"], b + 1)
                tt(by_pairs(ZA), paired(ps[:, A_BANK, :]), by_pairs(image(U, b)), ALU.add).then_inc(s["a_z"], 1)

            def a_sum_squares(k):
                def part(b, par):
                    vec.wait_ge(s["a_sq"], 2 * b + k + 1)
                    vr(ssA[:, :], SQA[:, :, :], X, ALU.add).then_inc(s["a_ss"], 1)
                    variance(ssA[:, :], varA[:, :], (LN_T_EPS, LN_C_EPS)[k], 2 * b + k + 1, "a_ss", "a_var")
                return part

            def a_zn(b, par):
                vec.wait_ge(s["a_rstd"], 2 * b + 1)
                tt(ZN[:, :, :], ZA[:, :, :], bcast(rstdA[:, :]), ALU.mult).then_inc(s["a_zn"], 1)
                vec.wait_ge(s["a_zn"], b + 1)
                tt(ZG, ZN, GAMMA[:, :].unsqueeze(1).broadcast_to([P, TILES, C]), ALU.mult).then_inc(s["a_zg"], 1)

            def a_residual(b, par):
                vec.wait_ge(s["a_zg"], b + 1)
                vec.wait_ge(s["t_beta"], b + 1)
                tt(TA[:, :, :], image(T, b), ZG[:, :, :], ALU.add).then_inc(s["a_t"], 1)

            def a_centre(b, par):
                vec.wait_ge(s["a_t"], b + 1)
                vr(sumA[:, :], TA[:, :, :], X, ALU.add).then_inc(s["a_sum"], 1)
                vec.wait_ge(s["a_sum"], b + 1)
                vec.scalar_tensor_tensor(XA[:, :, :], bcast(sumA[:, :]), -1.0 / C, TA[:, :, :], ALU.mult, ALU.add)\
                    .then_inc(s["a_xc"], 1)

            def a_normalise(b, par):
                vec.wait_ge(s["a_rstd"], 2 * b + 2)
                tt(V[:, :, :], XA[:, :, :], bcast(rstdA[:, :]), ALU.mult).then_inc(s["a_v"], 1)
                vec.wait_ge(s["a_v"], b + 1)
                split_tokens(V, VS, b, "a_vhi", "a_vlo", "a_vT")

            def b_residual(b, par):
                vec.wait_ge(s["b_cvT"], b + 1)
                tt(TF[:, par], by_pairs(TA[:, :, :]), paired(ps[:, B_BANK, :]), ALU.add).then_inc(s["b_t"], 1)

            def b_centre(b, par):
                vec.wait_ge(s["b_t"], b + 1)
                vr(sumB[:, :], TF[:, par].rearrange("p j h c -> p (j h) c"), X, ALU.add).then_inc(s["b_sum"], 1)
                vec.wait_ge(s["b_sum"], b + 1)
                vec.scalar_tensor_tensor(XB[:, :, :], bcast(sumB[:, :]), -1.0 / C,
                                         TF[:, par].rearrange("p j h c -> p (j h) c"), ALU.mult, ALU.add)\
                    .then_inc(s["b_xc"], 1)

            def b_sum_squares(b, par):
                vec.wait_ge(s["b_sq"], b + 1)
                vr(ssB[:, :], SQB[:, :, :], X, ALU.add).then_inc(s["b_ss"], 1)
                variance(ssB[:, :], varB[:, :], LN_T_EPS, b + 1, "b_ss", "b_var")

            def b_normalise(b, par):
                vec.wait_ge(s["b_rstd"], b + 1)
                tt(EN[:, :, :], XB[:, :, :], bcast(rstdB[:, :]), ALU.mult).then_inc(s["b_en"], 1)
                vec.wait_ge(s["b_en"], b + 1)
                split_tokens(EN, ES, b, "b_ehi", "b_elo", "b_eT")

            def b_logits(b, par):
                vec.wait_ge(s["b_gate"], b + 1)
                steps = steps_of(vec, s["b_lg"], 4 * b)
                parts = ps[:, B_BANK, 0:TILES * 2 * E].rearrange("p (t k e) -> p k t e", k=2, e=E)
                steps.done(tt(G[:, 0], parts[:, 0], GBB[:, :, :], ALU.add))
                steps.wait()
                steps.done(tt(G[:, 0], G[:, 0], parts[:, 1], ALU.add))
                steps.wait()
                steps.done(vr(gv[:, 0, :], G[:, 0], X, ALU.max))
                steps.wait()
                steps.done(tt(G[:, 1], G[:, 0], gv[:, 0, :].unsqueeze(2).broadcast_to([P, TILES, E]), ALU.subtract))

            def b_probs(b, par):
                vec.wait_ge(s["b_exp"], b + 1)
                steps = steps_of(vec, s["b_top"], 16 * b)
                steps.done(vr(gv[:, 1, :], G[:, 1], X, ALU.add))
                steps.wait()
                steps.done(vec.reciprocal(gv[:, 2, :], gv[:, 1, :]))
                steps.wait()
                steps.done(tt(G[:, 2], G[:, 1], gv[:, 2, :].unsqueeze(2).broadcast_to([P, TILES, E]), ALU.mult))

            def b_first(b, par):
                steps = steps_of(vec, s["b_top"], 16 * b + 3)
                largest(vec, steps, P, TILES, G[:, 2], rev, gv[:, 3, :], G[:, 3], G[:, 4], gq[:, 0, :], G[:, 5])
                without(vec, steps, G[:, 6], G[:, 5], G[:, 2])

            def b_second(b, par):
                steps = steps_of(vec, s["b_top"], 16 * b + 9)
                largest(vec, steps, P, TILES, G[:, 6], rev, gv[:, 3, :], G[:, 3], G[:, 4], gq[:, 1, :], G[:, 7])

            def b_weights(b, par):
                steps = steps_of(vec, s["b_top"], 16 * b + 14)
                steps.wait()
                steps.done(tt(G[:, 8], G[:, 5], G[:, 7], ALU.add))
                steps.wait()
                steps.done(tt(G[:, 9], G[:, 8], G[:, 2], ALU.mult))
                steps.wait()
                cw = G[:, 9].unsqueeze(2).broadcast_to([P, TILES, 2, E])
                ge(vec, s["b_cwT"], 2 * b)
                vec.tensor_copy(CWS[:, :, 0::2, :], cw).then_inc(s["b_cw"], 1)
                vec.wait_ge(s["b_cw"], 2 * b + 1)
                tt(CWS[:, :, 1::2, :], cw, f32(CWS[:, :, 0::2, :]), ALU.subtract).then_inc(s["b_cw"], 1)

            def f_gated(m):
                def part(b, par):
                    vec.wait_ge(s["f_gelu"], 16 * b + m + 1)
                    vec.wait_ge(s["f_cw"], 16 * b + m + 1)
                    ge(vec, s["f_w2"], 8 * b + m // 2 - 1)
                    tt(HG[:, m % 4, :], HB[:, m % 2, :], ps[:, CW_BANK[m % 2], :], ALU.mult).then_inc(s["f_hg"], 1)
                return part

            periods(vec, PLAN["vec"], dict(
                [(f"f_gated{m}", f_gated(m)) for m in range(SLOTS)]
                    + [("b_residual", b_residual), ("b_centre", b_centre),
                       ("b_ss", b_sum_squares), ("b_normalise", b_normalise), ("b_logits", b_logits),
                       ("b_probs", b_probs), ("b_first", b_first), ("b_second", b_second),
                       ("b_weights", b_weights), ("a_sum", a_sum), ("a_ss0", a_sum_squares(0)), ("a_zn", a_zn),
                       ("a_residual", a_residual), ("a_centre", a_centre), ("a_ss1", a_sum_squares(1)), ("a_normalise", a_normalise)]))

        @block.scalar
        def _(act):
            av = act.activation

            def square1(h):
                def part(p, par):
                    act.wait_ge(s["centred"], 2 * p + h + 1)
                    av(SQ1[:, 4 * h:4 * h + 4, :].rearrange("p t c -> p (t c)"), ps[:, h, :], ACT.Square)\
                        .then_inc(s["sq1"], 1)
                return part

            def channels1(h):
                def part(p, par):
                    act.wait_ge(s["xnT"], 2 * p + h + 1)
                    if p >= 2:
                        act.wait_ge(s["q_ps"], 4 * (p - 2) + 2 * h + 2)
                    av(XN[:, p % 2, h * HALF:(h + 1) * HALF], ps[:, h, :], ACT.Copy).then_inc(s["xn"], 1)
                return part

            def keys_values(h):
                def part(p, par):
                    act.wait_ge(s["kv_ps"], 2 * p + h + 1)
                    if p >= 1:
                        act.wait_ge(s["kvT_ps"], p)
                    av(KV[:, h * HALF:(h + 1) * HALF], ps[0:C, h, :], ACT.Identity, bias=BKV[:, 0:1])\
                        .then_inc(s["kv"], 1)
                return part

            def key_exp(p, par):
                act.wait_ge(s["kmax"], p + 1)
                av(KV[0:32, :], KV[0:32, :], ACT.Exp, bias=nkmax[:, 0:1], accum_out=ksum[:, 0:1])\
                    .then_inc(s["kexp"], 1)

            def tokens_kv(p, par):
                act.wait_ge(s["kvT_ps"], p + 1)
                av(KVT[:, :, :].rearrange("p t c -> p (t c)"), SA[:, 0:TILES * C], ACT.Copy).then_inc(s["kvT"], 1)

            def outputs(p, par):
                act.wait_ge(s["m_ps"], p + 1)
                if p >= 2:
                    act.wait_ge(s["att"], 4 * (p - 1))
                av(M[:, p % 2].rearrange("p i n -> p (i n)"), ps[:, 1, 0:2 * P], ACT.Copy).then_inc(s["m"], 1)

            def query_exp(g):
                def part(p, par):
                    n = 4 * p + g
                    act.wait_ge(s["qsub"], n + 1)
                    av(QS[:, n % 2, :], QS[:, n % 2, :], ACT.Exp).then_inc(s["qexp"], 1)
                return part

            def query_channels(g):
                def part(p, par):
                    n = 4 * p + g
                    act.wait_ge(s["qT_ps"], n + 1)
                    if n >= 2:
                        act.wait_ge(s["att"], n - 1)
                    av(QT[:, n % 2].rearrange("p r n -> p (r n)"), ps[:, QT_BANK, :], ACT.Copy).then_inc(s["qT"], 1)
                return part

            def residual(g):
                def part(p, par):
                    n, k = 4 * p + g, g % 2
                    a = ps[:, AT_BANK[k], :].rearrange("p (j b x c) -> p j b x c", j=UT_, b=2, x=2)
                    act.wait_ge(s["att"], n + 1)
                    if n >= 2:
                        act.wait_ge(s["ss2"], n - 1)
                    av(SQ2[:, k], ps[:, AT_BANK[k], :].rearrange("p (r x c) -> p r x c", x=2, c=C)[:, :, 1, :],
                       ACT.Square).then_inc(s["sq2"], 1)
                    for i in range(2):
                        ins = av(T[:, 2 * p + i, UT_ * g:UT_ * g + UT_, :], a[:, :, i, 0, :], ACT.Copy)
                    ins.then_inc(s["t_res"], 1)
                return part

            def u_channels(g):
                def part(p, par):
                    n = 4 * p + g
                    act.wait_ge(s["uT_ps"], n + 1)
                    src = ps[:, UT_BANK, :].rearrange("p (j b n) -> p j b n", j=UT_, b=2)
                    for i in range(2):
                        ins = av(UTR[:, 2 * p + i, UT_ * g * P:UT_ * (g + 1) * P].rearrange("p (j n) -> p j n", n=P),
                                 src[:, :, i, :], ACT.Copy, accum_out=usum[:, 2 * p + i, g:g + 1])
                    ins.then_inc(s["uT"], 1)
                return part

            def set_outputs(p, par):
                act.wait_ge(s["set_woc"], 1)
                av(WOC[:, :], ps[:, 6, 0:P], ACT.Copy).then_inc(s["set_wocev"], 1)

            pair_periods("act", [("set_outputs", set_outputs)] + [(f"{name}{h}", part(h)) for h in range(2) for name, part in (
                                     ("square1_", square1), ("channels1_", channels1), ("keys_values", keys_values))]
                         + [("key_exp", key_exp), ("tokens_kv", tokens_kv), ("outputs", outputs)]
                         + [(f"{name}{g}", part(g)) for g in range(4) for name, part in (
                             ("query_exp", query_exp), ("query_channels", query_channels), ("residual", residual),
                             ("u_channels", u_channels))])

            act.wait_ge(s["set_w2"], 2)
            av(W2A[:, :, :].rearrange("p e c -> p (e c)"), ps[:, Q_BANK[0], :], ACT.Copy).then_inc(s["set_w2ev"], 1)
            av(B2A[:, :], ps[0:E, Q_BANK[1], 0:C], ACT.Copy).then_inc(s["set_b2ev"], 1)
            act.wait_ge(s["router_dve"], RD_MAX1)
            av(R[:, 1, :], R[:, 0, :], ACT.Exp, bias=RV[:, 0], accum_out=RV[:, 1]).then_inc(s["router_act"], 1)
            act.wait_ge(s["router_dve"], RD_MAX2)
            av(R[:, 7, :], R[:, 6, :], ACT.Exp, bias=RV[:, 3], accum_out=RV[:, 4]).then_inc(s["router_act"], 1)
            act.wait_ge(s["router_dve"], RD_DIFF)
            av(RV[:, 8], RV[:, 10], ACT.Exp, scale=-1.0).then_inc(s["router_act"], 1)
            av(gelu_table[:, :], R[:, 1, 0:1], ACT.Gelu)

            def a_select(b, par):
                ge(act, s["a_z_ps"], b)
                for k in range(2):
                    e = act.value_load(IDX[0:1, bass.ds(2 * b + k, 1)], min_val=0, max_val=E - 1)
                    av(W1S[:, k], f32(W1A[:, bass.ds(e, 1), :, :]).rearrange("p a k f -> p (a k) f"), ACT.Copy)
                    av(B1S[:, k:k + 1], B1A[:, bass.ds(e, 1)], ACT.Copy)
                    av(W2S[:, k, :], W2A[:, bass.ds(e, 1), :].rearrange("p a c -> p (a c)"), ACT.Copy,
                       scale=WI[:, bass.ds(b, 1), k:k + 1].rearrange("p a k -> p (a k)")).then_inc(s["a_sel"], 1)

            def a_gelu(n):
                def part(b, par):
                    k, c = n // 2, n % 2
                    if n == 0:
                        act.wait_ge(s["a_sel"], 2 * (b + 1))
                    act.wait_ge(s["a_h"], 4 * b + n + 1)
                    av(HA[:, k, c * HALF:(c + 1) * HALF], ps[:, A_BANK, :], ACT.Gelu, bias=B1S[:, k:k + 1])\
                        .then_inc(s["a_gelu"], 1)
                return part

            def a_z_copy(b, par):
                act.wait_ge(s["a_z_ps"], b + 1)
                av(ZC, ps[:, A_BANK, :], ACT.Copy).then_inc(s["a_zc"], 1)

            def a_square(k):
                def part(b, par):
                    act.wait_ge(s[("a_z", "a_xc")[k]], b + 1)
                    av(SQA[:, :, :], (ZA, XA)[k][:, :, :], ACT.Square).then_inc(s["a_sq"], 1)
                return part

            def a_image(h):
                def part(b, par):
                    act.wait_ge(s["a_vT"], 2 * b + h + 1)
                    if h == 0:
                        ge(act, s["b_conv"], b - 1)
                    av(VP[:, par, h + 1:h + H:2, 1:W + 1],
                       ps[:, V_BANK, :].rearrange("p (y x) -> p y x", x=W), ACT.Copy).then_inc(s["a_img"], 1)
                return part

            def b_scale(b, par):
                act.wait_ge(s["b_conv"], b + 1)
                av(CV[:, :], ps[:, B_BANK, :], ACT.Copy, scale=CSCALE[:, 0:1]).then_inc(s["b_cv"], 1)

            def b_square(b, par):
                act.wait_ge(s["b_xc"], b + 1)
                av(SQB[:, :, :], XB[:, :, :], ACT.Square).then_inc(s["b_sq"], 1)

            def b_channels(h):
                def part(b, par):
                    act.wait_ge(s["b_eT"], 2 * b + h + 1)
                    av(ET[:, par, h * HALF:(h + 1) * HALF], ps[:, B_BANK, :], ACT.Copy).then_inc(s["b_et"], 1)
                return part

            def b_exp(b, par):
                act.wait_ge(s["b_lg"], 4 * b + 4)
                av(G[:, 1], G[:, 1], ACT.Exp).then_inc(s["b_exp"], 1)

            def b_gates_out(h):
                def part(b, par):
                    act.wait_ge(s["b_cwT"], 2 * b + h + 1)
                    av(CWT[:, par, h * HALF:(h + 1) * HALF], ps[0:32, B_BANK, :], ACT.Copy)\
                        .then_inc(s["b_cwt"], 1)
                return part

            def f_gelu(m):
                def part(b, par):
                    act.wait_ge(s["f_h"], 16 * b + m + 1)
                    ge(act, s["f_hg"], 16 * b + m - 1)
                    av(HB[:, m % 2, :], ps[:, H_BANK[m % 2], :], ACT.Gelu, bias=B1B[:, m // 2:m // 2 + 1])\
                        .then_inc(s["f_gelu"], 1)
                return part

            def f_result(b, par):
                act.wait_ge(s["f_w2"], 8 * b + 8)
                ge(act, s["f_stored"], 16 * b)
                for h in range(2):
                    ins = av(OUT.rearrange("p (y h x) -> p h y x", h=2, x=W)[:, h],
                             ps[h * C:(h + 1) * C, ACC_BANK, :].rearrange("p (y x) -> p y x", x=W), ACT.Copy)
                ins.then_inc(s["f_out"], 1)

            act.wait_ge(s["set_w2ev"], 1)
            act.wait_ge(s["router_dve"], RD_IDX)
            periods(act, PLAN["act"], dict(
                [(f"f_gelu{m}", f_gelu(m)) for m in range(SLOTS)]
                    + [("f_result", f_result), ("a_z_copy", a_z_copy)]
                    + [("a_select", a_select)]
                    + [(f"a_hidden{n}", a_gelu(n)) for n in range(4)]
                    + [("a_square0", a_square(0)), ("a_square1", a_square(1)), ("a_image0", a_image(0)),
                       ("a_image1", a_image(1)), ("b_scale", b_scale),
                       ("b_square", b_square), ("b_channels0", b_channels(0)),
                       ("b_channels1", b_channels(1)), ("b_exp", b_exp),
                       ("b_gates_out0", b_gates_out(0)), ("b_gates_out1", b_gates_out(1))]))


RD_U8, RD_MAX1, RD_P1 = 1, 3, 5
RD_MAX2 = 12
RD_DIFF = RD_MAX2 + 2 + 4 + 1 + 4 + 1
RD_D2 = RD_DIFF + 5
RD_WD = RD_D2 + 2
RD_IDX = RD_WD + 2
RD_WDT = RD_IDX + 1
RD_D1 = RD_WDT + 2
RD_B2 = RD_D1 + 1


def constants():
    k = np.zeros((P, K_N), np.float32)
    eye = np.eye(C, dtype=np.float32)
    c = eye - np.float32(1.0 / C)
    k[:, K_ID:K_ID + P] = np.eye(P)
    for i in range(2):
        rows = slice(i * C, (i + 1) * C)
        k[rows, K_CEN + i * C:K_CEN + (i + 1) * C] = c
        k[rows, K_IC + i * P:K_IC + i * P + C] = eye
        k[rows, K_IC + i * P + C:K_IC + (i + 1) * P] = c
        k[i * KD:(i + 1) * KD, K_PAIR + i] = 1.0
        k[i * KD:(i + 1) * KD, K_HL + i] = 1.0
    for h in range(HEADS):
        k[h * KD:(h + 1) * KD, K_HEAD + h] = 1.0
    k[:, K_REV:K_REV + E] = np.arange(E, 0, -1)
    sel = np.zeros((32, E, P), np.float32)
    for e in range(E):
        sel[e, e] = sel[E + e, e] = 1.0
    return k, sel


def kernel(**inputs):
    import concourse.bacc as bacc
    from concourse.bass_utils import run_bass_kernel_spmd

    a = {k: np.ascontiguousarray(v) for k, v in inputs.items()}
    k, sel = constants()
    wq, wk, wv = a["L0_conv_Wq"].T, a["L0_conv_Wk"].T, a["L0_conv_Wv"].T
    wqb = np.zeros((P, 256), np.float32)
    wkv = np.zeros((P, C), np.float32)
    bkv = np.zeros((C, 1), np.float32)
    for i in range(2):
        rows = slice(i * C, (i + 1) * C)
        wqb[rows, i * P:(i + 1) * P] = wq
        wkv[rows, i * KD:(i + 1) * KD] = wk
        wkv[rows, 32 + i * KD:32 + (i + 1) * KD] = wv
        bkv[i * KD:(i + 1) * KD, 0] = a["L0_conv_bk"]
        bkv[32 + i * KD:32 + (i + 1) * KD, 0] = a["L0_conv_bv"]
    bq2 = np.zeros((C, P), np.float32)
    bq2[0::32] = a["L0_conv_bq"]
    bout2 = np.zeros((C, C), np.float32)
    bout2[:, 0::32] = a["L0_conv_bout"][:, None]

    def twice(w):
        return np.concatenate([w, w])

    w = a["L1_conv_weight"]
    arrays = dict(
        x=a["x"].reshape(B, C, S), consts=k, wqb=wqb, bq2=bq2, wkv=wkv, bkv=bkv, wout=a["L0_conv_Wout"],
        bout2=bout2, wr=twice(a["L0_ffn_Wr"]), br=np.tile(a["L0_ffn_br"], (B, 1)),
        w1a=twice(a["L0_ffn_W1"].transpose(1, 0, 2)), b1a=a["L0_ffn_b1"].T,
        w2ta=a["L0_ffn_W2"].transpose(2, 0, 1), b2ta=a["L0_ffn_b2"].T,
        gammab=np.tile(a["L0_ffn_gamma"], (P, 1)), betab=np.tile(a["L0_ffn_beta"], (P, 1)),
        wconv=twice(w[:, :, ::-1].transpose(1, 3, 2, 0).reshape(C, TAPS, C)), wcs=twice(w.reshape(C, C * TAPS)),
        gw=twice(a["L1_ffn_gate_w"]), gbb=np.tile(a["L1_ffn_gate_b"], (P, TILES, 1)),
        w1b=twice(a["L1_ffn_W1"].transpose(1, 0, 2)), b1b=a["L1_ffn_b1"].T,
        w2b=a["L1_ffn_W2"].transpose(1, 0, 2), b2b=np.tile(a["L1_ffn_b2"], (4, 1)), selb=sel,
    )
    nc = bacc.Bacc("TRN2", target_bir_lowering=False, num_devices=1)
    arrays = {f"in_{n}": np.ascontiguousarray(v) for n, v in arrays.items()}
    args = [nc.dram_tensor(n, v.shape, mybir.dt.from_np(v.dtype), kind="ExternalInput").ap()
            for n, v in arrays.items()]
    out = nc.dram_tensor("out", (B, C, S), F32, kind="ExternalOutput").ap()
    build(nc, *args, out)
    r = run_bass_kernel_spmd(nc, [arrays], core_ids=[0])
    return r.results[0]["out"].reshape(B, C, H, W)
```
